# Optimizing a Trainium2 kernel written in Bass

```python
import numpy as np
import jax
import jax.numpy as jnp

def _softmax(x, axis=-1):
    return jax.nn.softmax(x, axis=axis)

def _gelu(x):
    return jax.nn.gelu(x, approximate=True)

def _silu(x):
    return jax.nn.silu(x)

def _sigmoid(x):
    return jax.nn.sigmoid(x)

def _layernorm(x, axis=-1, eps=1e-05):
    m = jnp.mean(x, axis=axis, keepdims=True)
    v = jnp.var(x, axis=axis, keepdims=True)
    return (x - m) / jnp.sqrt(v + eps)

def _scatter_add(tgt, idx, src, axis=0):
    return tgt.at[idx].add(src)

def _segment_sum(src, seg, n):
    return jax.ops.segment_sum(src, seg, n)
kernel_name = 'mk_hybrid_d1_jaxref_r4_30c344'

def setup_inputs(seed: int=0):
    np.random.seed(seed)
    _w = jnp.asarray

    def _L0_attn_a_setup():
        import math
        import jax, jax.numpy as jnp
        import numpy as np
        D_MODEL = 256
        D_STATE = 64
        BATCH = 8
        SEQLEN = 512

        def _reference_tuple_inner(x, log_Lam_real, Lam_imag, B_real, B_imag, C_real, C_imag, D, log_dt, W_out, b_out):
            B, L, H = x.shape
            N = log_Lam_real.shape[0]
            dt = jnp.exp(log_dt)
            Lam_r = -jnp.exp(log_Lam_real)
            mag = jnp.exp(Lam_r * dt)
            Lbar_r = mag * jnp.cos(Lam_imag * dt)
            Lbar_i = mag * jnp.sin(Lam_imag * dt)
            Bu_r = jnp.einsum('blh,nh->bln', x, dt * B_real)
            Bu_i = jnp.einsum('blh,nh->bln', x, dt * B_imag)

            def step(carry, bu):
                sr, si = carry
                bur, bui = bu
                nr = Lbar_r * sr - Lbar_i * si + bur
                ni = Lbar_r * si + Lbar_i * sr + bui
                return ((nr, ni), (nr, ni))
            sr0 = jnp.zeros((B, N), dtype=x.dtype)
            si0 = jnp.zeros((B, N), dtype=x.dtype)
            (sr, si), (SR, SI) = jax.lax.scan(step, (sr0, si0), (jnp.swapaxes(Bu_r, 0, 1), jnp.swapaxes(Bu_i, 0, 1)))
            y = jnp.einsum('lbn,hn->blh', SR, C_real) - jnp.einsum('lbn,hn->blh', SI, C_imag) + D * x
            out = y @ W_out.T + b_out
            return (out, (sr, si))
        key = jax.random.key(seed)
        ks = jax.random.split(key, 8)
        x = jax.random.normal(ks[0], (BATCH, SEQLEN, D_MODEL), dtype=jnp.float32)
        log_Lam_real = jnp.log(0.5 * jnp.ones((D_STATE,), dtype=jnp.float32))
        Lam_imag = math.pi * jnp.arange(D_STATE, dtype=jnp.float32)
        B_real = 0.02 * jax.random.normal(ks[1], (D_STATE, D_MODEL), dtype=jnp.float32)
        B_imag = 0.02 * jax.random.normal(ks[2], (D_STATE, D_MODEL), dtype=jnp.float32)
        C_real = 0.02 * jax.random.normal(ks[3], (D_MODEL, D_STATE), dtype=jnp.float32)
        C_imag = 0.02 * jax.random.normal(ks[4], (D_MODEL, D_STATE), dtype=jnp.float32)
        Dp = jnp.ones((D_MODEL,), dtype=jnp.float32)
        log_dt = jnp.zeros((1,), dtype=jnp.float32)
        W_out = 0.02 * jax.random.normal(ks[5], (D_MODEL, D_MODEL), dtype=jnp.float32)
        b_out = jnp.zeros((D_MODEL,), dtype=jnp.float32)
        return {'x': x, 'log_Lam_real': log_Lam_real, 'Lam_imag': Lam_imag, 'B_real': B_real, 'B_imag': B_imag, 'C_real': C_real, 'C_imag': C_imag, 'D': Dp, 'log_dt': log_dt, 'W_out': W_out, 'b_out': b_out}
    _L0_attn_a_in = _L0_attn_a_setup()

    def _L0_attn_b_setup():
        import jax, jax.numpy as jnp
        import numpy as np
        key = jax.random.key(seed)
        ks = jax.random.split(key, 5)
        B, T, C = (2, 512, 256)
        x = jax.random.normal(ks[0], (B, T, C), dtype=jnp.float32)
        Wqkv = jax.random.normal(ks[1], (C, 3 * C), dtype=jnp.float32) * C ** (-0.5)
        bqkv = jax.random.normal(ks[2], (3 * C,), dtype=jnp.float32) * 0.02
        Wproj = jax.random.normal(ks[3], (C, C), dtype=jnp.float32) * C ** (-0.5)
        bproj = jax.random.normal(ks[4], (C,), dtype=jnp.float32) * 0.02
        return {'x': x, 'Wqkv': Wqkv, 'bqkv': bqkv, 'Wproj': Wproj, 'bproj': bproj}
    _L0_attn_b_in = _L0_attn_b_setup()

    def _L0_ffn_setup():
        import jax, jax.numpy as jnp
        import numpy as np
        B, S, DIM = (4, 1024, 256)
        BASE_COUPLING = 0.1
        NUM_CYCLES = 3

        def _gelu(x):
            return jax.nn.gelu(x, approximate=False)

        def _coupling_net(h, w1, b1, w2, b2, w3, b3, w4, b4):
            h = _gelu(h @ w1 + b1)
            h = _gelu(h @ w2 + b2)
            h = _gelu(h @ w3 + b3)
            return jax.nn.sigmoid(h @ w4 + b4)

        def _global_net(h, w1, b1, w2, b2, w3, b3):
            h = _gelu(h @ w1 + b1)
            h = _gelu(h @ w2 + b2)
            return jax.nn.sigmoid(h @ w3 + b3)

        def _twist(x):
            o_r, o_i, p_r, p_i = jnp.split(x, 4, axis=-1)
            return jnp.concatenate([p_r, -p_i, -o_r, o_i], axis=-1)
        key = jax.random.key(seed)
        ks = jax.random.split(key, 9)
        d = DIM

        def w(k, fan_in, fan_out):
            return jax.random.normal(k, (fan_in, fan_out), dtype=jnp.float32) / np.sqrt(fan_in).astype(np.float32)
        inp = {'x': jax.random.normal(ks[0], (B, S, d), dtype=jnp.float32)}
        cn_dims = [(d, d), (d, d // 2), (d // 2, d // 4), (d // 4, 1)]
        for i, (a, b) in enumerate(cn_dims):
            inp[f'cn_w{i + 1}'] = w(ks[1 + i], a, b)
            inp[f'cn_b{i + 1}'] = jnp.zeros((b,), dtype=jnp.float32)
        gc_dims = [(d, d // 2), (d // 2, d // 4), (d // 4, 1)]
        for i, (a, b) in enumerate(gc_dims):
            inp[f'gc_w{i + 1}'] = w(ks[5 + i], a, b)
            inp[f'gc_b{i + 1}'] = jnp.zeros((b,), dtype=jnp.float32)
        inp['adaptive_range'] = jnp.full((1,), 0.2, dtype=jnp.float32)
        return inp
    _L0_ffn_in = _L0_ffn_setup()
    _d = {'L0_attn_a_x': _L0_attn_a_in['x'], 'L0_attn_a_log_Lam_real': _L0_attn_a_in['log_Lam_real'], 'L0_attn_a_Lam_imag': _L0_attn_a_in['Lam_imag'], 'L0_attn_a_B_real': _L0_attn_a_in['B_real'], 'L0_attn_a_B_imag': _L0_attn_a_in['B_imag'], 'L0_attn_a_C_real': _L0_attn_a_in['C_real'], 'L0_attn_a_C_imag': _L0_attn_a_in['C_imag'], 'L0_attn_a_D': _L0_attn_a_in['D'], 'L0_attn_a_log_dt': _L0_attn_a_in['log_dt'], 'L0_attn_a_W_out': _L0_attn_a_in['W_out'], 'L0_attn_a_b_out': _L0_attn_a_in['b_out'], 'L0_attn_b_Wqkv': _L0_attn_b_in['Wqkv'], 'L0_attn_b_bqkv': _L0_attn_b_in['bqkv'], 'L0_attn_b_Wproj': _L0_attn_b_in['Wproj'], 'L0_attn_b_bproj': _L0_attn_b_in['bproj'], 'L0_ffn_cn_w1': _L0_ffn_in['cn_w1'], 'L0_ffn_cn_b1': _L0_ffn_in['cn_b1'], 'L0_ffn_cn_w2': _L0_ffn_in['cn_w2'], 'L0_ffn_cn_b2': _L0_ffn_in['cn_b2'], 'L0_ffn_cn_w3': _L0_ffn_in['cn_w3'], 'L0_ffn_cn_b3': _L0_ffn_in['cn_b3'], 'L0_ffn_cn_w4': _L0_ffn_in['cn_w4'], 'L0_ffn_cn_b4': _L0_ffn_in['cn_b4'], 'L0_ffn_gc_w1': _L0_ffn_in['gc_w1'], 'L0_ffn_gc_b1': _L0_ffn_in['gc_b1'], 'L0_ffn_gc_w2': _L0_ffn_in['gc_w2'], 'L0_ffn_gc_b2': _L0_ffn_in['gc_b2'], 'L0_ffn_gc_w3': _L0_ffn_in['gc_w3'], 'L0_ffn_gc_b3': _L0_ffn_in['gc_b3'], 'L0_ffn_adaptive_range': _L0_ffn_in['adaptive_range']}
    _x0 = _d['L0_attn_a_x']
    _d['L0_attn_a_x'] = jax.random.normal(jax.random.fold_in(jax.random.key(seed), 1), (16, 1024, 256), dtype=_x0.dtype)
    del _x0
    return _d

def reference(L0_attn_a_x, L0_attn_a_log_Lam_real, L0_attn_a_Lam_imag, L0_attn_a_B_real, L0_attn_a_B_imag, L0_attn_a_C_real, L0_attn_a_C_imag, L0_attn_a_D, L0_attn_a_log_dt, L0_attn_a_W_out, L0_attn_a_b_out, L0_attn_b_Wqkv, L0_attn_b_bqkv, L0_attn_b_Wproj, L0_attn_b_bproj, L0_ffn_cn_w1, L0_ffn_cn_b1, L0_ffn_cn_w2, L0_ffn_cn_b2, L0_ffn_cn_w3, L0_ffn_cn_b3, L0_ffn_cn_w4, L0_ffn_cn_b4, L0_ffn_gc_w1, L0_ffn_gc_b1, L0_ffn_gc_w2, L0_ffn_gc_b2, L0_ffn_gc_w3, L0_ffn_gc_b3, L0_ffn_adaptive_range):

    def _L0_attn_a_ref(x, log_Lam_real, Lam_imag, B_real, B_imag, C_real, C_imag, D, log_dt, W_out, b_out):
        import math
        import jax, jax.numpy as jnp
        import numpy as np
        D_MODEL = 256
        D_STATE = 64
        BATCH = 8
        SEQLEN = 512

        def _reference_tuple_inner(x, log_Lam_real, Lam_imag, B_real, B_imag, C_real, C_imag, D, log_dt, W_out, b_out):
            B, L, H = x.shape
            N = log_Lam_real.shape[0]
            dt = jnp.exp(log_dt)
            Lam_r = -jnp.exp(log_Lam_real)
            mag = jnp.exp(Lam_r * dt)
            Lbar_r = mag * jnp.cos(Lam_imag * dt)
            Lbar_i = mag * jnp.sin(Lam_imag * dt)
            Bu_r = jnp.einsum('blh,nh->bln', x, dt * B_real)
            Bu_i = jnp.einsum('blh,nh->bln', x, dt * B_imag)

            def step(carry, bu):
                sr, si = carry
                bur, bui = bu
                nr = Lbar_r * sr - Lbar_i * si + bur
                ni = Lbar_r * si + Lbar_i * sr + bui
                return ((nr, ni), (nr, ni))
            sr0 = jnp.zeros((B, N), dtype=x.dtype)
            si0 = jnp.zeros((B, N), dtype=x.dtype)
            (sr, si), (SR, SI) = jax.lax.scan(step, (sr0, si0), (jnp.swapaxes(Bu_r, 0, 1), jnp.swapaxes(Bu_i, 0, 1)))
            y = jnp.einsum('lbn,hn->blh', SR, C_real) - jnp.einsum('lbn,hn->blh', SI, C_imag) + D * x
            out = y @ W_out.T + b_out
            return (out, (sr, si))
        return _reference_tuple_inner(x, log_Lam_real, Lam_imag, B_real, B_imag, C_real, C_imag, D, log_dt, W_out, b_out)[0]

    def _L0_attn_b_ref(x, Wqkv, bqkv, Wproj, bproj):
        import jax, jax.numpy as jnp
        import numpy as np
        B, T, C = x.shape
        n_head = 16
        hd = C // n_head
        x_proj = x @ Wqkv + bqkv
        q = x_proj[:, :, :C].reshape(B, n_head, T, hd)
        k = x_proj[:, :, C:2 * C].reshape(B, n_head, T, hd)
        v = x_proj[:, :, 2 * C:].reshape(B, n_head, T, hd)
        att = jnp.einsum('bhtd,bhsd->bhts', q, k) * (1.0 / jnp.sqrt(jnp.float32(hd)))
        causal = jnp.tril(jnp.ones((T, T), dtype=bool))
        att = jnp.where(causal, att, jnp.float32(-jnp.inf))
        att = jax.nn.softmax(att, axis=-1)
        y = att @ v
        y = jnp.transpose(y, (0, 2, 1, 3)).reshape(B, T, C)
        return y @ Wproj + bproj

    def _L0_ffn_ref(x, cn_w1, cn_b1, cn_w2, cn_b2, cn_w3, cn_b3, cn_w4, cn_b4, gc_w1, gc_b1, gc_w2, gc_b2, gc_w3, gc_b3, adaptive_range):
        import jax, jax.numpy as jnp
        import numpy as np
        B, S, DIM = (4, 1024, 256)
        BASE_COUPLING = 0.1
        NUM_CYCLES = 3

        def _gelu(x):
            return jax.nn.gelu(x, approximate=False)

        def _coupling_net(h, w1, b1, w2, b2, w3, b3, w4, b4):
            h = _gelu(h @ w1 + b1)
            h = _gelu(h @ w2 + b2)
            h = _gelu(h @ w3 + b3)
            return jax.nn.sigmoid(h @ w4 + b4)

        def _global_net(h, w1, b1, w2, b2, w3, b3):
            h = _gelu(h @ w1 + b1)
            h = _gelu(h @ w2 + b2)
            return jax.nn.sigmoid(h @ w3 + b3)

        def _twist(x):
            o_r, o_i, p_r, p_i = jnp.split(x, 4, axis=-1)
            return jnp.concatenate([p_r, -p_i, -o_r, o_i], axis=-1)
        global_context = x.mean(axis=1, keepdims=True)
        gf = _global_net(global_context, gc_w1, gc_b1, gc_w2, gc_b2, gc_w3, gc_b3)
        out = x
        for _ in range(NUM_CYCLES):
            tf = _coupling_net(out, cn_w1, cn_b1, cn_w2, cn_b2, cn_w3, cn_b3, cn_w4, cn_b4)
            combined = 0.7 * gf + 0.3 * tf
            coupling = BASE_COUPLING + adaptive_range * (combined - 0.5) * 2.0
            out = out + coupling * _twist(out)
        return out
    x = L0_attn_a_x
    x = x + _L0_attn_a_ref(_layernorm(x, axis=-1), L0_attn_a_log_Lam_real, L0_attn_a_Lam_imag, L0_attn_a_B_real, L0_attn_a_B_imag, L0_attn_a_C_real, L0_attn_a_C_imag, L0_attn_a_D, L0_attn_a_log_dt, L0_attn_a_W_out, L0_attn_a_b_out)
    x = x + _L0_ffn_ref(_layernorm(x, axis=-1), L0_ffn_cn_w1, L0_ffn_cn_b1, L0_ffn_cn_w2, L0_ffn_cn_b2, L0_ffn_cn_w3, L0_ffn_cn_b3, L0_ffn_cn_w4, L0_ffn_cn_b4, L0_ffn_gc_w1, L0_ffn_gc_b1, L0_ffn_gc_w2, L0_ffn_gc_b2, L0_ffn_gc_w3, L0_ffn_gc_b3, L0_ffn_adaptive_range)
    x = x + _L0_attn_b_ref(_layernorm(x, axis=-1), L0_attn_b_Wqkv, L0_attn_b_bqkv, L0_attn_b_Wproj, L0_attn_b_bproj)
    x = x + _L0_ffn_ref(_layernorm(x, axis=-1), L0_ffn_cn_w1, L0_ffn_cn_b1, L0_ffn_cn_w2, L0_ffn_cn_b2, L0_ffn_cn_w3, L0_ffn_cn_b3, L0_ffn_cn_w4, L0_ffn_cn_b4, L0_ffn_gc_w1, L0_ffn_gc_b1, L0_ffn_gc_w2, L0_ffn_gc_b2, L0_ffn_gc_w3, L0_ffn_gc_b3, L0_ffn_adaptive_range)
    return x

_drawn_inputs = setup_inputs


def setup_inputs(seed=0):
    import zlib

    import numpy as np

    out = dict(_drawn_inputs(seed))
    spreads = {'L0_attn_a_log_Lam_real': (-0.6931471824645996, 0.6),
     'L0_attn_a_D': (1.0, 0.2),
     'L0_attn_a_b_out': (0.0, 0.1),
     'L0_ffn_cn_b1': (0.0, 0.8),
     'L0_ffn_cn_b2': (0.0, 2.0),
     'L0_ffn_cn_b3': (0.0, 2.0),
     'L0_ffn_gc_b1': (0.0, 0.8),
     'L0_ffn_gc_b2': (0.0, 0.8)}
    factors = {'L0_attn_a_Lam_imag': 64.0,
     'L0_attn_a_B_real': 2.897,
     'L0_attn_a_B_imag': 2.896,
     'L0_attn_a_C_real': 2.882,
     'L0_attn_a_C_imag': 2.856,
     'L0_attn_b_bqkv': 8.0,
     'L0_attn_b_bproj': 5.972,
     'L0_ffn_cn_w1': 4.553,
     'L0_ffn_cn_w2': 4.775,
     'L0_ffn_cn_w3': 3.657,
     'L0_ffn_cn_w4': 4.124,
     'L0_ffn_gc_w1': 8.0,
     'L0_ffn_gc_w2': 8.0,
     'L0_ffn_gc_w3': 2.778}
    for name, (base, spread) in spreads.items():
        noise = np.random.default_rng([zlib.crc32(name.encode()), seed]).standard_normal(out[name].shape)
        drawn = base * np.exp(spread * noise) if base else spread * noise
        out[name] = jnp.asarray(drawn.astype(out[name].dtype))
    for name, factor in factors.items():
        out[name] = (out[name] * factor).astype(out[name].dtype)
    return out
```

```python
from contextlib import ExitStack

import numpy as np

import concourse.bass as bass
from concourse import mybir

F32 = mybir.dt.float32
BF16 = mybir.dt.bfloat16
I32 = mybir.dt.int32
ALU = mybir.AluOpType
ACT = mybir.ActivationFunctionType
AX = mybir.AxisListType

P = 128
D = 256
KT = D // P
L = 1024
CH = 512
TT = CH // P
NCH = L // CH
EPS = 1e-5
ROUND = 1.5 * 2.0 ** 23
TWO_PI = float(np.nextafter(np.float32(2 * np.pi), np.float32(0)))


class Chain:

    def __init__(self, eng, sem):
        self.eng, self.sem, self.n = eng, sem, 0

    def __call__(self, instruction):
        self.n += 1
        instruction.then_inc(self.sem, 1)
        self.eng.wait_ge(self.sem, self.n)


def make_identities(nc, sem, identf, identb):
    identity_zero, identity_one = sem("identity_zero"), sem("identity_one")
    with nc.Block() as block:
        @block.gpsimd
        def _(pool):
            nc.gpsimd.memset(identf[:, :], 0.0).then_inc(identity_zero, 1)
            nc.gpsimd.memset(identb[:, :], 0.0).then_inc(identity_zero, 1)
            pool.wait_ge(identity_zero, 2)
            for m in (identf, identb):
                nc.gpsimd.affine_select(out=m[:, :], in_=m[:, :], compare_op=ALU.not_equal, fill=1.0, base=0,
                                        pattern=[[-1, P]], channel_multiplier=1).then_inc(identity_one, 1)
            pool.wait_ge(identity_one, 2)


def ssm_phase(nc, sem, identf, x, x1, log_lam, lam_imag, b_real, b_imag, c_real, c_imag, d_skip, log_dt,
              w_out, b_out):
    N = log_lam.shape[0]
    n_chunks = x.shape[0] * NCH
    H2 = 2 * N
    assert H2 == P
    xs = x.rearrange("b (c t p) d -> (b c) p t d", c=NCH, p=P)
    x1s = x1.rearrange("b (c t p) d -> (b c) p t d", c=NCH, p=P)
    with ExitStack() as ctx:
        def sb(name, shape, dt=F32):
            return ctx.enter_context(nc.sbuf_tensor("ssm_" + name, shape, dt))

        cos_t, sin_t = sb("cos", [P, L]), sb("sin", [P, L])
        decay = sb("decay", [P, 1])
        bu_w = sb("bu_w", [P, KT, P])
        bu_turned_w = sb("bu_turned_w", [P, KT, P])
        out_cos_w = sb("out_cos_w", [P, D])
        out_sin_w = sb("out_sin_w", [P, D])
        skip_w = sb("skip_w", [P, KT, D])
        bias_row = sb("bias_row", [P, D])

        with ExitStack() as pre:
            def sbp(name, shape, dt=F32):
                return pre.enter_context(nc.sbuf_tensor("ssm_pre_" + name, shape, dt))

            bst = sbp("bst", [P, D])
            bst_dt = sbp("bst_dt", [P, D])
            cst = sbp("cst", [P, KT, 2, N])
            cl_cos, cl_sin = sbp("cl_cos", [P, KT, P]), sbp("cl_sin", [P, KT, P])
            wo = sbp("wo", [P, KT, D])
            wt = sbp("wt", [P, KT, D])
            dv = sbp("dv", [P, KT])
            col = sbp("col", [P, 40])
            steps_i = sbp("steps_i", [P, L], I32)
            steps = sbp("steps", [P, L])
            ang, tmp = sbp("ang", [P, L]), sbp("tmp", [P, L])
            euler = sbp("euler", [P, 1])
            bits = sbp("bits", [P, 4], BF16)
            t_ps = pre.enter_context(nc.psum_tensor("ssm_pre_t", [P, 4, 512], F32))
            m_ps = pre.enter_context(nc.psum_tensor("ssm_pre_m", [P, 2, 512], F32))
            names = ("loaded", "pool_step", "column_step", "dt_ready", "decay_ready", "bst_scaled", "w_turned",
                     "weights_step", "w_evacuated", "out_w_ready", "angle_ready", "cos_angle_ready",
                     "table_done", "steps_ready")
            (loaded, pool_step, column_step, dt_ready, decay_ready, bst_scaled, w_turned, weights_step,
             w_evacuated, out_w_ready, angle_ready, cos_angle_ready, table_done, steps_ready) = [
                 sem("ssm_pre_" + n) for n in names]
            loads = [
                (col[0:N, 0:1], log_lam.rearrange("(n a) -> n a", a=1)),
                (col[N:P, 0:1], log_lam.rearrange("(n a) -> n a", a=1)),
                (col[0:N, 1:2], lam_imag.rearrange("(n a) -> n a", a=1)),
                (col[N:P, 1:2], lam_imag.rearrange("(n a) -> n a", a=1)),
                (col[:, 2:3], log_dt.rearrange("(n a) -> n a", a=1).to_broadcast([P, 1])),
                (bst[0:N, :], b_real),
                (bst[N:P, :], b_imag),
                (cst[:, :, 0, :], c_real.rearrange("(k p) n -> p k n", p=P)),
                (cst[:, :, 1, :], c_imag.rearrange("(k p) n -> p k n", p=P)),
                (wo[:, :, :], w_out.rearrange("(k p) h -> p k h", p=P)),
                (dv[:, :], d_skip.rearrange("(k p) -> p k", p=P)),
                (bias_row[:, :], b_out.rearrange("(a d) -> a d", a=1).to_broadcast([P, D])),
            ]
            with nc.Block() as block:
                @block.sync
                def _(sp):
                    with nc.allow_non_contiguous_dma(reason="a few short columns, once"):
                        for dst, src in loads:
                            sp.dma_start(dst, src).then_inc(loaded, 16)

                @block.gpsimd
                def _(pool):
                    step = Chain(pool, pool_step)
                    step(nc.gpsimd.memset(euler[:, :], float(np.e)))
                    step(nc.gpsimd.iota(steps_i[:, :], [[1, L]], base=0, channel_multiplier=0))
                    nc.gpsimd.tensor_copy(steps[:, :], steps_i[:, :]).then_inc(steps_ready, 1)
                    pool.wait_ge(loaded, 16 * len(loads))
                    nc.gpsimd.tensor_tensor(col[:, 3:4], euler[:, :], col[:, 2:3], ALU.pow).then_inc(dt_ready, 1)
                    step(nc.gpsimd.tensor_tensor(col[:, 4:5], euler[:, :], col[:, 0:1], ALU.pow))
                    pool.wait_ge(dt_ready, 1)
                    step(nc.gpsimd.tensor_tensor(col[:, 5:6], col[:, 4:5], col[:, 3:4], ALU.mult))
                    step(nc.gpsimd.tensor_scalar(col[:, 6:7], col[:, 5:6], -1.0, 0.0, ALU.mult, ALU.add))
                    nc.gpsimd.tensor_tensor(decay[:, :], euler[:, :], col[:, 6:7], ALU.pow).then_inc(decay_ready, 1)
                    pool.wait_ge(decay_ready, 1)

                @block.vector
                def _(dve):
                    step = Chain(dve, column_step)
                    v = nc.vector
                    dve.wait_ge(dt_ready, 1)
                    v.tensor_scalar(bst_dt[:, :], bst[:, :], col[:, 3:4], None, ALU.mult).then_inc(bst_scaled, 1)
                    v.tensor_scalar(cl_cos[:, :, 0:N], cst[:, :, 0, :], 1.0, None, ALU.mult)
                    v.tensor_scalar(cl_cos[:, :, N:P], cst[:, :, 1, :], -1.0, None, ALU.mult)
                    v.tensor_scalar(cl_sin[:, :, 0:N], cst[:, :, 1, :], -1.0, None, ALU.mult)
                    v.tensor_scalar(cl_sin[:, :, N:P], cst[:, :, 0, :], -1.0, None, ALU.mult).then_inc(weights_step, 1)
                    dve.wait_ge(w_turned, 1)
                    v.tensor_copy(bu_w[:, :, :], t_ps[:, 0, 0:KT * P].rearrange("p (k n) -> p k n", k=KT))
                    tb = t_ps[:, 0, 0:KT * P].rearrange("p (k n) -> p k n", k=KT)
                    v.tensor_scalar(bu_turned_w[:, :, 0:N], tb[:, :, N:P], 1.0, None, ALU.mult)
                    v.tensor_scalar(bu_turned_w[:, :, N:P], tb[:, :, 0:N], -1.0, None, ALU.mult)
                    for k in range(KT):
                        v.tensor_copy(wt[:, k, :], t_ps[:, 1 + k, 0:D]).then_inc(w_evacuated, 1)
                    dve.wait_ge(w_evacuated, KT)
                    for k in range(KT):
                        v.tensor_scalar(skip_w[:, k, :], wt[:, k, :], dv[:, k:k + 1], None, ALU.mult)
                    dve.wait_ge(out_w_ready, 1)
                    v.tensor_copy(out_cos_w[:, :], m_ps[:, 0, 0:D])
                    step(v.tensor_copy(out_sin_w[:, :], m_ps[:, 1, 0:D]))

                    turn = 1.0 / (2 * np.pi)
                    c1 = float(np.floor(turn * 2.0 ** 18) / 2.0 ** 18)
                    c2 = float(np.floor((turn - c1) * 2.0 ** 34) / 2.0 ** 34)
                    c3 = float(turn - c1 - c2)
                    step(v.tensor_tensor(col[:, 7:8], col[:, 1:2], col[:, 3:4], ALU.mult))
                    rest = col[:, 7:8]
                    for i in range(3):
                        step(v.tensor_copy(bits[:, i:i + 1], rest))
                        step(v.tensor_copy(col[:, 8 + i:9 + i], bits[:, i:i + 1]))
                        step(v.tensor_tensor(col[:, 12 + i:13 + i], rest, col[:, 8 + i:9 + i], ALU.subtract))
                        rest = col[:, 12 + i:13 + i]
                    products = [(0, c1), (1, c1), (2, c1), (0, c2), (1, c2), (0, c3)]
                    step(v.memset(col[:, 16:17], 0.0))
                    total = 16
                    for i, (part, c) in enumerate(products):
                        step(v.tensor_scalar(col[:, 18:19], col[:, 8 + part:9 + part], c, None, ALU.mult))
                        step(v.tensor_scalar(col[:, 19:20], col[:, 18:19], ROUND, ROUND, ALU.add, ALU.subtract))
                        step(v.tensor_tensor(col[:, 20:21], col[:, 18:19], col[:, 19:20], ALU.subtract))
                        step(v.tensor_tensor(col[:, 21 + i:22 + i], col[:, total:total + 1], col[:, 20:21], ALU.add))
                        total = 21 + i
                    whole = col[:, total:total + 1]
                    step(v.tensor_scalar(col[:, 28:29], whole, ROUND, ROUND, ALU.add, ALU.subtract))
                    step(v.tensor_tensor(col[:, 29:30], whole, col[:, 28:29], ALU.subtract))
                    step(v.tensor_scalar(col[:, 30:31], col[:, 29:30], ROUND / 4096, ROUND / 4096, ALU.add, ALU.subtract))
                    step(v.tensor_tensor(col[:, 31:32], col[:, 29:30], col[:, 30:31], ALU.subtract))

                    def fraction(dst, src):
                        step(v.tensor_scalar(tmp[:, :], src, ROUND, ROUND, ALU.add, ALU.subtract))
                        step(v.tensor_tensor(dst, src, tmp[:, :], ALU.subtract))

                    dve.wait_ge(steps_ready, 1)
                    step(v.tensor_scalar(ang[:, :], steps[:, :], col[:, 30:31], None, ALU.mult))
                    fraction(ang[:, :], ang[:, :])
                    step(v.scalar_tensor_tensor(out=ang[:, :], in0=steps[:, :], scalar=col[:, 31:32], in1=ang[:, :],
                                                op0=ALU.mult, op1=ALU.add))
                    step(v.tensor_scalar(tmp[:, :], ang[:, :], ROUND, ROUND, ALU.add, ALU.subtract))
                    v.tensor_tensor(ang[:, :], ang[:, :], tmp[:, :], ALU.subtract).then_inc(angle_ready, 1)
                    dve.wait_ge(angle_ready, 1)
                    step(v.tensor_scalar(steps[:, :], ang[:, :], 0.25, None, ALU.add))
                    step(v.tensor_scalar(tmp[:, :], steps[:, :], ROUND, ROUND, ALU.add, ALU.subtract))
                    v.tensor_tensor(steps[:, :], steps[:, :], tmp[:, :], ALU.subtract).then_inc(cos_angle_ready, 1)

                @block.scalar
                def _(act):
                    act.wait_ge(angle_ready, 1)
                    nc.scalar.activation(sin_t[:, :], ang[:, :], ACT.Sin, scale=TWO_PI).then_inc(table_done, 1)
                    act.wait_ge(cos_angle_ready, 1)
                    nc.scalar.activation(cos_t[:, :], steps[:, :], ACT.Sin, scale=TWO_PI).then_inc(table_done, 1)
                    act.wait_ge(table_done, 2)

                @block.tensor
                def _(pe):
                    pe.wait_ge(loaded, 16 * len(loads))
                    pe.wait_ge(bst_scaled, 1)
                    for k in range(KT):
                        pe.transpose(t_ps[:, 0, k * P:(k + 1) * P], bst_dt[:, k * P:(k + 1) * P], identf[:, :])
                    for k in range(KT):
                        for o in range(KT):
                            last = pe.transpose(t_ps[:, 1 + k, o * P:(o + 1) * P], wo[:, o, k * P:(k + 1) * P],
                                                identf[:, :])
                    last.then_inc(w_turned, 1)
                    pe.wait_ge(weights_step, 1)
                    pe.wait_ge(w_evacuated, KT)
                    for m, lhs in enumerate((cl_cos, cl_sin)):
                        for k in range(KT):
                            last = pe.matmul(m_ps[:, m, 0:D], lhs[:, k, :], wt[:, k, :], start=(k == 0), stop=(k == KT - 1))
                    last.then_inc(out_w_ready, 1)

        xt = [sb(f"x{k}", [P, TT, D]) for k in range(2)]
        xb = [sb(f"xb{k}", [P, TT, D]) for k in range(2)]
        xn = [sb(f"xn{k}", [P, TT, D]) for k in range(2)]
        xnT = [sb(f"xnT{k}", [P, KT, CH]) for k in range(2)]
        y = [sb(f"y{k}", [P, TT, D]) for k in range(2)]
        stats = [sb(f"stats{k}", [P, TT, 6]) for k in range(2)]
        moments = [sb(f"moments{k}", [P, TT, 2]) for k in range(2)]
        rstd = [sb(f"rstd{k}", [P, TT]) for k in range(2)]
        var_eps = [sb(f"var_eps{k}", [P, TT]) for k in range(2)]
        carrier = sb("carrier", [1, 1])
        minus_half, eps = sb("minus_half", [P, TT]), sb("eps", [P, TT])
        u_cos, u_sin, u = sb("u_cos", [P, CH]), sb("u_sin", [P, CH]), sb("u", [P, CH])
        w = [sb(f"w{k}", [P, CH]) for k in range(2)]
        w_cos = [sb(f"w_cos{k}", [P, CH]) for k in range(2)]
        w_sin = [sb(f"w_sin{k}", [P, CH]) for k in range(2)]
        turned_ps = ctx.enter_context(nc.psum_tensor("ssm_turned", [P, KT, CH], F32))
        bu_ps = [ctx.enter_context(nc.psum_tensor(f"ssm_bu{k}", [P, 2, CH], F32)) for k in range(2)]
        out_ps = ctx.enter_context(nc.psum_tensor("ssm_out", [P, TT, D], F32))

        x_loaded = [sem(f"ssm_x_loaded{k}") for k in range(2)]
        y_stored = [sem(f"ssm_y_stored{k}") for k in range(2)]
        (stats_done, moments_done, eps_added, rstd_ready, xn_ready, turned, xnT_ready, bu_ready, u_parts, u_ready,
         w_ready, w_turned, out_ready, xb_ready, y_ready, const_ready) = [sem("ssm_" + n) for n in (
             "stats_done", "moments_done", "eps_added", "rstd_ready", "xn_ready", "turned", "xnT_ready", "bu_ready",
             "u_parts", "u_ready", "w_ready", "w_turned", "out_ready", "xb_ready", "y_ready", "const_ready")]
        n_steps = n_chunks // 2
        with nc.Block() as block:
            @block.sync
            def _(sp):
                def load(n, k, old):
                    if old:
                        sp.wait_ge(xn_ready, n - 1)
                        sp.wait_ge(xb_ready, n - 1)
                    sp.dma_start(xt[k][:, :, :], xs[n]).then_inc(x_loaded[k], 16)

                def store(n, k):
                    sp.wait_ge(y_ready, n + 1)
                    sp.dma_start(x1s[n], y[k][:, :, :]).then_inc(y_stored[k], 16)

                load(0, 0, False)
                load(1, 1, False)
                with sp.Fori(0, n_steps - 1) as it:
                    for k in range(2):
                        load(2 * it + k + 2, k, True)
                        store(2 * it + k, k)
                for k in range(2):
                    store(2 * (n_steps - 1) + k, k)
                for k in range(2):
                    sp.wait_ge(y_stored[k], 16 * n_steps)

            @block.gpsimd
            def _(pool):
                nc.gpsimd.memset(eps[:, :], EPS).then_inc(const_ready, 1)
                nc.gpsimd.memset(minus_half[:, :], -0.5).then_inc(const_ready, 1)
                pool.wait_ge(const_ready, 2)

                def chunk(n, it, k, old):
                    pool.wait_ge(moments_done, n + 1)
                    nc.gpsimd.tensor_tensor(var_eps[k][:, :], moments[k][:, :, 1], eps[:, :],
                                            ALU.add).then_inc(eps_added, 1)
                    pool.wait_ge(eps_added, n + 1)
                    if old:
                        pool.wait_ge(xn_ready, n - 1)
                    nc.gpsimd.tensor_tensor(rstd[k][:, :], var_eps[k][:, :], minus_half[:, :],
                                            ALU.pow).then_inc(rstd_ready, 1)
                    pool.wait_ge(x_loaded[k], 16 * it + 16)
                    if old:
                        pool.wait_ge(y_ready, n - 1)
                    nc.gpsimd.tensor_tensor(xb[k][:, :, :], xt[k][:, :, :],
                                            bias_row[:, :].unsqueeze(1).to_broadcast([P, TT, D]),
                                            ALU.add).then_inc(xb_ready, 1)

                chunk(0, 0, 0, False)
                chunk(1, 0, 1, False)
                with pool.Fori(1, n_steps) as it:
                    for k in range(2):
                        chunk(2 * it + k, it, k, True)

            @block.vector
            def _(dve):
                def normalise(n, it, k, old):
                    dve.wait_ge(x_loaded[k], 16 * it + 16)
                    for t in range(TT):
                        last = nc.vector.bn_stats(stats[k][:, t, :], xt[k][:, t, :])
                    last.then_inc(stats_done, 1)
                    if old:
                        dve.wait_ge(eps_added, n - 1)
                    dve.wait_ge(stats_done, n + 1)
                    nc.vector.memset(carrier[:, :], 0.0)
                    for t in range(TT):
                        last = nc.vector.bn_aggr(moments[k][:, t, :], stats[k][:, t, :])
                    last.then_inc(moments_done, 1)

                def scale(n, k, old):
                    dve.wait_ge(rstd_ready, n + 1)
                    if old:
                        dve.wait_ge(turned, n - 1)
                    for t in range(TT):
                        last = nc.vector.tensor_scalar(xn[k][:, t, :], xt[k][:, t, :], moments[k][:, t, 0:1],
                                                       rstd[k][:, t:t + 1], ALU.subtract, ALU.mult)
                    last.then_inc(xn_ready, 1)

                def scan(n, k, old):
                    cos_k, sin_k = cos_t[:, k * CH:(k + 1) * CH], sin_t[:, k * CH:(k + 1) * CH]
                    dve.wait_ge(bu_ready, n + 1)
                    nc.vector.tensor_tensor(u_cos[:, :], bu_ps[k][:, 0, :], cos_k, ALU.mult)
                    nc.vector.tensor_tensor(u_sin[:, :], bu_ps[k][:, 1, :], sin_k, ALU.mult).then_inc(u_parts, 1)
                    dve.wait_ge(u_parts, n + 1)
                    nc.vector.tensor_tensor(u[:, :], u_cos[:, :], u_sin[:, :], ALU.add).then_inc(u_ready, 1)
                    dve.wait_ge(u_ready, n + 1)
                    nc.vector.tensor_tensor_scan(w[k][:, :], decay[:, 0:1].to_broadcast([P, CH]), u[:, :],
                                                 w[1 - k][:, CH - 1:CH] if k else 0.0,
                                                 ALU.mult, ALU.add).then_inc(w_ready, 1)
                    dve.wait_ge(w_ready, n + 1)
                    if old:
                        dve.wait_ge(out_ready, n - 1)
                    nc.vector.tensor_tensor(w_cos[k][:, :], w[k][:, :], cos_k, ALU.mult)
                    nc.vector.tensor_tensor(w_sin[k][:, :], w[k][:, :], sin_k, ALU.mult).then_inc(w_turned, 1)

                def residual(n, it, k, old):
                    dve.wait_ge(out_ready, n + 1)
                    dve.wait_ge(xb_ready, n + 1)
                    if old:
                        dve.wait_ge(y_stored[k], 16 * it)
                    nc.vector.tensor_tensor(y[k][:, :, :], out_ps[:, :, :], xb[k][:, :, :],
                                            ALU.add).then_inc(y_ready, 1)

                normalise(0, 0, 0, False)
                scale(0, 0, False)
                normalise(1, 0, 1, False)
                scan(0, 0, False)
                scale(1, 1, False)

                def slot(n, it, k, old, more):
                    if more:
                        normalise(n + 2, it + 1, k, True)
                    scan(n + 1, 1 - k, old or k == 1)
                    if more:
                        scale(n + 2, k, True)
                    residual(n, it, k, old)

                slot(0, 0, 0, False, True)
                slot(1, 0, 1, False, True)
                with dve.Fori(1, n_steps - 1) as it:
                    for k in range(2):
                        slot(2 * it + k, it, k, True, True)
                it = n_steps - 1
                slot(2 * it, it, 0, True, False)
                residual(2 * it + 1, it, 1, True)

            @block.scalar
            def _(act):
                def evacuate(n, k, old):
                    act.wait_ge(turned, n + 1)
                    if old:
                        act.wait_ge(out_ready, n - 1)
                    nc.scalar.activation(xnT[k][:, :, :], turned_ps[:, :, :], ACT.Copy).then_inc(xnT_ready, 1)

                evacuate(0, 0, False)
                evacuate(1, 1, False)
                with act.Fori(1, n_steps) as it:
                    for k in range(2):
                        evacuate(2 * it + k, k, True)

            @block.tensor
            def _(pe):
                def turn(n, k, first):
                    pe.wait_ge(xn_ready, n + 1)
                    if not first:
                        pe.wait_ge(xnT_ready, n)
                    for f in range(KT):
                        for t in range(TT):
                            last = pe.transpose(turned_ps[:, f, t * P:(t + 1) * P], xn[k][:, t, f * P:(f + 1) * P],
                                                identf[:, :])
                    last.then_inc(turned, 1)

                def project(n, k, old):
                    pe.wait_ge(xnT_ready, n + 1)
                    if old:
                        pe.wait_ge(u_parts, n - 1)
                    for m, weights in enumerate((bu_w, bu_turned_w)):
                        for f in range(KT):
                            last = pe.matmul(bu_ps[k][:, m, :], weights[:, f, :], xnT[k][:, f, :],
                                             start=(f == 0), stop=(f == KT - 1))
                    last.then_inc(bu_ready, 1)

                def out(n, k, first):
                    if not first:
                        pe.wait_ge(y_ready, n)
                    pe.wait_ge(w_turned, n + 1)
                    for t in range(TT):
                        cols = slice(t * P, (t + 1) * P)
                        terms = [(xnT[k][:, f, cols], skip_w[:, f, :]) for f in range(KT)]
                        terms += [(w_cos[k][:, cols], out_cos_w[:, :]), (w_sin[k][:, cols], out_sin_w[:, :])]
                        for i, (lhs, rhs) in enumerate(terms):
                            last = pe.matmul(out_ps[:, t, :], lhs, rhs, start=(i == 0), stop=(i == len(terms) - 1))
                    last.then_inc(out_ready, 1)

                turn(0, 0, True)
                project(0, 0, False)

                def slot(n, k, first, old):
                    turn(n + 1, 1 - k, False)
                    project(n + 1, 1 - k, old or k == 1)
                    out(n, k, first)

                slot(0, 0, True, False)
                slot(1, 1, False, False)
                with pe.Fori(1, n_steps - 1) as it:
                    for k in range(2):
                        slot(2 * it + k, k, False, True)
                slot(2 * (n_steps - 1), 0, False, True)
                out(2 * (n_steps - 1) + 1, 1, False)


def ffn_phase(nc, sem, name, identf, x1, x2, cn, gc, adaptive_range):
    HALF, QUARTER = D // 2, D // 4
    CHAINS = 2 * NCH
    SLOTS = 3 * CHAINS
    n_steps = x1.shape[0] // 2
    xs = x1.rearrange("b (c t p) d -> (b c) p t d", c=NCH, p=P)
    ys = x2.rearrange("b (c t p) d -> (b c) p t d", c=NCH, p=P)
    cn_w1, cn_b1, cn_w2, cn_b2, cn_w3, cn_b3, cn_w4, cn_b4 = cn
    gc_w1, gc_b1, gc_w2, gc_b2, gc_w3, gc_b3 = gc
    with ExitStack() as ctx:
        def sb(n, shape, dt=F32):
            return ctx.enter_context(nc.sbuf_tensor(name + n, shape, dt))

        def psum(n, shape):
            return ctx.enter_context(nc.psum_tensor(name + n, shape, F32))

        def sems(names):
            return [sem(name + n) for n in names.split()]

        w1, w2, w3, w4 = sb("w1", [P, KT, D]), sb("w2", [P, KT, P]), sb("w3", [P, 64]), sb("w4", [64, 1])
        g1w, g2w, g3w = sb("g1w", [P, KT, P]), sb("g2w", [P, 64]), sb("g3w", [64, P])
        g3col = sb("g3col", [64, 1])
        b1, b2, b3 = sb("b1", [P, KT]), sb("b2", [P, 1]), sb("b3", [64, 1])
        gb1, gb2 = sb("gb1", [P, 1]), sb("gb2", [64, 1])
        half_bias = sb("half_bias", [P, 2])
        b4_half, gb3_half = half_bias[:, 0:1], half_bias[:, 1:2]
        ar = sb("ar", [P, 1])
        ar_cols = sb("ar_cols", [P, 3])
        eps, minus_half = sb("eps", [P, TT]), sb("minus_half", [P, TT])
        carrier = sb("carrier", [1, 1])
        xt = [sb(f"x{c}", [P, TT, D]) for c in range(CHAINS)]
        z = [[sb(f"z{c}_{i}", [P, TT, D]) for i in range(3)] for c in range(CHAINS)]
        y = [sb(f"y{k}", [P, TT, D]) for k in range(2)]
        zT = [sb(f"zT{k}", [P, KT, CH]) for k in range(2)]
        h1 = [sb(f"h1_{k}", [P, KT, CH]) for k in range(2)]
        h2 = [sb(f"h2_{k}", [P, CH]) for k in range(2)]
        h3 = [sb(f"h3_{k}", [64, CH]) for k in range(2)]
        stats, moments = sb("stats", [P, TT, 6]), sb("moments", [P, TT, 2])
        var_eps, rstd, rstd_neg = sb("var_eps", [P, TT]), sb("rstd", [P, TT]), sb("rstd_neg", [P, TT])
        minus_one = sb("minus_one", [P, TT])
        tanh_token = [sb(f"tanh_token{k}", [P, TT]) for k in range(2)]
        c_pos = [sb(f"c_pos{k}", [P, TT]) for k in range(2)]
        c_neg = [sb(f"c_neg{k}", [P, TT]) for k in range(2)]
        sums = sb("sums", [P, CHAINS, KT])
        g1, g2 = sb("g1", [P, 1]), sb("g2", [64, 1])
        tanh_global = sb("tanh_global", [P, 2])
        kappa = sb("kappa", [P, 2, 2])

        turned_ps, h1_ps = psum("turned", [P, KT, CH]), psum("h1p", [P, KT, CH])
        h2_ps, h3_ps, token_ps, global_ps = psum("h2p", [P, 512]), psum("h3p", [P, 512]), psum("tp", [P, 512]), psum("gp", [P, 512])

        x_loaded = [sem(f"{name}x_loaded{c}") for c in range(CHAINS)]
        y_stored = [sem(f"{name}y_stored{k}") for k in range(2)]
        (loaded, const_ready, weights_signed, stats_done, moments_done, eps_added, rstd_ready, rstd_neg_ready,
         z0_ready, rotated) = sems(
            "loaded const_ready weights_signed stats_done moments_done eps_added rstd_ready rstd_neg_ready "
            "z0_ready rotated")
        (turned, zT_ready, h1_done, h1_ready, h2_done, h2_ready, h3_done, h3_ready, token_done, token_ready,
         g1_done, g1_ready, g2_done, g2_ready, g3_done, global_ready, kappa_pos, kappa_ready, coupling_ready,
         blended, y_ready) = sems(
            "turned zT_ready h1_done h1_ready h2_done h2_ready h3_done h3_ready token_done token_ready "
            "g1_done g1_ready g2_done g2_ready g3_done global_ready kappa_pos kappa_ready coupling_ready "
            "blended y_ready")

        def column(v, n=P):
            return v.rearrange("(n a) -> n a", a=1) if n == v.shape[0] else \
                v.rearrange("(n a) -> n a", a=1).to_broadcast([n, 1])

        loads = [
            (w1[:, :, :], cn_w1.rearrange("(k p) n -> p k n", p=P)),
            (w2[:, :, :], cn_w2.rearrange("(k p) n -> p k n", p=P)),
            (w3[:, :], cn_w3), (w4[:, :], cn_w4),
            (g1w[:, :, :], gc_w1.rearrange("(k p) n -> p k n", p=P)),
            (g2w[:, :], gc_w2), (g3col[:, :], gc_w3),
            (b1[:, :], cn_b1.rearrange("(k p) -> p k", p=P)),
            (b2[:, :], column(cn_b2)), (b3[:, :], column(cn_b3, 64)),
            (gb1[:, :], column(gc_b1)), (gb2[:, :], column(gc_b2, 64)),
            (b4_half, column(cn_b4)), (gb3_half, column(gc_b3)), (ar[:, :], column(adaptive_range)),
        ]

        with nc.Block() as block:
            @block.sync
            def _(sp):
                with nc.allow_non_contiguous_dma(reason="a few short columns, once"):
                    for c in range(CHAINS):
                        sp.dma_start(xt[c][:, :, :], xs[c]).then_inc(x_loaded[c], 16)
                        if c == 0:
                            for dst, src in loads:
                                sp.dma_start(dst, src).then_inc(loaded, 16)

                def step(it, last):
                    for c in range(CHAINS):
                        sp.wait_ge(y_ready, CHAINS * it + c + 1)
                        if not last:
                            sp.dma_start(xt[c][:, :, :], xs[CHAINS * (it + 1) + c]).then_inc(x_loaded[c], 16)
                        sp.dma_start(ys[CHAINS * it + c], y[c % 2][:, :, :]).then_inc(y_stored[c % 2], 16)

                with sp.Fori(0, n_steps - 1) as it:
                    step(it, False)
                step(n_steps - 1, True)
                for k in range(2):
                    sp.wait_ge(y_stored[k], 16 * (CHAINS // 2) * n_steps)

            @block.gpsimd
            def _(pool):
                nc.gpsimd.memset(eps[:, :], EPS).then_inc(const_ready, 1)
                nc.gpsimd.memset(minus_half[:, :], -0.5).then_inc(const_ready, 1)
                nc.gpsimd.memset(minus_one[:, :], -1.0).then_inc(const_ready, 1)
                pool.wait_ge(const_ready, 3)

                def rstds(n):
                    pool.wait_ge(moments_done, n + 1)
                    nc.gpsimd.tensor_tensor(var_eps[:, :], moments[:, :, 1], eps[:, :], ALU.add).then_inc(eps_added, 1)
                    pool.wait_ge(eps_added, n + 1)
                    nc.gpsimd.tensor_tensor(rstd[:, :], var_eps[:, :], minus_half[:, :], ALU.pow).then_inc(rstd_ready, 1)
                    pool.wait_ge(rstd_ready, n + 1)
                    nc.gpsimd.tensor_tensor(rstd_neg[:, :], rstd[:, :], minus_one[:, :],
                                            ALU.mult).then_inc(rstd_neg_ready, 1)

                def blend(it, c):
                    pool.wait_ge(rotated, 2 * CHAINS * it + CHAINS + c + 1)
                    split = D - QUARTER
                    nc.gpsimd.tensor_tensor(xt[c][:, :, 0:split], xt[c][:, :, 0:split], z[c][2][:, :, 0:split], ALU.add)
                    nc.gpsimd.tensor_tensor(xt[c][:, :, split:D], xt[c][:, :, split:D], z[c][2][:, :, split:D],
                                            ALU.subtract).then_inc(blended, 1)

                def step(it, last):
                    for m in range(SLOTS):
                        if 1 <= m + 1 < CHAINS:
                            rstds(CHAINS * it + m + 1)
                        if m == SLOTS - 1 and not last:
                            rstds(CHAINS * (it + 1))
                        if 2 * CHAINS - 1 <= m < 3 * CHAINS - 1:
                            blend(it, m - (2 * CHAINS - 1))

                rstds(0)
                with pool.Fori(0, n_steps - 1) as it:
                    step(it, False)
                step(n_steps - 1, True)

            @block.vector
            def _(dve):
                v = nc.vector
                dve.wait_ge(loaded, 16 * len(loads))
                v.tensor_scalar(w1[64:P, 1, :], w1[64:P, 1, :], -1.0, None, ALU.mult)
                v.tensor_scalar(g1w[64:P, 1, :], g1w[64:P, 1, :], -1.0, None, ALU.mult)
                v.tensor_scalar(half_bias[:, :], half_bias[:, :], 0.5, None, ALU.mult)
                v.tensor_scalar(ar_cols[:, 0:1], ar[:, :], 0.3, None, ALU.mult)
                v.tensor_scalar(ar_cols[:, 1:2], ar[:, :], -0.3, None, ALU.mult)
                v.tensor_scalar(ar_cols[:, 2:3], ar[:, :], 0.7, None, ALU.mult)
                v.tensor_copy(g3w[:, :], g3col[:, 0:1].to_broadcast([64, P])).then_inc(weights_signed, 1)

                def prepare(it, c):
                    n = CHAINS * it + c
                    dve.wait_ge(x_loaded[c], 16 * it + 16)
                    for t in range(TT):
                        last = v.bn_stats(stats[:, t, :], xt[c][:, t, :])
                    last.then_inc(stats_done, 1)
                    dve.wait_ge(stats_done, n + 1)
                    v.memset(carrier[:, :], 0.0)
                    for t in range(TT):
                        last = v.bn_aggr(moments[:, t, :], stats[:, t, :])
                    last.then_inc(moments_done, 1)
                    dve.wait_ge(rstd_neg_ready, n + 1)
                    split = D - QUARTER
                    for t in range(TT):
                        v.tensor_scalar(z[c][0][:, t, 0:split], xt[c][:, t, 0:split], moments[:, t, 0:1],
                                        rstd[:, t:t + 1], ALU.subtract, ALU.mult)
                        last = v.tensor_scalar(z[c][0][:, t, split:D], xt[c][:, t, split:D], moments[:, t, 0:1],
                                               rstd_neg[:, t:t + 1], ALU.subtract, ALU.mult)
                    last.then_inc(z0_ready, 1)

                def couple(it, m):
                    g, k, j = SLOTS * it + m, m % 2, (m % CHAINS) // NCH
                    if m < CHAINS and m % NCH == 0:
                        dve.wait_ge(global_ready, 2 * it + j + 1)
                        v.tensor_scalar(kappa[:, j, 0:1], tanh_global[:, j:j + 1], ar_cols[:, 2:3], 0.1, ALU.mult,
                                        ALU.add).then_inc(kappa_pos, 1)
                        dve.wait_ge(kappa_pos, 2 * it + j + 1)
                        v.tensor_scalar(kappa[:, j, 1:2], kappa[:, j, 0:1], -1.0, None,
                                        ALU.mult).then_inc(kappa_ready, 1)
                        dve.wait_ge(kappa_ready, 2 * it + j + 1)
                    dve.wait_ge(token_ready, g + 1)
                    v.tensor_scalar(c_pos[k][:, :], tanh_token[k][:, :], ar_cols[:, 0:1], kappa[:, j, 0:1],
                                    ALU.mult, ALU.add)
                    v.tensor_scalar(c_neg[k][:, :], tanh_token[k][:, :], ar_cols[:, 1:2], kappa[:, j, 1:2],
                                    ALU.mult, ALU.add).then_inc(coupling_ready, 1)
                    dve.wait_ge(coupling_ready, g + 1)

                def rotate(it, m):
                    c, cycle, k = m % CHAINS, m // CHAINS, m % 2
                    old, new = z[c][cycle], z[c][cycle + 1]
                    for t in range(TT):
                        a, b = old[:, t, 0:HALF], old[:, t, HALF:D]
                        v.scalar_tensor_tensor(out=new[:, t, 0:HALF], in0=b, scalar=c_pos[k][:, t:t + 1], in1=a,
                                               op0=ALU.mult, op1=ALU.add)
                        last = v.scalar_tensor_tensor(out=new[:, t, HALF:D], in0=a, scalar=c_neg[k][:, t:t + 1],
                                                      in1=b, op0=ALU.mult, op1=ALU.add)
                    last.then_inc(rotated, 1)

                def finish(it, m, old):
                    c, k = m % CHAINS, m % 2
                    split = D - QUARTER
                    dve.wait_ge(blended, CHAINS * it + c + 1)
                    if old or c >= 2:
                        dve.wait_ge(y_stored[c % 2], 16 * ((CHAINS // 2) * it + c // 2))
                    for t in range(TT):
                        a, b, base = z[c][2][:, t, 0:HALF], z[c][2][:, t, HALF:D], xt[c][:, t, :]
                        out = y[c % 2][:, t, :]
                        v.scalar_tensor_tensor(out=out[:, 0:HALF], in0=b, scalar=c_pos[k][:, t:t + 1],
                                               in1=base[:, 0:HALF], op0=ALU.mult, op1=ALU.add)
                        v.scalar_tensor_tensor(out=out[:, HALF:split], in0=a[:, 0:QUARTER],
                                               scalar=c_neg[k][:, t:t + 1], in1=base[:, HALF:split],
                                               op0=ALU.mult, op1=ALU.add)
                        last = v.scalar_tensor_tensor(out=out[:, split:D], in0=a[:, QUARTER:HALF],
                                                      scalar=c_pos[k][:, t:t + 1], in1=base[:, split:D],
                                                      op0=ALU.mult, op1=ALU.add)
                    last.then_inc(y_ready, 1)

                def behind(it, m, old):
                    couple(it, m)
                    if m < 2 * CHAINS:
                        rotate(it, m)
                    else:
                        finish(it, m, old)

                def step(it, first, last):
                    for m in range(SLOTS):
                        if m >= 2:
                            behind(it, m - 2, not first)
                        elif not first:
                            behind(it - 1, SLOTS + m - 2, True)
                        if m + 1 < CHAINS:
                            prepare(it, m + 1)
                        if m == SLOTS - 1 and not last:
                            prepare(it + 1, 0)

                prepare(0, 0)
                step(0, True, False)
                with dve.Fori(1, n_steps - 1) as it:
                    step(it, False, False)
                step(n_steps - 1, False, True)
                for m in range(SLOTS - 2, SLOTS):
                    behind(n_steps - 1, m, True)

            @block.scalar
            def _(act):
                a = nc.scalar.activation

                def gelu3(it, m, old):
                    g, k = SLOTS * it + m, m % 2
                    act.wait_ge(h3_done, g + 1)
                    if old:
                        act.wait_ge(token_done, g - 1)
                    a(h3[k][:, :], h3_ps[0:64, :], ACT.Gelu, bias=b3[:, 0:1]).then_inc(h3_ready, 1)

                def tanh(it, m, old):
                    g, k = SLOTS * it + m, m % 2
                    act.wait_ge(token_done, g + 1)
                    if old:
                        act.wait_ge(coupling_ready, g - 1)
                    a(tanh_token[k][:, :], token_ps[:, 0:TT], ACT.Tanh, bias=b4_half, scale=0.5).then_inc(token_ready, 1)

                def gelu2(it, m, old):
                    g, k = SLOTS * it + m, m % 2
                    act.wait_ge(h2_done, g + 1)
                    if old:
                        act.wait_ge(h3_done, g - 1)
                    a(h2[k][:, :], h2_ps[:, :], ACT.Gelu, bias=b2[:, 0:1]).then_inc(h2_ready, 1)

                def evacuate(it, m, old):
                    g, k = SLOTS * it + m, m % 2
                    act.wait_ge(turned, g + 1)
                    if old:
                        act.wait_ge(h1_done, KT * (g - 1))
                    if m < CHAINS:
                        for f in range(KT):
                            last = a(zT[k][:, f, :], turned_ps[:, f, :], ACT.Copy, accum_out=sums[:, m, f:f + 1])
                    else:
                        last = a(zT[k][:, :, :], turned_ps[:, :, :], ACT.Copy)
                    last.then_inc(zT_ready, 1)

                def gelu1(it, m, f, old):
                    g, k = SLOTS * it + m, m % 2
                    act.wait_ge(h1_done, KT * g + f + 1)
                    if f == 0 and old:
                        act.wait_ge(h2_done, g - 1)
                    last = a(h1[k][:, f, :], h1_ps[:, f, :], ACT.Gelu, bias=b1[:, f:f + 1])
                    if f == KT - 1:
                        last.then_inc(h1_ready, 1)

                def step(it, first):
                    for m in range(SLOTS):
                        old = not first or m >= 2
                        older = not first or m >= 4
                        j = (m - NCH) // NCH if 0 < m <= CHAINS and m % NCH == 0 else None
                        if m >= 2:
                            gelu3(it, m - 2, older)
                        elif not first:
                            gelu3(it - 1, SLOTS + m - 2, True)
                        evacuate(it, m, old)
                        if j is not None:
                            act.wait_ge(g1_done, 2 * it + j + 1)
                            a(g1[:, :], global_ps[:, 0:1], ACT.Gelu, bias=gb1[:, 0:1], scale=1.0 / L).then_inc(g1_ready, 1)
                        if m >= 1:
                            gelu2(it, m - 1, not first or m >= 3)
                        elif not first:
                            gelu2(it - 1, SLOTS - 1, True)
                        if j is not None:
                            act.wait_ge(g2_done, 2 * it + j + 1)
                            a(g2[:, :], global_ps[0:64, 1:2], ACT.Gelu, bias=gb2[:, 0:1]).then_inc(g2_ready, 1)
                        if m >= 2:
                            tanh(it, m - 2, older)
                        elif not first:
                            tanh(it - 1, SLOTS + m - 2, True)
                        gelu1(it, m, 0, old)
                        if j is not None:
                            act.wait_ge(g3_done, 2 * it + j + 1)
                            a(tanh_global[:, j:j + 1], global_ps[:, 2:3], ACT.Tanh, bias=gb3_half,
                              scale=0.5).then_inc(global_ready, 1)
                        gelu1(it, m, 1, old)

                act.wait_ge(weights_signed, 1)
                step(0, True)
                with act.Fori(1, n_steps) as it:
                    step(it, False)
                it = n_steps - 1
                gelu3(it, SLOTS - 2, True)
                gelu2(it, SLOTS - 1, True)
                tanh(it, SLOTS - 2, True)
                gelu3(it, SLOTS - 1, True)
                tanh(it, SLOTS - 1, True)

            @block.tensor
            def _(pe):
                mm = pe.matmul

                def layer3(it, m, first):
                    g, k = SLOTS * it + m, m % 2
                    pe.wait_ge(h2_ready, g + 1)
                    if not first:
                        pe.wait_ge(h3_ready, g)
                    mm(h3_ps[0:64, :], w3[:, :], h2[k][:, :], start=True, stop=True).then_inc(h3_done, 1)

                def layer4(it, m, first):
                    g, k = SLOTS * it + m, m % 2
                    pe.wait_ge(h3_ready, g + 1)
                    if not first:
                        pe.wait_ge(token_ready, g)
                    for t in range(TT):
                        last = mm(token_ps[:, t:t + 1], h3[k][:, t * P:(t + 1) * P], w4[:, 0:1], start=True, stop=True)
                    last.then_inc(token_done, 1)

                def turn(it, m, first):
                    g, c, cycle = SLOTS * it + m, m % CHAINS, m // CHAINS
                    if cycle == 0:
                        pe.wait_ge(z0_ready, CHAINS * it + c + 1)
                    else:
                        pe.wait_ge(rotated, 2 * CHAINS * it + (m - CHAINS) + 1)
                    if not first:
                        pe.wait_ge(zT_ready, g)
                    for f in range(KT):
                        for t in range(TT):
                            last = pe.transpose(turned_ps[:, f, t * P:(t + 1) * P],
                                                z[c][cycle][:, t, f * P:(f + 1) * P], identf[:, :])
                    last.then_inc(turned, 1)

                def layer2(it, m, first):
                    g, k = SLOTS * it + m, m % 2
                    pe.wait_ge(h1_ready, g + 1)
                    if not first:
                        pe.wait_ge(h2_ready, g)
                    for f in range(KT):
                        last = mm(h2_ps[:, :], w2[:, f, :], h1[k][:, f, :], start=(f == 0), stop=(f == KT - 1))
                    last.then_inc(h2_done, 1)

                def layer1(it, m, o, first):
                    g, k = SLOTS * it + m, m % 2
                    if o == 0:
                        pe.wait_ge(zT_ready, g + 1)
                        if not first:
                            pe.wait_ge(h1_ready, g)
                    for f in range(KT):
                        last = mm(h1_ps[:, o, :], w1[:, f, o * P:(o + 1) * P], zT[k][:, f, :],
                                  start=(f == 0), stop=(f == KT - 1))
                    last.then_inc(h1_done, 1)

                def step(it, first):
                    for m in range(SLOTS):
                        j = (m - NCH) // NCH if 0 < m <= CHAINS and m % NCH == 0 else None
                        if m >= 2:
                            layer3(it, m - 2, first and m == 2)
                        elif not first:
                            layer3(it - 1, SLOTS + m - 2, False)
                        turn(it, m, first and m == 0)
                        if j is not None:
                            for i, (c, f) in enumerate([(NCH * j + h, f) for h in range(NCH) for f in range(KT)]):
                                last = mm(global_ps[:, 0:1], g1w[:, f, :], sums[:, c, f:f + 1], start=(i == 0),
                                          stop=(i == NCH * KT - 1))
                            last.then_inc(g1_done, 1)
                        if m >= 1:
                            layer2(it, m - 1, first and m == 1)
                        elif not first:
                            layer2(it - 1, SLOTS - 1, False)
                        if j is not None:
                            pe.wait_ge(g1_ready, 2 * it + j + 1)
                            mm(global_ps[0:64, 1:2], g2w[:, :], g1[:, :], start=True, stop=True).then_inc(g2_done, 1)
                        if m >= 2:
                            layer4(it, m - 2, first and m == 2)
                        elif not first:
                            layer4(it - 1, SLOTS + m - 2, False)
                        layer1(it, m, 0, first and m == 0)
                        if j is not None:
                            pe.wait_ge(g2_ready, 2 * it + j + 1)
                            mm(global_ps[:, 2:3], g3w[:, :], g2[:, :], start=True, stop=True).then_inc(g3_done, 1)
                        layer1(it, m, 1, False)

                pe.wait_ge(weights_signed, 1)
                step(0, True)
                with pe.Fori(1, n_steps) as it:
                    step(it, False)
                it = n_steps - 1
                layer3(it, SLOTS - 2, False)
                layer2(it, SLOTS - 1, False)
                layer4(it, SLOTS - 2, False)
                layer3(it, SLOTS - 1, False)
                layer4(it, SLOTS - 1, False)


def attention_phase(nc, sem, identf, identb, x2, x3, wqkv, bqkv, wproj, bproj, qk_scratch, v_scratch):
    HD = 16
    HT = 64
    BT = P // HD
    NBLK = HT // BT
    HALF_T = HT // 2
    PARTS = 3
    PAIRS_Q, PAIRS_K = (0, 0, 0, 1, 1, 2), (0, 1, 2, 0, 1, 0)
    KROWS = HD * len(PAIRS_Q)
    STEPS, UNITS1, UNITS2 = 40, 9, 10
    NB = x2.shape[0]
    SCALE = 1.0 / np.sqrt(HD)
    PASS1 = [[(7, 0, 32)], [(7, 32, 64)], [(6, 0, 32)], [(6, 32, 56), (0, 0, 8)], [(5, 0, 32)],
             [(5, 32, 48), (1, 0, 16)], [(4, 0, 32)], [(4, 32, 40), (2, 0, 24)], [(3, 0, 32)]]
    PASS2 = [[(0, 0, 32)], [(1, 8, 32), (3, 24, 32)], [(2, 16, 32)],
             [(0, 32, 64)], [(1, 32, 64)], [(2, 32, 64)], [(3, 32, 64)], [(4, 32, 64)],
             [(5, 40, 64), (7, 56, 64)], [(6, 48, 64)]]
    FIRST_U2 = (0, 3)
    LAST_U2 = (2, 9)
    ROWS_AT = [(11, 13), (20, 22), (28, 30), (37, 38)]
    PROJECT_AT = [4, 6, 8, 14, 16, 18, 23, 25]
    NORM_AT = {0: (8, 14), 1: (31, 35), 2: (8, 14), 3: (8, 14)}
    FINISH_AT = [(2, 5), (9, 12), (16, 19), (23, 26)]
    A_OFF, A_TOTAL, A_PROLOGUE = (0, 16, 24, 40), 48, 16
    B_OFF, B_TOTAL, B_SKIPPED = (0, 10, 12, 14), 16, 10

    xs = x2.rearrange("b (c t p) d -> (b c) p t d", c=NCH, p=P)
    xr = x2.rearrange("b (n t c) d -> (b n) c t d", t=BT, c=HD)
    ys = x3.rearrange("b (n t c) d -> (b n) c t d", t=BT, c=HD)

    def a_events(project, pass1):
        events = []
        if project:
            events += [(s, "project", j) for j, s in enumerate(PROJECT_AT)]
        if pass1:
            events += [(s, "rows", (i, e)) for i, at in enumerate(ROWS_AT) for e, s in enumerate(at)]
        return [(s, kind, which, k) for k, (s, kind, which) in enumerate(sorted(events))]

    with ExitStack() as ctx:
        def sb(n, shape, dt=F32):
            return ctx.enter_context(nc.sbuf_tensor("att_" + n, shape, dt))

        def psum(n, shape):
            return ctx.enter_context(nc.psum_tensor("att_" + n, shape, F32))

        staged = sb("staged", [KROWS, HD, CH], BF16)
        qs = [sb(f"qs{s}", [P, HD * CH], BF16) for s in range(2)]
        ks = [sb(f"ks{s}", [P, HD * CH], BF16) for s in range(2)]
        vs = [sb(f"vs{s}", [P, CH * HD // P, 32]) for s in range(2)]
        probs = [[sb(f"probs{k}_{i}", [P, CH]) for i in range(4)] for k in range(2)]
        o_sb = [sb(f"o{k}", [P, 2, CH]) for k in range(2)]
        y_sb = sb("y", [P, L // P, D])
        yT = [sb(f"yT{k}", [P, KT, 2 * P]) for k in range(2)]
        x_res = [sb(f"x_res{k}", [P, 2, D]) for k in range(2)]
        x_bias = [sb(f"x_bias{k}", [P, 2, D]) for k in range(2)]
        out_sb = [sb(f"out{k}", [P, 2, D]) for k in range(2)]
        xt = [sb(f"x{s}", [P, TT, D]) for s in range(2)]
        xn, xnT = sb("xn", [P, TT, D]), sb("xnT", [P, KT, CH])
        whole = [sb(f"whole{k}", [P, CH]) for k in range(2)]
        rest = [sb(f"rest{k}", [P, CH]) for k in range(2)]
        parts = sb("parts", [P, 4, PARTS, CH], BF16)
        v_raw, v_tok = sb("v_raw", [P, TT, D]), sb("v_tok", [P, TT, D])
        wq, wp = sb("wqkv", [P, KT, 3 * D]), sb("wproj", [P, KT, D])
        b_raw, b_qk = sb("b_raw", [P, 4]), sb("b_qk", [P, 4])
        bv_row, bp_row = sb("bv_row", [P, D]), sb("bp_row", [P, D])
        mask_raw = [sb(f"mask_raw{k}", [P, P], BF16) for k in range(2)]
        mask = [sb(f"mask{k}", [P, P], BF16) for k in range(2)]
        stats, moments = sb("stats", [P, TT, 6]), sb("moments", [P, TT, 2])
        var_eps, rstd = sb("var_eps", [P, TT]), sb("rstd", [P, TT])
        eps, minus_half = sb("eps", [P, TT]), sb("minus_half", [P, TT])
        carrier = sb("carrier", [1, 1])
        row_max = [sb(f"row_max{k}", [P, NBLK]) for k in range(2)]
        max_lo = [sb(f"max_lo{k}", [P, NBLK // 2]) for k in range(2)]
        max_hi = [sb(f"max_hi{k}", [P, NBLK // 2]) for k in range(2)]
        neg_parts = [sb(f"neg_parts{k}", [P, NBLK, 32], BF16) for k in range(2)]
        recip = sb("recip", [P, 4, 4])

        s1_ps = [psum(f"s1_{k}", [P, 512]) for k in range(3)]
        s2_ps = [psum(f"s2_{k}", [P, 512]) for k in range(2)]
        o_ps, a_ps, b_ps = psum("o_ps", [P, 512]), psum("a_ps", [P, 512]), psum("b_ps", [P, 512])

        x_loaded = [sem(f"att_x_loaded{s}") for s in range(2)]
        v_loaded = [sem(f"att_v_loaded{s}") for s in range(2)]
        res_loaded = [sem(f"att_res_loaded{k}") for k in range(2)]
        out_stored = [sem(f"att_out_stored{k}") for k in range(2)]
        (loaded, const_ready, zeroed, weights_ready, stats_done, moments_done, eps_added, rstd_ready, xn_ready,
         a_full, a_free, rest_ready, middle_ready, parts_ready, v_ready, q_stored, k_stored, v_stored,
         stack_staged, q_laid_out, k_laid_out, mask_made, mask_ready, s1_full, s1_free,
         row_maxima, row_max_ready, neg_hi_ready, neg_ready, s2_full, exp_done, pv_done, o_free, b_full,
         b_free, recip_ready, bias_added) = [sem("att_" + n) for n in (
             "loaded const_ready zeroed weights_ready stats_done moments_done eps_added rstd_ready xn_ready "
             "a_full a_free rest_ready middle_ready parts_ready v_ready q_stored k_stored v_stored stack_staged q_laid_out k_laid_out mask_made mask_ready s1_full s1_free "
             "row_maxima row_max_ready neg_hi_ready neg_ready s2_full exp_done pv_done o_free b_full "
             "b_free recip_ready bias_added").split()]

        loads = [
            (wq[:, :, :], wqkv.rearrange("(k p) n -> p k n", p=P)),
            (wp[:, :, :], wproj.rearrange("(k p) n -> p k n", p=P)),
            (b_raw[:, :], bqkv[0:2 * D].rearrange("(k p) -> p k", p=P)),
            (bv_row[:, :], bqkv[2 * D:3 * D].rearrange("(a n) -> a n", a=1).to_broadcast([P, D])),
            (bp_row[:, :], bproj.rearrange("(a n) -> a n", a=1).to_broadcast([P, D])),
        ]

        def stack_loads(s, side):
            for g, part in enumerate((PAIRS_Q, PAIRS_K)[side]):
                yield (staged[HD * g:HD * (g + 1), :, :],
                       qk_scratch[s, side, part].rearrange("(c d) t -> d c t", d=HD))

        def v_loads(s):
            src = v_scratch[s].rearrange("(n t c) d -> t c n d", t=BT, c=HD)
            for t in range(BT):
                yield vs[s][t:P:BT, :, 0:HD], src[t]

        N_STACK, N_V = len(PAIRS_Q), BT

        def slots(body):
            def sequence(b, first, last):
                for q in range(4):
                    body(b, q, first, not (last and q == 3), q % 2 == 0 and not (last and q == 2))
            return sequence

        def run(eng, sequence):
            sequence(0, True, False)
            with eng.Fori(1, NB - 1) as b:
                sequence(b, False, False)
            sequence(NB - 1, False, True)

        def coming(b, q):
            return (2 * b + 1, 1, b) if q == 0 else (2 * b + 2, 0, b + 1)

        with nc.Block() as block:
            @block.sync
            def _(sp):
                with nc.allow_non_contiguous_dma(reason="a few short columns, once"):
                    sp.dma_start(xt[0][:, :, :], xs[0]).then_inc(x_loaded[0], 16)
                    for dst, src in loads:
                        sp.dma_start(dst, src).then_inc(loaded, 16)
                sp.dma_start(xt[1][:, :, :], xs[1]).then_inc(x_loaded[1], 16)

                def project(hb, s, turn, first, more):
                    for side, stored in enumerate((q_stored, k_stored)):
                        for o in range(2):
                            sp.wait_ge(parts_ready, 4 * hb + 2 * side + o + 1)
                            sp.dma_start(qk_scratch[s, side].rearrange("r (o p) t -> o p r t", p=P)[o],
                                         parts[:, 2 * side + o, :, :]).then_inc(stored, 16)
                        sp.wait_ge(stored, 32 * (hb + 1))
                        sp.wait_ge((k_laid_out, q_laid_out)[side], 32 * (hb + 1))
                        for dst, src in stack_loads(s, side):
                            sp.dma_start(dst, src).then_inc(stack_staged, 16)
                    sp.wait_ge(v_ready, 2 * hb + 2)
                    if more:
                        sp.dma_start(xt[s][:, :, :], xs[hb + 2]).then_inc(x_loaded[s], 16)
                    if not first:
                        sp.wait_ge(v_loaded[s], 16 * N_V * turn)
                    sp.dma_start(v_scratch[s].rearrange("(t p c) d -> p t (c d)", p=P, c=HD),
                                 v_tok[:, :, :]).then_inc(v_stored, 16)
                    sp.wait_ge(v_stored, 16 * (hb + 1))
                    if not first:
                        sp.wait_ge(pv_done, UNITS2 * (2 * hb - 2))
                    for dst, src in v_loads(s):
                        sp.dma_start(dst, src).then_inc(v_loaded[s], 16)

                def finish_loads(b):
                    for r in range(4):
                        sp.wait_ge(bias_added, 4 * b + r - 1) if r >= 2 else None
                        for n in range(2):
                            sp.dma_start(x_res[r % 2][:, n, :], xr[8 * b + 2 * r + n]).then_inc(res_loaded[r % 2], 16)
                        if r >= 1:
                            finish_store(b, r - 1)
                    finish_store(b, 3)

                def finish_store(b, r):
                    sp.wait_ge(b_free, B_TOTAL * (b + 1) + 2 + 2 * r + 2)
                    for n in range(2):
                        sp.dma_start(ys[8 * b + 2 * r + n], out_sb[r % 2][:, n, :]).then_inc(out_stored[r % 2], 16)

                def sequence(b, first, second_last, last):
                    project(*coming(b, 0), first, not last)
                    if not first:
                        finish_loads(b - 1)
                    if not last:
                        project(*coming(b, 2), False, not second_last)

                for k, m in enumerate(mask_raw):
                    sp.wait_ge(mask_made, k + 1)
                    for t in range(BT):
                        sp.dma_start(mask[k][t:P:BT, :], m[HD * t:HD * (t + 1), :]).then_inc(mask_ready, 16)
                project(0, 0, 0, True, True)
                sequence(0, True, False, False)
                with sp.Fori(1, NB - 2) as b:
                    sequence(b, False, False, False)
                sequence(NB - 2, False, True, False)
                sequence(NB - 1, False, False, True)
                finish_loads(NB - 1)
                for k in range(2):
                    sp.wait_ge(out_stored[k], 64 * NB)

            @block.gpsimd
            def _(pool):
                g = nc.gpsimd
                g.memset(eps[:, :], EPS).then_inc(const_ready, 1)
                g.memset(minus_half[:, :], -0.5).then_inc(const_ready, 1)
                for s in range(2):
                    g.memset(vs[s][:, :, HD:32], 0.0).then_inc(zeroed, 1)
                    g.memset(neg_parts[s][:, :, :], 0.0).then_inc(zeroed, 1)
                for k in range(2):
                    g.memset(mask_raw[k][:, :], 0.0).then_inc(zeroed, 1)
                pool.wait_ge(zeroed, 6)
                for s in range(2):
                    g.memset(vs[s][:, :, HD:HD + 1], 1.0).then_inc(const_ready, 1)
                for k, sign in enumerate((1, -1)):
                    m = mask_raw[k][:, :].rearrange("p (c t) -> p c t", c=HD)
                    g.affine_select(out=m, in_=m, pattern=[[-sign, HD], [-sign * HD, BT]], compare_op=ALU.is_ge,
                                    fill=-1e30, base=0, channel_multiplier=sign).then_inc(mask_made, 1)
                pool.wait_ge(const_ready, 4)

                def rstds(hb):
                    pool.wait_ge(moments_done, hb + 1)
                    g.tensor_tensor(var_eps[:, :], moments[:, :, 1], eps[:, :], ALU.add).then_inc(eps_added, 1)
                    pool.wait_ge(eps_added, hb + 1)
                    g.tensor_tensor(rstd[:, :], var_eps[:, :], minus_half[:, :], ALU.pow).then_inc(rstd_ready, 1)

                def take_rest(hb, j, a_index):
                    pool.wait_ge(a_free, a_index + 1)
                    g.tensor_tensor(rest[j % 2][:, :], whole[j % 2][:, :], parts[:, j, 0, :],
                                    ALU.subtract).then_inc(rest_ready, 1)

                def last_part(hb, j):
                    pool.wait_ge(middle_ready, 4 * hb + j + 1)
                    g.tensor_tensor(parts[:, j, 2, :], rest[j % 2][:, :], parts[:, j, 1, :],
                                    ALU.subtract).then_inc(parts_ready, 1)

                def v_bias(hb, e, a_index):
                    pool.wait_ge(a_free, a_index + 1)
                    g.tensor_tensor(v_tok[:, 2 * e:2 * e + 2, :], v_raw[:, 2 * e:2 * e + 2, :],
                                    bv_row[:, :].unsqueeze(1).to_broadcast([P, 2, D]), ALU.add).then_inc(v_ready, 1)

                def a_index_of(b, q, project_j):
                    if b is None:
                        return project_j
                    k = {w: k for _, kind, w, k in a_events(True, True) if kind == "project"}[project_j]
                    return A_PROLOGUE + A_TOTAL * b + A_OFF[q] + k

                def project_tasks(hb, b, q):
                    yield 1, lambda: rstds(hb)
                    for j in range(4):
                        at = PROJECT_AT[2 + j]
                        yield at + 2, lambda j=j: take_rest(hb, j, a_index_of(b, q, 2 + j))
                        yield at + 4, lambda j=j: last_part(hb, j)
                    for e in range(2):
                        yield PROJECT_AT[6 + e] + 2, lambda e=e: v_bias(hb, e, a_index_of(b, q, 6 + e))

                def bias(b, r):
                    pool.wait_ge(res_loaded[r % 2], 64 * b + 32 * (r // 2) + 32)
                    if not isinstance(b, int) or 4 * b + r >= 2:
                        pool.wait_ge(b_free, B_TOTAL * (b + 1 if r >= 2 else b) + 2 + 2 * ((r - 2) % 4) + 2)
                    g.tensor_tensor(x_bias[r % 2][:, :, :], x_res[r % 2][:, :, :],
                                    bp_row[:, :].unsqueeze(1).to_broadcast([P, 2, D]), ALU.add).then_inc(bias_added, 1)

                def slot(b, q, first, pass1, projects):
                    tasks = list(project_tasks(coming(b, q)[0], b, q)) if projects else []
                    if q == 1 and not first:
                        tasks += [(FINISH_AT[r][0], lambda r=r: bias(b - 1, r)) for r in range(4)]
                    for step in range(STEPS):
                        for at, task in tasks:
                            if at == step:
                                task()

                pool.wait_ge(loaded, 16 * len(loads))
                for _, task in sorted(project_tasks(0, None, 0), key=lambda x: x[0]):
                    task()
                run(pool, slots(slot))
                for r in range(4):
                    bias(NB - 1, r)

            @block.vector
            def _(dve):
                v = nc.vector

                def prepare(hb, s, turn):
                    dve.wait_ge(x_loaded[s], 16 * turn + 16)
                    for t in range(TT):
                        last = v.bn_stats(stats[:, t, :], xt[s][:, t, :])
                    last.then_inc(stats_done, 1)
                    dve.wait_ge(stats_done, hb + 1)
                    v.memset(carrier[:, :], 0.0)
                    for t in range(TT):
                        last = v.bn_aggr(moments[:, t, :], stats[:, t, :])
                    last.then_inc(moments_done, 1)

                def normalise(hb, s):
                    dve.wait_ge(rstd_ready, hb + 1)
                    for t in range(TT):
                        last = v.tensor_scalar(xn[:, t, :], xt[s][:, t, :], moments[:, t, 0:1], rstd[:, t:t + 1],
                                               ALU.subtract, ALU.mult)
                    last.then_inc(xn_ready, 1)

                def lay_out(hb, s, side, e):
                    stack = (qs, ks)[side][s]
                    if e == 0:
                        dve.wait_ge(stack_staged, 16 * N_STACK * (2 * hb + side + 1))
                    n = CH // BT // 2
                    last = v.tensor_copy(
                        stack[0:KROWS, :].rearrange("p (n c t) -> p n c t", c=HD, t=BT)[:, e * n:(e + 1) * n],
                        staged[:, :, :].rearrange("p c (n t) -> p n c t", t=BT)[:, e * n:(e + 1) * n])
                    if e:
                        last.then_inc((q_laid_out, k_laid_out)[side], 32)

                def middle_part(hb, j):
                    dve.wait_ge(rest_ready, 4 * hb + j + 1)
                    v.tensor_copy(parts[:, j, 1, :], rest[j % 2][:, :]).then_inc(middle_ready, 1)

                def maxima(q_next, step):
                    i, unit, k = step // UNITS1, PASS1[step % UNITS1], (step // UNITS1) % 2
                    dve.wait_ge(s1_full, 4 * UNITS1 * q_next + step + 1)
                    col = 0
                    for blk, t0, t1 in unit:
                        n = HD * (t1 - t0)
                        dst = row_max[k][:, blk:blk + 1] if blk < 4 else \
                            (max_hi if t0 else max_lo)[k][:, blk - 4:blk - 3]
                        last = v.tensor_reduce(dst, s1_ps[step % 3][:, col:col + n], AX.X, ALU.max)
                        col += n
                    last.then_inc(s1_free, 1)
                    if step % UNITS1 == UNITS1 - 1:
                        n = 4 * q_next + i
                        dve.wait_ge(s1_free, 4 * UNITS1 * q_next + step + 1)
                        v.tensor_tensor(row_max[k][:, 4:8], max_lo[k][:, :], max_hi[k][:, :],
                                        ALU.max).then_inc(row_max_ready, 1)
                        dve.wait_ge(row_max_ready, n + 1)
                        v.tensor_scalar(neg_parts[k][:, :, 0], row_max[k][:, :], -1.0, None,
                                        ALU.mult).then_inc(neg_hi_ready, 1)
                        dve.wait_ge(neg_hi_ready, n + 1)
                        v.scalar_tensor_tensor(out=neg_parts[k][:, :, 1], in0=row_max[k][:, :], scalar=-1.0,
                                               in1=neg_parts[k][:, :, 0], op0=ALU.mult,
                                               op1=ALU.subtract).then_inc(neg_ready, 1)

                def evacuate(quad, k, half):
                    dve.wait_ge(pv_done, UNITS2 * quad + LAST_U2[half] + 1)
                    v.tensor_copy(o_sb[k][:, half, :], o_ps[:, :]).then_inc(o_free, 1)

                def divide(b_index, quad, q, e):
                    dve.wait_ge(b_full, b_index + 1)
                    heads = b_ps[:, :].rearrange("p (n h w) -> p n h w", n=4, h=4)
                    v.reciprocal(recip[:, :, :], heads[:, :, :, HD]).then_inc(recip_ready, 1)
                    dve.wait_ge(recip_ready, 2 * quad + e + 1)
                    v.tensor_tensor(
                        y_sb[:, 4 * e:4 * e + 4, 64 * q:64 * q + 64].rearrange("p n (h w) -> p n h w", h=4),
                        heads[:, :, :, 0:HD], recip[:, :, :].unsqueeze(3).to_broadcast([P, 4, 4, HD]),
                        ALU.mult).then_inc(b_free, 1)

                def finish_turn(b_index, r):
                    dve.wait_ge(b_full, b_index + 1)
                    v.tensor_copy(yT[r % 2][:, :, :], b_ps[:, :].rearrange("p (k n) -> p k n", k=KT)).then_inc(b_free, 1)

                def finish_add(b_index, b, r):
                    dve.wait_ge(b_full, b_index + 1)
                    dve.wait_ge(bias_added, 4 * b + r + 1)
                    if not isinstance(b, int) or 4 * b + r >= 2:
                        dve.wait_ge(out_stored[r % 2], 64 * b + 32 * (r // 2))
                    v.tensor_tensor(out_sb[r % 2][:, :, :], b_ps[:, :].rearrange("p (t d) -> p t d", t=2),
                                    x_bias[r % 2][:, :, :], ALU.add).then_inc(b_free, 1)

                def divide_tasks(b, q_done, base, at):
                    for e in range(2):
                        yield at[e] + 1, lambda e=e: divide(base + e, 4 * b + q_done, q_done, e)

                def finish_tasks(b, base):
                    for r, (turn_at, add_at) in enumerate(FINISH_AT):
                        yield turn_at + 1, lambda r=r: finish_turn(base + 2 * r, r)
                        yield add_at + 1, lambda r=r: finish_add(base + 2 * r + 1, b, r)

                def slot(b, q, first, pass1, projects):
                    tasks = []
                    base = B_TOTAL * b - B_SKIPPED
                    if projects:
                        hb, s, turn = coming(b, q)
                        tasks += [(0, lambda: prepare(hb, s, turn)), (3, lambda: normalise(hb, s))]
                        tasks += [(PROJECT_AT[2 + j] + 3, lambda j=j: middle_part(hb, j)) for j in range(4)]
                        tasks += [(at, lambda side=side, e=e: lay_out(hb, s, side, e))
                                  for at, side, e in ((29, 0, 0), (30, 0, 1), (38, 1, 0), (39, 1, 1))]
                    if q == 0 and not first:
                        tasks += [(4, lambda: evacuate(4 * b - 1, 1, 1))]
                        tasks += divide_tasks(b - 1, 3, base, NORM_AT[0])
                    if q > 0:
                        tasks += [(4, lambda: evacuate(4 * b + q - 1, (q - 1) % 2, 1))]
                    if q == 1 and not first:
                        tasks += finish_tasks(b - 1, base + 2)
                    if q > 0:
                        tasks += divide_tasks(b, q - 1, base + B_OFF[q], NORM_AT[q])
                    tasks += [(16, lambda: evacuate(4 * b + q, q % 2, 0))]
                    for step in range(STEPS):
                        if pass1 and step < 4 * UNITS1:
                            maxima(4 * b + q + 1, step)
                        for at, task in tasks:
                            if at == step:
                                task()

                dve.wait_ge(loaded, 16 * len(loads))
                dve.wait_ge(const_ready, 4)
                v.memset(ks[0][KROWS:P, :], 1.0)
                v.memset(ks[1][KROWS:P, :], 1.0).then_inc(k_laid_out, 32)
                v.memset(carrier[:, :], 0.0).then_inc(b_free, B_SKIPPED)
                v.tensor_scalar(b_qk[:, 0:2], b_raw[:, 0:2], SCALE, None, ALU.mult)
                v.tensor_copy(b_qk[:, 2:4], b_raw[:, 2:4]).then_inc(weights_ready, 1)
                prepare(0, 0, 0)
                normalise(0, 0)
                for j in range(4):
                    middle_part(0, j)
                for side in range(2):
                    for e in range(2):
                        lay_out(0, 0, side, e)
                for step in range(4 * UNITS1):
                    maxima(0, step)
                run(dve, slots(slot))
                evacuate(4 * NB - 1, 1, 1)
                base = B_TOTAL * NB - B_SKIPPED
                for at, task in sorted(divide_tasks(NB - 1, 3, base, (0, 1)), key=lambda x: x[0]):
                    task()
                for at, task in sorted(finish_tasks(NB - 1, base + 2), key=lambda x: x[0]):
                    task()

            @block.scalar
            def _(act):
                a = nc.scalar.activation

                def exponentiate(b, q, step, old):
                    u, i = step // 4, step % 4
                    quad = 4 * b + q
                    act.wait_ge(s2_full, STEPS * quad + step + 1)
                    if old or u >= 2:
                        act.wait_ge(pv_done, UNITS2 * quad + u - 1)
                    n = sum(HD * (t1 - t0) for _, t0, t1 in PASS2[u])
                    a(probs[u % 2][i][:, 0:n], s2_ps[step % 2][:, 0:n], ACT.Exp).then_inc(exp_done, 1)

                def project(j, a_index, hb, old):
                    act.wait_ge(a_full, a_index + 1)
                    if j < 2:
                        a(xnT[:, j, :], a_ps[:, :], ACT.Copy).then_inc(a_free, 1)
                    elif j < 6:
                        j -= 2
                        if j >= 2:
                            act.wait_ge(rest_ready, 4 * hb + j - 1)
                        elif old:
                            act.wait_ge(rest_ready, 4 * hb + j - 1)
                        if old:
                            act.wait_ge((q_stored, k_stored)[j // 2], 32 * hb)
                        scale = SCALE if j < 2 else 1.0
                        a(whole[j % 2][:, :], a_ps[:, :], ACT.Identity, bias=b_qk[:, j:j + 1], scale=scale)
                        a(parts[:, j, 0, :], a_ps[:, :], ACT.Identity, bias=b_qk[:, j:j + 1],
                          scale=scale).then_inc(a_free, 1)
                    else:
                        e = j - 6
                        a(v_raw[:, 2 * e:2 * e + 2, :], a_ps[:, :].rearrange("p (t d) -> p t d", t=2),
                          ACT.Copy).then_inc(a_free, 1)

                def rows(s, head, e, a_index):
                    act.wait_ge(a_full, a_index + 1)
                    n0 = HD * (HT * head + HALF_T * e)
                    a(qs[s][KROWS:P, n0:n0 + CH], a_ps[KROWS:P, :], ACT.Copy).then_inc(a_free, 1)

                def a_tasks(b, q, projects, pass1, base, hb, old):
                    for step, kind, which, k in a_events(projects, pass1):
                        if kind == "project":
                            yield step + 1, lambda which=which, k=k: project(which, base + k, hb, old)
                        else:
                            i, e = which
                            s1, head = ((q + 1) // 2) % 2, 4 * ((q + 1) % 2) + i
                            yield step + 1, lambda s1=s1, head=head, e=e, k=k: rows(s1, head, e, base + k)

                def slot(b, q, first, pass1, projects):
                    base = A_PROLOGUE + A_TOTAL * b + A_OFF[q]
                    hb = coming(b, q)[0] if projects else None
                    tasks = list(a_tasks(b, q, projects, pass1, base, hb, True))
                    for step in range(STEPS):
                        exponentiate(b, q, step, not first or q > 0)
                        for at, task in tasks:
                            if at == step:
                                task()

                act.wait_ge(weights_ready, 1)
                for j in range(8):
                    project(j, j, 0, False)
                for _, task in a_tasks(None, -1, False, True, 8, None, True):
                    task()
                run(act, slots(slot))

            @block.tensor
            def _(pe):
                mm = pe.matmul

                def block_of(stack, rows, head, blk):
                    return span_of(stack, rows, head, BT * blk, BT * (blk + 1))

                def span_of(stack, rows, head, t0, t1):
                    return stack[0:rows, HD * (HT * head + t0):HD * (HT * head + t1)]

                def pass_one(q_next, quad_in_seq, step):
                    i, unit = step // UNITS1, PASS1[step % UNITS1]
                    s, head = quad_in_seq // 2, 4 * (quad_in_seq % 2) + i
                    if not isinstance(q_next, int) or q_next > 0 or step >= 3:
                        pe.wait_ge(s1_free, 4 * UNITS1 * q_next + step - 2)
                    col = 0
                    for blk, t0, t1 in unit:
                        n = t1 - t0
                        out = s1_ps[step % 3][:, col:col + HD * n]
                        diagonal = t1 == BT * (blk + 1)
                        last = mm(out, block_of(qs[s], KROWS, head, blk), span_of(ks[s], KROWS, head, t0, t1),
                                  start=True, stop=not diagonal)
                        if diagonal:
                            last = mm(out[:, HD * n - P:HD * n], identb[:, :], mask[0][:, :], start=False, stop=True)
                        col += HD * n
                    last.then_inc(s1_full, 1)

                def rows(q_next, i, e, a_index, first):
                    pe.wait_ge(neg_ready, 4 * q_next + i + 1)
                    if not first:
                        pe.wait_ge(a_free, a_index)
                    for n in range(4):
                        last = mm(a_ps[KROWS:P, n * P:(n + 1) * P], neg_parts[i % 2][:, 4 * e + n, :], identb[:, :],
                                  start=True, stop=True)
                    last.then_inc(a_full, 1)

                def pass_two(b, q, step, row_index, old):
                    u, i = step // 4, step % 4
                    s, head = q // 2, 4 * (q % 2) + i
                    if old or step >= 2:
                        pe.wait_ge(exp_done, STEPS * (4 * b + q) + step - 1)
                    if u == 0:
                        pe.wait_ge(a_free, row_index + 1)
                    col = 0
                    for j, t0, t1 in PASS2[u]:
                        n = HD * (t1 - t0)
                        diagonal = t0 == BT * j
                        last = mm(s2_ps[step % 2][:, col:col + n], block_of(ks[s], P, head, j),
                                  span_of(qs[s], P, head, t0, t1), start=True, stop=not diagonal)
                        if diagonal:
                            last = mm(s2_ps[step % 2][:, col:col + P], identb[:, :], mask[1][:, :], start=False,
                                      stop=True)
                        col += n
                    last.then_inc(s2_full, 1)

                def times_v(b, q, u, old):
                    quad, s = 4 * b + q, q // 2
                    half = 0 if u <= LAST_U2[0] else 1
                    if u == FIRST_U2[0] and old:
                        pe.wait_ge(o_free, 2 * quad)
                    if u == FIRST_U2[1]:
                        pe.wait_ge(o_free, 2 * quad + 1)
                    pe.wait_ge(exp_done, STEPS * quad + 4 * u + 4)
                    if u == 0 and q % 2 == 0:
                        pe.wait_ge(v_loaded[s], 16 * N_V * ((b if q < 2 else b) + 1))
                    col = 0
                    for n_piece, (j, t0, t1) in enumerate(PASS2[u]):
                        n = t1 - t0
                        for i in range(4):
                            head = 4 * (q % 2) + i
                            first_t = HALF_T * half
                            last = mm(o_ps[32 * i:32 * i + 32, HD * (t0 - first_t):HD * (t1 - first_t)],
                                      vs[s][:, NBLK * head + j, :],
                                      probs[u % 2][i][:, col:col + HD * n],
                                      start=(u == FIRST_U2[half]), stop=(u == LAST_U2[half] and n_piece == len(PASS2[u]) - 1))
                        col += HD * n
                    last.then_inc(pv_done, 1)

                def project(j, s, a_index, first):
                    if j == 0:
                        pe.wait_ge(xn_ready, project.hb + 1)
                    if not first:
                        pe.wait_ge(a_free, a_index)
                    if j < 2:
                        for t in range(TT):
                            last = pe.transpose(a_ps[:, t * P:(t + 1) * P], xn[:, t, j * P:(j + 1) * P], identf[:, :])
                    elif j < 6:
                        cols = slice((j - 2) * P, (j - 1) * P)
                        for f in range(KT):
                            last = mm(a_ps[:, :], wq[:, f, cols], xnT[:, f, :], start=(f == 0), stop=(f == KT - 1))
                    else:
                        for t in range(2):
                            tok = slice((2 * (j - 6) + t) * P, (2 * (j - 6) + t + 1) * P)
                            for f in range(KT):
                                last = mm(a_ps[:, t * D:(t + 1) * D], xnT[:, f, tok], wq[:, f, 2 * D:3 * D],
                                          start=(f == 0), stop=(f == KT - 1))
                    last.then_inc(a_full, 1)

                def turn_heads(quad, k, b_index, e, first):
                    pe.wait_ge(o_free, 2 * quad + 2)
                    pe.wait_ge(b_free, b_index + B_SKIPPED)
                    for n in range(4):
                        last = pe.transpose(b_ps[:, n * P:(n + 1) * P], o_sb[k][:, e, n * P:(n + 1) * P], identf[:, :])
                    last.then_inc(b_full, 1)

                def finish_turn(b_index, r):
                    pe.wait_ge(b_free, b_index + B_SKIPPED)
                    for f in range(KT):
                        for t in range(2):
                            last = pe.transpose(b_ps[:, (2 * f + t) * P:(2 * f + t + 1) * P],
                                                y_sb[:, 2 * r + t, f * P:(f + 1) * P], identf[:, :])
                    last.then_inc(b_full, 1)

                def finish_project(b_index, r):
                    pe.wait_ge(b_free, b_index + B_SKIPPED)
                    for t in range(2):
                        for f in range(KT):
                            last = mm(b_ps[:, t * D:(t + 1) * D], yT[r % 2][:, f, t * P:(t + 1) * P], wp[:, f, :],
                                      start=(f == 0), stop=(f == KT - 1))
                    last.then_inc(b_full, 1)

                def heads_tasks(quad, k, base, at, first):
                    for e in range(2):
                        yield at[e], lambda e=e: turn_heads(quad, k, base + e, e, first and e == 0)

                def finish_tasks(base):
                    for r, (turn_at, project_at) in enumerate(FINISH_AT):
                        yield turn_at, lambda r=r: finish_turn(base + 2 * r, r)
                        yield project_at, lambda r=r: finish_project(base + 2 * r + 1, r)

                def row_use(projects, i):
                    return [k for _, kind, w, k in a_events(projects, True) if kind == "rows" and w == (i, 1)][0]

                def slot(b, q, first, pass1, projects):
                    a_base = A_PROLOGUE + A_TOTAL * b + A_OFF[q]
                    b_base = B_TOTAL * b - B_SKIPPED
                    tasks = []
                    s = coming(b, q)[1]
                    for step, kind, which, k in a_events(projects, pass1):
                        if kind == "project":
                            def task(which=which, k=k):
                                project.hb = coming(b, q)[0]
                                project(which, s, a_base + k, False)
                        else:
                            def task(which=which, k=k):
                                rows(4 * b + q + 1, which[0], which[1], a_base + k, False)
                        tasks.append((step, task))
                    if q == 0 and not first:
                        tasks += heads_tasks(4 * b - 1, 1, b_base, NORM_AT[0], False)
                    if q == 1 and not first:
                        tasks += finish_tasks(b_base + 2)
                    if q > 0:
                        tasks += heads_tasks(4 * b + q - 1, (q - 1) % 2, b_base + B_OFF[q], NORM_AT[q], first and q == 1)
                    for step in range(STEPS):
                        u, i = step // 4, step % 4
                        if pass1 and step < 4 * UNITS1:
                            if step == 0 and q in (1, 3):
                                pe.wait_ge(k_laid_out, 32 * (2 * b + 3 if q == 1 else 2 * b + 4))
                            pass_one(4 * b + q + 1, (q + 1) % 4, step)
                        before = (q - 1) % 4
                        row_base = A_PROLOGUE + A_TOTAL * (b if q else b - 1) + A_OFF[before]
                        k = row_use(before % 2 == 0 and pass1, i)
                        if first and q == 0:
                            row_base = 8
                        pass_two(b, q, step, row_base + k, not first or q > 0)
                        if i == 3:
                            if u > 0:
                                times_v(b, q, u - 1, not first or q > 0)
                            elif q > 0:
                                times_v(b, q - 1, UNITS2 - 1, True)
                            elif not first:
                                times_v(b - 1, 3, UNITS2 - 1, True)
                        for at, task in tasks:
                            if at == step:
                                task()

                pe.wait_ge(weights_ready, 1)
                project.hb = 0
                for j in range(8):
                    project(j, 0, j, j == 0)
                pe.wait_ge(k_laid_out, 64)
                pe.wait_ge(mask_ready, 32 * BT)
                rows_at = {at: w for at, kind, w, k in a_events(False, True)}
                for step in range(STEPS):
                    if step < 4 * UNITS1:
                        pass_one(0, 0, step)
                    if step in rows_at:
                        i, e = rows_at[step]
                        rows(0, i, e, 8 + 2 * i + e, False)
                run(pe, slots(slot))
                times_v(NB - 1, 3, UNITS2 - 1, True)
                b_base = B_TOTAL * NB - B_SKIPPED
                for _, task in sorted(heads_tasks(4 * NB - 1, 1, b_base, (0, 1), False), key=lambda x: x[0]):
                    task()
                for _, task in sorted(finish_tasks(b_base + 2), key=lambda x: x[0]):
                    task()


def mixed_layer(nc, ins, out):
    x, ssm, attention = ins[0], ins[1:11], ins[11:15]
    coupling, global_context, adaptive_range = ins[15:23], ins[23:29], ins[29]
    x1, x2, x3 = [nc.dram_tensor(n, x.shape, F32).ap() for n in ("x1", "x2", "x3")]
    qk_scratch = nc.dram_tensor("qk_scratch", (NCH, 2, 3, D, CH), BF16).ap()
    v_scratch = nc.dram_tensor("v_scratch", (NCH, CH * 16, 16), F32).ap()
    with ExitStack() as ctx:
        def sem(name):
            return ctx.enter_context(nc.semaphore(name))

        identf = ctx.enter_context(nc.sbuf_tensor("identf", [P, P], F32))
        identb = ctx.enter_context(nc.sbuf_tensor("identb", [P, P], BF16))
        make_identities(nc, sem, identf, identb)
        ssm_phase(nc, sem, identf, x, x1, *ssm)
        ffn_phase(nc, sem, "ffn1_", identf, x1, x2, coupling, global_context, adaptive_range)
        attention_phase(nc, sem, identf, identb, x2, x3, *attention, qk_scratch, v_scratch)
        ffn_phase(nc, sem, "ffn2_", identf, x3, out, coupling, global_context, adaptive_range)


_INS = ["L0_attn_a_x", "L0_attn_a_log_Lam_real", "L0_attn_a_Lam_imag", "L0_attn_a_B_real", "L0_attn_a_B_imag",
        "L0_attn_a_C_real", "L0_attn_a_C_imag", "L0_attn_a_D", "L0_attn_a_log_dt", "L0_attn_a_W_out",
        "L0_attn_a_b_out", "L0_attn_b_Wqkv", "L0_attn_b_bqkv", "L0_attn_b_Wproj", "L0_attn_b_bproj",
        "L0_ffn_cn_w1", "L0_ffn_cn_b1", "L0_ffn_cn_w2", "L0_ffn_cn_b2", "L0_ffn_cn_w3", "L0_ffn_cn_b3",
        "L0_ffn_cn_w4", "L0_ffn_cn_b4", "L0_ffn_gc_w1", "L0_ffn_gc_b1", "L0_ffn_gc_w2", "L0_ffn_gc_b2",
        "L0_ffn_gc_w3", "L0_ffn_gc_b3", "L0_ffn_adaptive_range"]


def kernel(**inputs):
    import numpy as _np
    import concourse.bacc as _bacc
    from concourse import mybir as _mybir
    from concourse.bass_utils import run_bass_kernel_spmd as _run

    nc = _bacc.Bacc("TRN2", target_bir_lowering=False, num_devices=1)
    arrays, args = {}, []
    for name in _INS:
        a = _np.ascontiguousarray(inputs[name])
        arrays[f"in_{name}_dram"] = a
        args.append(nc.dram_tensor(f"in_{name}_dram", a.shape, _mybir.dt.from_np(a.dtype), kind="ExternalInput").ap())
    shape = inputs["L0_attn_a_x"].shape
    out = nc.dram_tensor("out_0_dram", shape, _mybir.dt.float32, kind="ExternalOutput").ap()
    mixed_layer(nc, args, out)
    r = _run(nc, [arrays], core_ids=[0])
    return r.results[0]["out_0_dram"]
```

```python
from contextlib import ExitStack

import numpy as np

import concourse.bass as bass
from concourse import mybir

F32 = mybir.dt.float32
BF16 = mybir.dt.bfloat16
F32R = mybir.dt.float32r
I32 = mybir.dt.int32
ALU = mybir.AluOpType
ACT = mybir.ActivationFunctionType
AX = mybir.AxisListType

P = 128
D = 256
KT = D // P
L = 1024
CH = 512
TT = CH // P
NCH = L // CH
EPS = 1e-5
ROUND = 1.5 * 2.0 ** 23
TWO_PI = float(np.nextafter(np.float32(2 * np.pi), np.float32(0)))


class Chain:

    def __init__(self, eng, sem):
        self.eng, self.sem, self.n = eng, sem, 0

    def __call__(self, instruction):
        self.n += 1
        instruction.then_inc(self.sem, 1)
        self.eng.wait_ge(self.sem, self.n)


def make_identities(nc, sem, identf, identb):
    identity_zero, identity_one = sem("identity_zero"), sem("identity_one")
    with nc.Block() as block:
        @block.gpsimd
        def _(pool):
            nc.gpsimd.memset(identf[:, :], 0.0).then_inc(identity_zero, 1)
            nc.gpsimd.memset(identb[:, :], 0.0).then_inc(identity_zero, 1)
            pool.wait_ge(identity_zero, 2)
            for m in (identf, identb):
                nc.gpsimd.affine_select(out=m[:, :], in_=m[:, :], compare_op=ALU.not_equal, fill=1.0, base=0,
                                        pattern=[[-1, P]], channel_multiplier=1).then_inc(identity_one, 1)
            pool.wait_ge(identity_one, 2)


def ssm_phase(nc, sem, identf, x, x1, log_lam, lam_imag, b_real, b_imag, c_real, c_imag, d_skip, log_dt,
              w_out, b_out):
    N = log_lam.shape[0]
    n_chunks = x.shape[0] * NCH
    H2 = 2 * N
    assert H2 == P
    xs = x.rearrange("b (c t p) d -> (b c) p t d", c=NCH, p=P)
    x1s = x1.rearrange("b (c t p) d -> (b c) p t d", c=NCH, p=P)
    with ExitStack() as ctx:
        def sb(name, shape, dt=F32):
            return ctx.enter_context(nc.sbuf_tensor("ssm_" + name, shape, dt))

        cos_t, sin_t = sb("cos", [P, L]), sb("sin", [P, L])
        decay = sb("decay", [P, 1])
        bu_w = sb("bu_w", [P, KT, P])
        bu_turned_w = sb("bu_turned_w", [P, KT, P])
        out_cos_w = sb("out_cos_w", [P, D])
        out_sin_w = sb("out_sin_w", [P, D])
        skip_w = sb("skip_w", [P, KT, D])
        bias_row = sb("bias_row", [P, D])
        bu_parts, bu_turned_parts = [[sb(f"{n}{i}", [P, KT, P], F32R) for i in range(2)] for n in ("bu_p", "bu_turned_p")]
        skip_parts = [sb(f"skip_p{i}", [P, KT, D], F32R) for i in range(2)]

        with ExitStack() as pre:
            def sbp(name, shape, dt=F32):
                return pre.enter_context(nc.sbuf_tensor("ssm_pre_" + name, shape, dt))

            bst = sbp("bst", [P, D])
            bst_dt = sbp("bst_dt", [P, D])
            cst = sbp("cst", [P, KT, 2, N])
            cl_cos, cl_sin = sbp("cl_cos", [P, KT, P]), sbp("cl_sin", [P, KT, P])
            wo = sbp("wo", [P, KT, D])
            wt = sbp("wt", [P, KT, D])
            dv = sbp("dv", [P, KT])
            col = sbp("col", [P, 40])
            steps_i = sbp("steps_i", [P, L], I32)
            steps = sbp("steps", [P, L])
            ang, tmp = sbp("ang", [P, L]), sbp("tmp", [P, L])
            euler = sbp("euler", [P, 1])
            bits = sbp("bits", [P, 4], BF16)
            t_ps = pre.enter_context(nc.psum_tensor("ssm_pre_t", [P, 4, 512], F32))
            m_ps = pre.enter_context(nc.psum_tensor("ssm_pre_m", [P, 2, 512], F32))
            names = ("loaded", "pool_step", "column_step", "dt_ready", "decay_ready", "bst_scaled", "w_turned",
                     "weights_step", "w_evacuated", "out_w_ready", "angle_ready", "cos_angle_ready",
                     "table_done", "steps_ready")
            (loaded, pool_step, column_step, dt_ready, decay_ready, bst_scaled, w_turned, weights_step,
             w_evacuated, out_w_ready, angle_ready, cos_angle_ready, table_done, steps_ready) = [
                 sem("ssm_pre_" + n) for n in names]
            loads = [
                (col[0:N, 0:1], log_lam.rearrange("(n a) -> n a", a=1)),
                (col[N:P, 0:1], log_lam.rearrange("(n a) -> n a", a=1)),
                (col[0:N, 1:2], lam_imag.rearrange("(n a) -> n a", a=1)),
                (col[N:P, 1:2], lam_imag.rearrange("(n a) -> n a", a=1)),
                (col[:, 2:3], log_dt.rearrange("(n a) -> n a", a=1).to_broadcast([P, 1])),
                (bst[0:N, :], b_real),
                (bst[N:P, :], b_imag),
                (cst[:, :, 0, :], c_real.rearrange("(k p) n -> p k n", p=P)),
                (cst[:, :, 1, :], c_imag.rearrange("(k p) n -> p k n", p=P)),
                (wo[:, :, :], w_out.rearrange("(k p) h -> p k h", p=P)),
                (dv[:, :], d_skip.rearrange("(k p) -> p k", p=P)),
                (bias_row[:, :], b_out.rearrange("(a d) -> a d", a=1).to_broadcast([P, D])),
            ]
            with nc.Block() as block:
                @block.sync
                def _(sp):
                    with nc.allow_non_contiguous_dma(reason="a few short columns, once"):
                        for dst, src in loads:
                            sp.dma_start(dst, src).then_inc(loaded, 16)

                @block.gpsimd
                def _(pool):
                    step = Chain(pool, pool_step)
                    step(nc.gpsimd.memset(euler[:, :], float(np.e)))
                    step(nc.gpsimd.iota(steps_i[:, :], [[1, L]], base=0, channel_multiplier=0))
                    nc.gpsimd.tensor_copy(steps[:, :], steps_i[:, :]).then_inc(steps_ready, 1)
                    pool.wait_ge(loaded, 16 * len(loads))
                    nc.gpsimd.tensor_tensor(col[:, 3:4], euler[:, :], col[:, 2:3], ALU.pow).then_inc(dt_ready, 1)
                    step(nc.gpsimd.tensor_tensor(col[:, 4:5], euler[:, :], col[:, 0:1], ALU.pow))
                    pool.wait_ge(dt_ready, 1)
                    step(nc.gpsimd.tensor_tensor(col[:, 5:6], col[:, 4:5], col[:, 3:4], ALU.mult))
                    step(nc.gpsimd.tensor_scalar(col[:, 6:7], col[:, 5:6], -1.0, 0.0, ALU.mult, ALU.add))
                    nc.gpsimd.tensor_tensor(decay[:, :], euler[:, :], col[:, 6:7], ALU.pow).then_inc(decay_ready, 1)
                    pool.wait_ge(decay_ready, 1)

                @block.vector
                def _(dve):
                    step = Chain(dve, column_step)
                    v = nc.vector
                    dve.wait_ge(dt_ready, 1)
                    v.tensor_scalar(bst_dt[:, :], bst[:, :], col[:, 3:4], None, ALU.mult).then_inc(bst_scaled, 1)
                    v.tensor_scalar(cl_cos[:, :, 0:N], cst[:, :, 0, :], 1.0, None, ALU.mult)
                    v.tensor_scalar(cl_cos[:, :, N:P], cst[:, :, 1, :], -1.0, None, ALU.mult)
                    v.tensor_scalar(cl_sin[:, :, 0:N], cst[:, :, 1, :], -1.0, None, ALU.mult)
                    v.tensor_scalar(cl_sin[:, :, N:P], cst[:, :, 0, :], -1.0, None, ALU.mult).then_inc(weights_step, 1)
                    dve.wait_ge(w_turned, 1)
                    v.tensor_copy(bu_w[:, :, :], t_ps[:, 0, 0:KT * P].rearrange("p (k n) -> p k n", k=KT))
                    tb = t_ps[:, 0, 0:KT * P].rearrange("p (k n) -> p k n", k=KT)
                    v.tensor_scalar(bu_turned_w[:, :, 0:N], tb[:, :, N:P], 1.0, None, ALU.mult)
                    v.tensor_scalar(bu_turned_w[:, :, N:P], tb[:, :, 0:N], -1.0, None, ALU.mult)
                    for k in range(KT):
                        v.tensor_copy(wt[:, k, :], t_ps[:, 1 + k, 0:D]).then_inc(w_evacuated, 1)
                    dve.wait_ge(w_evacuated, KT)
                    for k in range(KT):
                        last = v.tensor_scalar(skip_w[:, k, :], wt[:, k, :], dv[:, k:k + 1], None, ALU.mult)
                    step(last)
                    dve.wait_ge(out_w_ready, 1)
                    weights = ((bu_parts, bu_w), (bu_turned_parts, bu_turned_w), (skip_parts, skip_w))
                    for parts, w in weights:
                        last = v.tensor_copy(parts[0][:, :, :], w[:, :, :])
                    step(last)
                    for parts, w in weights:
                        v.tensor_tensor(parts[1][:, :, :], w[:, :, :], parts[0][:, :, :], ALU.subtract)
                    v.tensor_copy(out_cos_w[:, :], m_ps[:, 0, 0:D])
                    step(v.tensor_copy(out_sin_w[:, :], m_ps[:, 1, 0:D]))

                    turn = 1.0 / (2 * np.pi)
                    c1 = float(np.floor(turn * 2.0 ** 18) / 2.0 ** 18)
                    c2 = float(np.floor((turn - c1) * 2.0 ** 34) / 2.0 ** 34)
                    c3 = float(turn - c1 - c2)
                    step(v.tensor_tensor(col[:, 7:8], col[:, 1:2], col[:, 3:4], ALU.mult))
                    rest = col[:, 7:8]
                    for i in range(3):
                        step(v.tensor_copy(bits[:, i:i + 1], rest))
                        step(v.tensor_copy(col[:, 8 + i:9 + i], bits[:, i:i + 1]))
                        step(v.tensor_tensor(col[:, 12 + i:13 + i], rest, col[:, 8 + i:9 + i], ALU.subtract))
                        rest = col[:, 12 + i:13 + i]
                    products = [(0, c1), (1, c1), (2, c1), (0, c2), (1, c2), (0, c3)]
                    step(v.memset(col[:, 16:17], 0.0))
                    total = 16
                    for i, (part, c) in enumerate(products):
                        step(v.tensor_scalar(col[:, 18:19], col[:, 8 + part:9 + part], c, None, ALU.mult))
                        step(v.tensor_scalar(col[:, 19:20], col[:, 18:19], ROUND, ROUND, ALU.add, ALU.subtract))
                        step(v.tensor_tensor(col[:, 20:21], col[:, 18:19], col[:, 19:20], ALU.subtract))
                        step(v.tensor_tensor(col[:, 21 + i:22 + i], col[:, total:total + 1], col[:, 20:21], ALU.add))
                        total = 21 + i
                    whole = col[:, total:total + 1]
                    step(v.tensor_scalar(col[:, 28:29], whole, ROUND, ROUND, ALU.add, ALU.subtract))
                    step(v.tensor_tensor(col[:, 29:30], whole, col[:, 28:29], ALU.subtract))
                    step(v.tensor_scalar(col[:, 30:31], col[:, 29:30], ROUND / 4096, ROUND / 4096, ALU.add, ALU.subtract))
                    step(v.tensor_tensor(col[:, 31:32], col[:, 29:30], col[:, 30:31], ALU.subtract))

                    def fraction(dst, src):
                        step(v.tensor_scalar(tmp[:, :], src, ROUND, ROUND, ALU.add, ALU.subtract))
                        step(v.tensor_tensor(dst, src, tmp[:, :], ALU.subtract))

                    dve.wait_ge(steps_ready, 1)
                    step(v.tensor_scalar(ang[:, :], steps[:, :], col[:, 30:31], None, ALU.mult))
                    fraction(ang[:, :], ang[:, :])
                    step(v.scalar_tensor_tensor(out=ang[:, :], in0=steps[:, :], scalar=col[:, 31:32], in1=ang[:, :],
                                                op0=ALU.mult, op1=ALU.add))
                    step(v.tensor_scalar(tmp[:, :], ang[:, :], ROUND, ROUND, ALU.add, ALU.subtract))
                    v.tensor_tensor(ang[:, :], ang[:, :], tmp[:, :], ALU.subtract).then_inc(angle_ready, 1)
                    dve.wait_ge(angle_ready, 1)
                    step(v.tensor_scalar(steps[:, :], ang[:, :], 0.25, None, ALU.add))
                    step(v.tensor_scalar(tmp[:, :], steps[:, :], ROUND, ROUND, ALU.add, ALU.subtract))
                    v.tensor_tensor(steps[:, :], steps[:, :], tmp[:, :], ALU.subtract).then_inc(cos_angle_ready, 1)

                @block.scalar
                def _(act):
                    act.wait_ge(angle_ready, 1)
                    nc.scalar.activation(sin_t[:, :], ang[:, :], ACT.Sin, scale=TWO_PI).then_inc(table_done, 1)
                    act.wait_ge(cos_angle_ready, 1)
                    nc.scalar.activation(cos_t[:, :], steps[:, :], ACT.Sin, scale=TWO_PI).then_inc(table_done, 1)
                    act.wait_ge(table_done, 2)

                @block.tensor
                def _(pe):
                    pe.wait_ge(loaded, 16 * len(loads))
                    pe.wait_ge(bst_scaled, 1)
                    for k in range(KT):
                        pe.transpose(t_ps[:, 0, k * P:(k + 1) * P], bst_dt[:, k * P:(k + 1) * P], identf[:, :])
                    for k in range(KT):
                        for o in range(KT):
                            last = pe.transpose(t_ps[:, 1 + k, o * P:(o + 1) * P], wo[:, o, k * P:(k + 1) * P],
                                                identf[:, :])
                    last.then_inc(w_turned, 1)
                    pe.wait_ge(weights_step, 1)
                    pe.wait_ge(w_evacuated, KT)
                    for m, lhs in enumerate((cl_cos, cl_sin)):
                        for k in range(KT):
                            last = pe.matmul(m_ps[:, m, 0:D], lhs[:, k, :], wt[:, k, :], start=(k == 0), stop=(k == KT - 1))
                    last.then_inc(out_w_ready, 1)

        xt = [sb(f"x{k}", [P, TT, D]) for k in range(2)]
        xb = [sb(f"xb{k}", [P, TT, D]) for k in range(2)]
        xn = [sb(f"xn{k}", [P, TT, D]) for k in range(2)]
        xnT, xnT_lo = [[sb(f"{n}{k}", [P, KT, CH], F32R) for k in range(2)] for n in ("xnT", "xnT_lo")]
        y = [sb(f"y{k}", [P, TT, D]) for k in range(2)]
        stats = [sb(f"stats{k}", [P, TT, 6]) for k in range(2)]
        moments = [sb(f"moments{k}", [P, TT, 2]) for k in range(2)]
        rstd = [sb(f"rstd{k}", [P, TT]) for k in range(2)]
        var_eps = [sb(f"var_eps{k}", [P, TT]) for k in range(2)]
        carrier = sb("carrier", [1, 1])
        minus_half, eps = sb("minus_half", [P, TT]), sb("eps", [P, TT])
        u_cos, u_sin, u = sb("u_cos", [P, CH]), sb("u_sin", [P, CH]), sb("u", [P, CH])
        w = [sb(f"w{k}", [P, CH]) for k in range(2)]
        w_cos = [sb(f"w_cos{k}", [P, CH]) for k in range(2)]
        w_sin = [sb(f"w_sin{k}", [P, CH]) for k in range(2)]
        turned_ps = ctx.enter_context(nc.psum_tensor("ssm_turned", [P, KT, CH], F32))
        bu_ps = [ctx.enter_context(nc.psum_tensor(f"ssm_bu{k}", [P, 2, CH], F32)) for k in range(2)]
        out_ps = ctx.enter_context(nc.psum_tensor("ssm_out", [P, TT, D], F32))

        x_loaded = [sem(f"ssm_x_loaded{k}") for k in range(2)]
        y_stored = [sem(f"ssm_y_stored{k}") for k in range(2)]
        (stats_done, moments_done, eps_added, rstd_ready, xn_ready, turned, xnT_ready, xnT_lo_ready, bu_ready, u_parts, u_ready,
         w_ready, w_turned, out_ready, xb_ready, y_ready, const_ready) = [sem("ssm_" + n) for n in (
             "stats_done", "moments_done", "eps_added", "rstd_ready", "xn_ready", "turned", "xnT_ready", "xnT_lo_ready", "bu_ready",
             "u_parts", "u_ready", "w_ready", "w_turned", "out_ready", "xb_ready", "y_ready", "const_ready")]
        n_steps = n_chunks // 2
        with nc.Block() as block:
            @block.sync
            def _(sp):
                def load(n, k, old):
                    if old:
                        sp.wait_ge(xn_ready, n - 1)
                        sp.wait_ge(xb_ready, n - 1)
                    sp.dma_start(xt[k][:, :, :], xs[n]).then_inc(x_loaded[k], 16)

                def store(n, k):
                    sp.wait_ge(y_ready, n + 1)
                    sp.dma_start(x1s[n], y[k][:, :, :]).then_inc(y_stored[k], 16)

                load(0, 0, False)
                load(1, 1, False)
                load(2, 0, True)
                load(3, 1, True)
                store(0, 0)
                with sp.Fori(1, n_steps - 1) as it:
                    for k in range(2):
                        load(2 * it + k + 2, k, True)
                        store(2 * it + k - 1, 1 - k)
                for n in range(2 * (n_steps - 1) - 1, n_chunks):
                    store(n, n % 2)
                for k in range(2):
                    sp.wait_ge(y_stored[k], 16 * n_steps)

            @block.gpsimd
            def _(pool):
                nc.gpsimd.memset(eps[:, :], EPS).then_inc(const_ready, 1)
                nc.gpsimd.memset(minus_half[:, :], -0.5).then_inc(const_ready, 1)
                pool.wait_ge(const_ready, 2)

                def chunk(n, it, k, old):
                    pool.wait_ge(moments_done, n + 1)
                    nc.gpsimd.tensor_tensor(var_eps[k][:, :], moments[k][:, :, 1], eps[:, :],
                                            ALU.add).then_inc(eps_added, 1)
                    pool.wait_ge(eps_added, n + 1)
                    if old:
                        pool.wait_ge(xn_ready, n - 1)
                    nc.gpsimd.tensor_tensor(rstd[k][:, :], var_eps[k][:, :], minus_half[:, :],
                                            ALU.pow).then_inc(rstd_ready, 1)
                    pool.wait_ge(x_loaded[k], 16 * it + 16)
                    if old:
                        pool.wait_ge(y_ready, n - 1)
                    nc.gpsimd.tensor_tensor(xb[k][:, :, :], xt[k][:, :, :],
                                            bias_row[:, :].unsqueeze(1).to_broadcast([P, TT, D]),
                                            ALU.add).then_inc(xb_ready, 1)

                chunk(0, 0, 0, False)
                chunk(1, 0, 1, False)
                with pool.Fori(1, n_steps) as it:
                    for k in range(2):
                        chunk(2 * it + k, it, k, True)

            @block.vector
            def _(dve):
                def normalise(n, it, k, old):
                    dve.wait_ge(x_loaded[k], 16 * it + 16)
                    for t in range(TT):
                        last = nc.vector.bn_stats(stats[k][:, t, :], xt[k][:, t, :])
                    last.then_inc(stats_done, 1)
                    if old:
                        dve.wait_ge(eps_added, n - 1)
                    dve.wait_ge(stats_done, n + 1)
                    nc.vector.memset(carrier[:, :], 0.0)
                    for t in range(TT):
                        last = nc.vector.bn_aggr(moments[k][:, t, :], stats[k][:, t, :])
                    last.then_inc(moments_done, 1)

                def scale(n, k, old):
                    dve.wait_ge(rstd_ready, n + 1)
                    if old:
                        dve.wait_ge(turned, KT * (n - 1))
                    for t in range(TT):
                        last = nc.vector.tensor_scalar(xn[k][:, t, :], xt[k][:, t, :], moments[k][:, t, 0:1],
                                                       rstd[k][:, t:t + 1], ALU.subtract, ALU.mult)
                    last.then_inc(xn_ready, 1)

                def low(n, k):
                    for f in range(KT):
                        dve.wait_ge(xnT_ready, KT * n + f + 1)
                        nc.vector.tensor_tensor(xnT_lo[k][:, f, :], turned_ps[:, f, :], xnT[k][:, f, :],
                                                ALU.subtract).then_inc(xnT_lo_ready, 1)

                def scan(n, k, old):
                    cos_k, sin_k = cos_t[:, k * CH:(k + 1) * CH], sin_t[:, k * CH:(k + 1) * CH]
                    dve.wait_ge(bu_ready, n + 1)
                    nc.vector.tensor_tensor(u_cos[:, :], bu_ps[k][:, 0, :], cos_k, ALU.mult)
                    nc.vector.tensor_tensor(u_sin[:, :], bu_ps[k][:, 1, :], sin_k, ALU.mult).then_inc(u_parts, 1)
                    dve.wait_ge(u_parts, n + 1)
                    nc.vector.tensor_tensor(u[:, :], u_cos[:, :], u_sin[:, :], ALU.add).then_inc(u_ready, 1)
                    dve.wait_ge(u_ready, n + 1)
                    nc.vector.tensor_tensor_scan(w[k][:, :], decay[:, 0:1].to_broadcast([P, CH]), u[:, :],
                                                 w[1 - k][:, CH - 1:CH] if k else 0.0,
                                                 ALU.mult, ALU.add).then_inc(w_ready, 1)
                    dve.wait_ge(w_ready, n + 1)
                    if old:
                        dve.wait_ge(out_ready, n - 1)
                    nc.vector.tensor_tensor(w_cos[k][:, :], w[k][:, :], cos_k, ALU.mult)
                    nc.vector.tensor_tensor(w_sin[k][:, :], w[k][:, :], sin_k, ALU.mult).then_inc(w_turned, 1)

                def residual(n, it, k, old):
                    dve.wait_ge(out_ready, n + 1)
                    dve.wait_ge(xb_ready, n + 1)
                    if old:
                        dve.wait_ge(y_stored[k], 16 * it)
                    nc.vector.tensor_tensor(y[k][:, :, :], out_ps[:, :, :], xb[k][:, :, :],
                                            ALU.add).then_inc(y_ready, 1)

                normalise(0, 0, 0, False)
                scale(0, 0, False)
                normalise(1, 0, 1, False)
                low(0, 0)
                scan(0, 0, False)
                scale(1, 1, False)

                def slot(n, it, k, old, more):
                    low(n + 1, 1 - k)
                    if more:
                        normalise(n + 2, it + 1, k, True)
                    scan(n + 1, 1 - k, old or k == 1)
                    if more:
                        scale(n + 2, k, True)
                    residual(n, it, k, old)

                slot(0, 0, 0, False, True)
                slot(1, 0, 1, False, True)
                with dve.Fori(1, n_steps - 1) as it:
                    for k in range(2):
                        slot(2 * it + k, it, k, True, True)
                it = n_steps - 1
                slot(2 * it, it, 0, True, False)
                residual(2 * it + 1, it, 1, True)

            @block.scalar
            def _(act):
                def evacuate(n, k, old):
                    act.wait_ge(turned, KT * n + 1)
                    if old:
                        act.wait_ge(out_ready, n - 1)
                    for f in range(KT):
                        if f:
                            act.wait_ge(turned, KT * n + f + 1)
                        nc.scalar.activation(xnT[k][:, f, :], turned_ps[:, f, :], ACT.Copy).then_inc(xnT_ready, 1)

                evacuate(0, 0, False)
                evacuate(1, 1, False)
                with act.Fori(1, n_steps) as it:
                    for k in range(2):
                        evacuate(2 * it + k, k, True)

            @block.tensor
            def _(pe):
                def turn(n, k, first):
                    pe.wait_ge(xn_ready, n + 1)
                    if not first:
                        pe.wait_ge(xnT_lo_ready, KT * n)
                    for f in range(KT):
                        for t in range(TT):
                            last = pe.transpose(turned_ps[:, f, t * P:(t + 1) * P], xn[k][:, t, f * P:(f + 1) * P],
                                                identf[:, :])
                        last.then_inc(turned, 1)

                def project(n, k, old):
                    for f in range(KT):
                        pe.wait_ge(xnT_ready, KT * n + f + 1)
                        if old and f == 0:
                            pe.wait_ge(u_parts, n - 1)
                        for m, parts in enumerate((bu_parts, bu_turned_parts)):
                            for i in range(2):
                                pe.matmul(bu_ps[k][:, m, :], parts[i][:, f, :], xnT[k][:, f, :],
                                          start=(f == 0 and i == 0), stop=False)
                    for f in range(KT):
                        pe.wait_ge(xnT_lo_ready, KT * n + f + 1)
                        for m, parts in enumerate((bu_parts, bu_turned_parts)):
                            last = pe.matmul(bu_ps[k][:, m, :], parts[0][:, f, :], xnT_lo[k][:, f, :],
                                             start=False, stop=(f == KT - 1))
                    last.then_inc(bu_ready, 1)

                def out(n, k, first):
                    if not first:
                        pe.wait_ge(y_ready, n)
                    pe.wait_ge(w_turned, n + 1)
                    for t in range(TT):
                        cols = slice(t * P, (t + 1) * P)
                        terms = [(xnT[k][:, f, cols], skip_parts[i][:, f, :]) for f in range(KT) for i in range(2)]
                        terms += [(xnT_lo[k][:, f, cols], skip_parts[0][:, f, :]) for f in range(KT)]
                        terms += [(w_cos[k][:, cols], out_cos_w[:, :]), (w_sin[k][:, cols], out_sin_w[:, :])]
                        for i, (lhs, rhs) in enumerate(terms):
                            last = pe.matmul(out_ps[:, t, :], lhs, rhs, start=(i == 0), stop=(i == len(terms) - 1))
                    last.then_inc(out_ready, 1)

                turn(0, 0, True)
                project(0, 0, False)

                def slot(n, k, first, old):
                    turn(n + 1, 1 - k, False)
                    project(n + 1, 1 - k, old or k == 1)
                    out(n, k, first)

                slot(0, 0, True, False)
                slot(1, 1, False, False)
                with pe.Fori(1, n_steps - 1) as it:
                    for k in range(2):
                        slot(2 * it + k, k, False, True)
                slot(2 * (n_steps - 1), 0, False, True)
                out(2 * (n_steps - 1) + 1, 1, False)


def ffn_phase(nc, sem, name, identf, x1, x2, cn, gc, adaptive_range):
    HALF, QUARTER = D // 2, D // 4
    CHAINS = 2 * NCH
    SLOTS = 3 * CHAINS
    PAIRS = SLOTS // 2
    PREPARE_AT = (6, 8, 10)
    n_steps = x1.shape[0] // 2
    xs = x1.rearrange("b (c t p) d -> (b c) p t d", c=NCH, p=P)
    ys = x2.rearrange("b (c t p) d -> (b c) p t d", c=NCH, p=P)
    cn_w1, cn_b1, cn_w2, cn_b2, cn_w3, cn_b3, cn_w4, cn_b4 = cn
    gc_w1, gc_b1, gc_w2, gc_b2, gc_w3, gc_b3 = gc
    with ExitStack() as ctx:
        def sb(n, shape, dt=F32):
            return ctx.enter_context(nc.sbuf_tensor(name + n, shape, dt))

        def psum(n, shape):
            return ctx.enter_context(nc.psum_tensor(name + n, shape, F32))

        def sems(names):
            return [sem(name + n) for n in names.split()]

        w1, w2, w3 = sb("w1", [P, KT, D]), sb("w2", [P, KT, P]), sb("w3", [P, 64])
        w4 = sb("w4", [P, 2])
        g1w, g2w, g3w = sb("g1w", [P, KT, P]), sb("g2w", [P, 64]), sb("g3w", [64, P])
        g3col = sb("g3col", [64, 1])
        b1, b2, b3 = sb("b1", [P, KT]), sb("b2", [P, 1]), sb("b3", [P, 1])
        gb1, gb2 = sb("gb1", [P, 1]), sb("gb2", [64, 1])
        half_bias = sb("half_bias", [P, 2])
        b4_half, gb3_half = half_bias[:, 0:1], half_bias[:, 1:2]
        ar = sb("ar", [P, 1])
        ar_cols = sb("ar_cols", [P, 3])
        eps, minus_half = sb("eps", [P, TT]), sb("minus_half", [P, TT])
        carrier = sb("carrier", [1, 1])
        xt = [sb(f"x{c}", [P, TT, D]) for c in range(CHAINS)]
        residual = [sb(f"residual{c}", [P, TT, D]) for c in range(CHAINS)]
        z = [[sb(f"z{c}_{i}", [P, TT, D]) for i in range(3)] for c in range(CHAINS)]
        y = [sb(f"y{k}", [P, TT, D]) for k in range(2)]
        w1_hi, w1_lo = sb("w1_hi", [P, KT, D], F32R), sb("w1_lo", [P, KT, D], F32R)
        zT_hi, zT_lo = [[sb(f"{n}{k}", [P, KT, CH], F32R) for k in range(2)] for n in ("zT_hi", "zT_lo")]
        h1 = [sb(f"h1_{k}", [P, KT, CH]) for k in range(2)]
        h2 = [sb(f"h2_{k}", [P, CH]) for k in range(2)]
        h3 = sb("h3", [P, CH])
        stats, moments = sb("stats", [P, TT, 6]), sb("moments", [P, TT, 2])
        var_eps, rstd, rstd_neg = sb("var_eps", [P, TT]), sb("rstd", [P, TT]), sb("rstd_neg", [P, TT])
        minus_one = sb("minus_one", [P, TT])
        tanh_token = sb("tanh_token", [P, TT, 2])
        c_pos, c_neg = [[sb(f"{n}{k}", [P, TT, 2]) for k in range(2)] for n in ("c_pos", "c_neg")]
        sums = sb("sums", [P, CHAINS, KT])
        g1, g2 = sb("g1", [P, 1]), sb("g2", [64, 1])
        tanh_global = sb("tanh_global", [P, 2])
        kappa = sb("kappa", [P, 2, 2])

        turned_ps, h1_ps = psum("turned", [P, KT, CH]), psum("h1p", [P, KT, CH])
        h2_ps, h3_ps, token_ps, global_ps = psum("h2p", [P, 512]), psum("h3p", [P, 512]), psum("tp", [P, 512]), psum("gp", [P, 512])

        x_loaded = [sem(f"{name}x_loaded{c}") for c in range(CHAINS)]
        residuals_loaded = sem(name + "residuals_loaded")
        y_stored = [sem(f"{name}y_stored{k}") for k in range(2)]
        (loaded, const_ready, weights_ready, stats_done, moments_done, eps_added, rstd_ready, rstd_neg_ready,
         z0_ready, rotated) = sems(
            "loaded const_ready weights_ready stats_done moments_done eps_added rstd_ready rstd_neg_ready "
            "z0_ready rotated")
        (turned, zT_hi_ready, zT_lo_ready, h1_done, h1_ready, h2_done, h2_ready, h3_done, h3_ready, token_done, token_ready,
         weights_negated, weights_rounded, global_done, global_ready, kappa_pos, kappa_ready, coupling_ready,
         blended, y_ready) = sems(
            "turned zT_hi_ready zT_lo_ready h1_done h1_ready h2_done h2_ready h3_done h3_ready token_done token_ready "
            "weights_negated weights_rounded global_done global_ready kappa_pos kappa_ready coupling_ready "
            "blended y_ready")

        def column(v, n=P):
            return v.rearrange("(n a) -> n a", a=1) if n == v.shape[0] else \
                v.rearrange("(n a) -> n a", a=1).to_broadcast([n, 1])

        loads = [
            (w1[:, :, :], cn_w1.rearrange("(k p) n -> p k n", p=P)),
            (w2[:, :, :], cn_w2.rearrange("(k p) n -> p k n", p=P)),
            (w3[:, :], cn_w3), (w4[0:64, 0:1], cn_w4), (w4[64:P, 1:2], cn_w4),
            (g1w[:, :, :], gc_w1.rearrange("(k p) n -> p k n", p=P)),
            (g2w[:, :], gc_w2), (g3col[:, :], gc_w3),
            (b1[:, :], cn_b1.rearrange("(k p) -> p k", p=P)),
            (b2[:, :], column(cn_b2)), (b3[0:64, :], column(cn_b3, 64)), (b3[64:P, :], column(cn_b3, 64)),
            (gb1[:, :], column(gc_b1)), (gb2[:, :], column(gc_b2, 64)),
            (b4_half, column(cn_b4)), (gb3_half, column(gc_b3)), (ar[:, :], column(adaptive_range)),
        ]

        with nc.Block() as block:
            @block.sync
            def _(sp):
                with nc.allow_non_contiguous_dma(reason="a few short columns, once"):
                    for c in range(CHAINS):
                        sp.dma_start(xt[c][:, :, :], xs[c]).then_inc(x_loaded[c], 16)
                        if c == 0:
                            sp.wait_ge(const_ready, 4)
                            for dst, src in loads:
                                sp.dma_start(dst, src).then_inc(loaded, 16)

                for c in range(CHAINS):
                    sp.dma_start(residual[c][:, :, :], xs[c]).then_inc(residuals_loaded, 16)

                def step(it, last):
                    if not last:
                        for c in range(CHAINS):
                            sp.wait_ge(z0_ready, CHAINS * it + c + 1)
                            sp.dma_start(xt[c][:, :, :], xs[CHAINS * (it + 1) + c]).then_inc(x_loaded[c], 16)
                    for c in range(CHAINS):
                        sp.wait_ge(y_ready, CHAINS * it + c + 1)
                        if not last:
                            sp.dma_start(residual[c][:, :, :],
                                         xs[CHAINS * (it + 1) + c]).then_inc(residuals_loaded, 16)
                        sp.dma_start(ys[CHAINS * it + c], y[c % 2][:, :, :]).then_inc(y_stored[c % 2], 16)

                with sp.Fori(0, n_steps - 1) as it:
                    step(it, False)
                step(n_steps - 1, True)
                for k in range(2):
                    sp.wait_ge(y_stored[k], 16 * (CHAINS // 2) * n_steps)

            @block.gpsimd
            def _(pool):
                nc.gpsimd.memset(eps[:, :], EPS).then_inc(const_ready, 1)
                nc.gpsimd.memset(minus_half[:, :], -0.5).then_inc(const_ready, 1)
                nc.gpsimd.memset(minus_one[:, :], -1.0).then_inc(const_ready, 1)
                nc.gpsimd.memset(w4[:, :], 0.0).then_inc(const_ready, 1)
                pool.wait_ge(const_ready, 4)

                def rstds(n):
                    pool.wait_ge(moments_done, n + 1)
                    nc.gpsimd.tensor_tensor(var_eps[:, :], moments[:, :, 1], eps[:, :], ALU.add).then_inc(eps_added, 1)
                    pool.wait_ge(eps_added, n + 1)
                    nc.gpsimd.tensor_tensor(rstd[:, :], var_eps[:, :], minus_half[:, :], ALU.pow).then_inc(rstd_ready, 1)
                    pool.wait_ge(rstd_ready, n + 1)
                    nc.gpsimd.tensor_tensor(rstd_neg[:, :], rstd[:, :], minus_one[:, :],
                                            ALU.mult).then_inc(rstd_neg_ready, 1)

                def blend(it, c):
                    pool.wait_ge(residuals_loaded, 16 * CHAINS * (it + 1))
                    pool.wait_ge(rotated, 2 * CHAINS * it + CHAINS + c + 1)
                    split = D - QUARTER
                    base = residual[c]
                    nc.gpsimd.tensor_tensor(base[:, :, 0:split], base[:, :, 0:split], z[c][2][:, :, 0:split], ALU.add)
                    nc.gpsimd.tensor_tensor(base[:, :, split:D], base[:, :, split:D], z[c][2][:, :, split:D],
                                            ALU.subtract).then_inc(blended, 1)

                def step(it, last):
                    for m in range(SLOTS):
                        if m == 0:
                            rstds(CHAINS * it + CHAINS - 1)
                        if m in PREPARE_AT and not last:
                            rstds(CHAINS * (it + 1) + PREPARE_AT.index(m))
                        if 2 * CHAINS - 1 <= m < 3 * CHAINS - 1:
                            blend(it, m - (2 * CHAINS - 1))

                for c in range(CHAINS - 1):
                    rstds(c)
                with pool.Fori(0, n_steps - 1) as it:
                    step(it, False)
                step(n_steps - 1, True)

            @block.vector
            def _(dve):
                v = nc.vector
                def prepare(it, c):
                    n = CHAINS * it + c
                    dve.wait_ge(x_loaded[c], 16 * it + 16)
                    for t in range(TT):
                        last = v.bn_stats(stats[:, t, :], xt[c][:, t, :])
                    last.then_inc(stats_done, 1)
                    dve.wait_ge(stats_done, n + 1)
                    v.memset(carrier[:, :], 0.0)
                    for t in range(TT):
                        last = v.bn_aggr(moments[:, t, :], stats[:, t, :])
                    last.then_inc(moments_done, 1)
                    dve.wait_ge(rstd_neg_ready, n + 1)
                    split = D - QUARTER
                    for t in range(TT):
                        v.tensor_scalar(z[c][0][:, t, 0:split], xt[c][:, t, 0:split], moments[:, t, 0:1],
                                        rstd[:, t:t + 1], ALU.subtract, ALU.mult)
                        last = v.tensor_scalar(z[c][0][:, t, split:D], xt[c][:, t, split:D], moments[:, t, 0:1],
                                               rstd_neg[:, t:t + 1], ALU.subtract, ALU.mult)
                    last.then_inc(z0_ready, 1)

                def couple(it, p):
                    g, j = PAIRS * it + p, p % 2
                    if p < 2:
                        dve.wait_ge(global_ready, 3 * (2 * it + j + 1))
                        v.tensor_scalar(kappa[:, j, 0:1], tanh_global[:, j:j + 1], ar_cols[:, 2:3], 0.1, ALU.mult,
                                        ALU.add).then_inc(kappa_pos, 1)
                        dve.wait_ge(kappa_pos, 2 * it + j + 1)
                        v.tensor_scalar(kappa[:, j, 1:2], kappa[:, j, 0:1], -1.0, None,
                                        ALU.mult).then_inc(kappa_ready, 1)
                        dve.wait_ge(kappa_ready, 2 * it + j + 1)
                    dve.wait_ge(token_ready, g + 1)
                    v.tensor_scalar(c_pos[j][:, :, :], tanh_token[:, :, :], ar_cols[:, 0:1], kappa[:, j, 0:1],
                                    ALU.mult, ALU.add)
                    v.tensor_scalar(c_neg[j][:, :, :], tanh_token[:, :, :], ar_cols[:, 1:2], kappa[:, j, 1:2],
                                    ALU.mult, ALU.add).then_inc(coupling_ready, 1)
                    dve.wait_ge(coupling_ready, g + 1)

                def rotate(it, m):
                    c, cycle, k, j = m % CHAINS, m // CHAINS, m % 2, m // 2 % 2
                    old, new = z[c][cycle], z[c][cycle + 1]
                    for t in range(TT):
                        a, b = old[:, t, 0:HALF], old[:, t, HALF:D]
                        v.scalar_tensor_tensor(out=new[:, t, 0:HALF], in0=b, scalar=c_pos[j][:, t, k:k + 1], in1=a,
                                               op0=ALU.mult, op1=ALU.add)
                        last = v.scalar_tensor_tensor(out=new[:, t, HALF:D], in0=a, scalar=c_neg[j][:, t, k:k + 1],
                                                      in1=b, op0=ALU.mult, op1=ALU.add)
                    last.then_inc(rotated, 1)

                def finish(it, m, old):
                    c, k, j = m % CHAINS, m % 2, m // 2 % 2
                    split = D - QUARTER
                    dve.wait_ge(blended, CHAINS * it + c + 1)
                    if old or c >= 2:
                        dve.wait_ge(y_stored[c % 2], 16 * ((CHAINS // 2) * it + c // 2))
                    for t in range(TT):
                        a, b, base = z[c][2][:, t, 0:HALF], z[c][2][:, t, HALF:D], residual[c][:, t, :]
                        out = y[c % 2][:, t, :]
                        v.scalar_tensor_tensor(out=out[:, 0:HALF], in0=b, scalar=c_pos[j][:, t, k:k + 1],
                                               in1=base[:, 0:HALF], op0=ALU.mult, op1=ALU.add)
                        v.scalar_tensor_tensor(out=out[:, HALF:split], in0=a[:, 0:QUARTER],
                                               scalar=c_neg[j][:, t, k:k + 1], in1=base[:, HALF:split],
                                               op0=ALU.mult, op1=ALU.add)
                        last = v.scalar_tensor_tensor(out=out[:, split:D], in0=a[:, QUARTER:HALF],
                                                      scalar=c_pos[j][:, t, k:k + 1], in1=base[:, split:D],
                                                      op0=ALU.mult, op1=ALU.add)
                    last.then_inc(y_ready, 1)

                def zT_low(it, m):
                    g, k = SLOTS * it + m, m % 2
                    dve.wait_ge(zT_hi_ready, g + 1)
                    v.tensor_tensor(zT_lo[k][:, :, :], turned_ps[:, :, :], zT_hi[k][:, :, :],
                                    ALU.subtract).then_inc(zT_lo_ready, 1)

                def behind(it, p, old):
                    couple(it, p)
                    for m in (2 * p, 2 * p + 1):
                        if m < 2 * CHAINS:
                            rotate(it, m)
                        else:
                            finish(it, m, old)

                def step(it, first, last):
                    for m in range(SLOTS):
                        zT_low(it, m)
                        if m == 0:
                            prepare(it, CHAINS - 1)
                        if m in PREPARE_AT and not last:
                            prepare(it + 1, PREPARE_AT.index(m))
                        if m % 2 and m >= 3:
                            behind(it, (m - 3) // 2, not first)
                        elif m % 2 and not first:
                            behind(it - 1, PAIRS - 1, True)

                prepare(0, 0)
                dve.wait_ge(loaded, 16 * len(loads))
                v.tensor_scalar(w1[64:P, 1, :], w1[64:P, 1, :], -1.0, None, ALU.mult)
                v.tensor_scalar(g1w[64:P, 1, :], g1w[64:P, 1, :], -1.0, None, ALU.mult)
                v.tensor_scalar(half_bias[:, :], half_bias[:, :], 0.5, None, ALU.mult)
                v.tensor_scalar(ar_cols[:, 0:1], ar[:, :], 0.3, None, ALU.mult)
                v.tensor_scalar(ar_cols[:, 1:2], ar[:, :], -0.3, None, ALU.mult)
                v.tensor_scalar(ar_cols[:, 2:3], ar[:, :], 0.7, None, ALU.mult)
                v.tensor_copy(g3w[:, :], g3col[:, 0:1].to_broadcast([64, P])).then_inc(weights_negated, 1)
                dve.wait_ge(weights_negated, 1)
                v.tensor_copy(w1_hi[:, :, :], w1[:, :, :]).then_inc(weights_rounded, 1)
                dve.wait_ge(weights_rounded, 1)
                v.tensor_tensor(w1_lo[:, :, :], w1[:, :, :], w1_hi[:, :, :], ALU.subtract).then_inc(weights_ready, 1)
                for c in range(1, CHAINS - 1):
                    prepare(0, c)
                step(0, True, False)
                with dve.Fori(1, n_steps - 1) as it:
                    step(it, False, False)
                step(n_steps - 1, False, True)
                behind(n_steps - 1, PAIRS - 1, True)

            @block.scalar
            def _(act):
                a = nc.scalar.activation

                def gelu3(it, p, old):
                    g = PAIRS * it + p
                    act.wait_ge(h3_done, g + 1)
                    if old:
                        act.wait_ge(token_done, g)
                    a(h3[:, :], h3_ps[:, :], ACT.Gelu, bias=b3[:, 0:1]).then_inc(h3_ready, 1)

                def tanh(it, p, old):
                    g = PAIRS * it + p
                    act.wait_ge(token_done, g + 1)
                    if old:
                        act.wait_ge(coupling_ready, g)
                    a(tanh_token[:, :, :], token_ps[:, 0:2 * TT].rearrange("p (t k) -> p t k", k=2), ACT.Tanh,
                      bias=b4_half, scale=0.5).then_inc(token_ready, 1)

                def gelu2(it, m, old):
                    g, k = SLOTS * it + m, m % 2
                    act.wait_ge(h2_done, g + 1)
                    if old:
                        act.wait_ge(h3_done, PAIRS * it + (m - 2) // 2 + 1)
                    a(h2[k][:, :], h2_ps[:, :], ACT.Gelu, bias=b2[:, 0:1]).then_inc(h2_ready, 1)

                def evacuate(it, m, old):
                    g, k = SLOTS * it + m, m % 2
                    act.wait_ge(turned, g + 1)
                    if old:
                        act.wait_ge(h1_done, KT * (g - 1))
                    if m < CHAINS:
                        for f in range(KT):
                            last = a(zT_hi[k][:, f, :], turned_ps[:, f, :], ACT.Copy, accum_out=sums[:, m, f:f + 1])
                    else:
                        last = a(zT_hi[k][:, :, :], turned_ps[:, :, :], ACT.Copy)
                    last.then_inc(zT_hi_ready, 1)

                def gelu1(it, m, f, old):
                    g, k = SLOTS * it + m, m % 2
                    act.wait_ge(h1_done, KT * g + f + 1)
                    if f == 0 and old:
                        act.wait_ge(h2_done, g - 1)
                    last = a(h1[k][:, f, :], h1_ps[:, f, :], ACT.Gelu, bias=b1[:, f:f + 1])
                    if f == KT - 1:
                        last.then_inc(h1_ready, 1)

                def step(it, first):
                    for m in range(SLOTS):
                        old = not first or m >= 2
                        pair = (m - 3) // 2 if m % 2 and m >= 3 else None
                        j = (m - NCH) // NCH if 0 < m <= CHAINS and m % NCH == 0 else None
                        if pair is not None:
                            gelu3(it, pair, not first or pair > 0)
                        elif m % 2 and not first:
                            gelu3(it - 1, PAIRS - 1, True)
                        evacuate(it, m, old)
                        if j is not None:
                            act.wait_ge(global_done, 3 * (2 * it + j) + 1)
                            a(g1[:, :], global_ps[:, 0:1], ACT.Gelu, bias=gb1[:, 0:1], scale=1.0 / L).then_inc(global_ready, 1)
                        if m >= 1:
                            gelu2(it, m - 1, not first or m >= 3)
                        elif not first:
                            gelu2(it - 1, SLOTS - 1, True)
                        if j is not None:
                            act.wait_ge(global_done, 3 * (2 * it + j) + 2)
                            a(g2[:, :], global_ps[0:64, 1:2], ACT.Gelu, bias=gb2[:, 0:1]).then_inc(global_ready, 1)
                        if pair is not None:
                            tanh(it, pair, not first or pair > 0)
                        elif m % 2 and not first:
                            tanh(it - 1, PAIRS - 1, True)
                        if j is not None:
                            act.wait_ge(global_done, 3 * (2 * it + j) + 3)
                            a(tanh_global[:, j:j + 1], global_ps[:, 2:3], ACT.Tanh, bias=gb3_half,
                              scale=0.5).then_inc(global_ready, 1)
                        gelu1(it, m, 0, old)
                        gelu1(it, m, 1, old)

                act.wait_ge(weights_ready, 1)
                step(0, True)
                with act.Fori(1, n_steps) as it:
                    step(it, False)
                it = n_steps - 1
                gelu2(it, SLOTS - 1, True)
                gelu3(it, PAIRS - 1, True)
                tanh(it, PAIRS - 1, True)

            @block.tensor
            def _(pe):
                mm = pe.matmul

                def layer3(it, p, first):
                    g = PAIRS * it + p
                    pe.wait_ge(h2_ready, 2 * g + 2)
                    if not first:
                        pe.wait_ge(h3_ready, g)
                    for k in range(2):
                        last = mm(h3_ps[64 * k:64 * k + 64, :], w3[:, :], h2[k][:, :], start=True, stop=True)
                    last.then_inc(h3_done, 1)

                def layer4(it, p, first):
                    g = PAIRS * it + p
                    pe.wait_ge(h3_ready, g + 1)
                    if not first:
                        pe.wait_ge(token_ready, g)
                    for t in range(TT):
                        last = mm(token_ps[:, 2 * t:2 * t + 2], h3[:, t * P:(t + 1) * P], w4[:, :], start=True, stop=True)
                    last.then_inc(token_done, 1)

                def turn(it, m, first):
                    g, c, cycle = SLOTS * it + m, m % CHAINS, m // CHAINS
                    if cycle == 0:
                        pe.wait_ge(z0_ready, CHAINS * it + c + 1)
                    else:
                        pe.wait_ge(rotated, 2 * CHAINS * it + (m - CHAINS) + 1)
                    if not first:
                        pe.wait_ge(zT_lo_ready, g)
                    for f in range(KT):
                        for t in range(TT):
                            last = pe.transpose(turned_ps[:, f, t * P:(t + 1) * P],
                                                z[c][cycle][:, t, f * P:(f + 1) * P], identf[:, :])
                    last.then_inc(turned, 1)

                def layer2(it, m, first):
                    g, k = SLOTS * it + m, m % 2
                    pe.wait_ge(h1_ready, g + 1)
                    if not first:
                        pe.wait_ge(h2_ready, g)
                    for f in range(KT):
                        last = mm(h2_ps[:, :], w2[:, f, :], h1[k][:, f, :], start=(f == 0), stop=(f == KT - 1))
                    last.then_inc(h2_done, 1)

                def layer1(it, m, o, first):
                    g, k, cols = SLOTS * it + m, m % 2, slice(o * P, (o + 1) * P)
                    if o == 0:
                        pe.wait_ge(zT_hi_ready, g + 1)
                        if not first:
                            pe.wait_ge(h1_ready, g)
                    for f in range(KT):
                        for i, part in enumerate((w1_hi, w1_lo)):
                            mm(h1_ps[:, o, :], part[:, f, cols], zT_hi[k][:, f, :], start=(f == 0 and i == 0), stop=False)

                def layer1_low(it, m):
                    g, k = SLOTS * it + m, m % 2
                    pe.wait_ge(zT_lo_ready, g + 1)
                    for o in range(KT):
                        for f in range(KT):
                            last = mm(h1_ps[:, o, :], w1_hi[:, f, o * P:(o + 1) * P], zT_lo[k][:, f, :],
                                      start=False, stop=(f == KT - 1))
                        last.then_inc(h1_done, 1)

                def step(it, first):
                    for m in range(SLOTS):
                        j = (m - NCH) // NCH if 0 < m <= CHAINS and m % NCH == 0 else None
                        pair = (m - 3) // 2 if m % 2 and m >= 3 else None
                        if pair is not None:
                            layer3(it, pair, first and pair == 0)
                        elif m % 2 and not first:
                            layer3(it - 1, PAIRS - 1, False)
                        turn(it, m, first and m == 0)
                        if first and m == 0:
                            pe.wait_ge(weights_ready, 1)
                        if j is not None:
                            for i, (c, f) in enumerate([(NCH * j + h, f) for h in range(NCH) for f in range(KT)]):
                                last = mm(global_ps[:, 0:1], g1w[:, f, :], sums[:, c, f:f + 1], start=(i == 0),
                                          stop=(i == NCH * KT - 1))
                            last.then_inc(global_done, 1)
                        if m >= 1:
                            layer2(it, m - 1, first and m == 1)
                        elif not first:
                            layer2(it - 1, SLOTS - 1, False)
                        if j is not None:
                            pe.wait_ge(global_ready, 3 * (2 * it + j) + 1)
                            mm(global_ps[0:64, 1:2], g2w[:, :], g1[:, :], start=True, stop=True).then_inc(global_done, 1)
                        if pair is not None:
                            layer4(it, pair, first and pair == 0)
                        elif m % 2 and not first:
                            layer4(it - 1, PAIRS - 1, False)
                        layer1(it, m, 0, first and m == 0)
                        if j is not None:
                            pe.wait_ge(global_ready, 3 * (2 * it + j) + 2)
                            mm(global_ps[:, 2:3], g3w[:, :], g2[:, :], start=True, stop=True).then_inc(global_done, 1)
                        layer1(it, m, 1, False)
                        layer1_low(it, m)

                step(0, True)
                with pe.Fori(1, n_steps) as it:
                    step(it, False)
                it = n_steps - 1
                layer2(it, SLOTS - 1, False)
                layer3(it, PAIRS - 1, False)
                layer4(it, PAIRS - 1, False)


def attention_phase(nc, sem, identf, identb, x2, x3, wqkv, bqkv, wproj, bproj, qk_scratch, v_scratch):
    HD = 16
    HT = 64
    BT = P // HD
    NBLK = HT // BT
    HALF_T = HT // 2
    PARTS = 3
    PAIRS_Q, PAIRS_K = (0, 0, 0, 1, 1, 2), (0, 1, 2, 0, 1, 0)
    PARTS_R = (0, 0), (1, 0), (0, 1)
    KROWS = HD * len(PAIRS_Q)
    STEPS, UNITS1, UNITS2 = 40, 9, 10
    NB = x2.shape[0]
    S1_BANKS, A_BANKS = 3, 1
    SCALE = 1.0 / np.sqrt(HD)
    PASS1 = [[(7, 0, 32)], [(7, 32, 64)], [(6, 0, 32)], [(6, 32, 56), (0, 0, 8)], [(5, 0, 32)],
             [(5, 32, 48), (1, 0, 16)], [(4, 0, 32)], [(4, 32, 40), (2, 0, 24)], [(3, 0, 32)]]
    PASS2 = [[(0, 0, 32)], [(1, 8, 32), (3, 24, 32)], [(2, 16, 32)],
             [(0, 32, 64)], [(1, 32, 64)], [(2, 32, 64)], [(3, 32, 64)], [(4, 32, 64)],
             [(5, 40, 64), (7, 56, 64)], [(6, 48, 64)]]
    FIRST_U2 = (0, 3)
    LAST_U2 = (2, 9)
    ROWS_AT = [(12, 14), (20, 22), (29, 31), (37, 39)]
    PROJECT_AT = [0, 2, 4, 6, 8, 10, 16, 18]
    PREPARE_AT = 28
    LAY_OUT_AT, LAY_OUT_RATE, PIECES = (18, 34), 2, 8
    NORM_AT = {0: (8, 14), 1: (31, 35), 2: (8, 14), 3: (8, 14)}
    FINISH_AT = [(2, 6), (9, 13), (16, 20), (23, 27)]
    A_OFF, A_TOTAL, A_PROLOGUE = (0, 16, 24, 40), 48, 16
    B_OFF, B_TOTAL, B_SKIPPED = (0, 10, 12, 14), 16, 10

    xs = x2.rearrange("b (c t p) d -> (b c) p t d", c=NCH, p=P)
    xr = x2.rearrange("b (n t c) d -> (b n) c t d", t=BT, c=HD)
    ys = x3.rearrange("b (n t c) d -> (b n) c t d", t=BT, c=HD)

    def a_events(project, pass1):
        events = []
        if project:
            events += [(s, "project", j) for j, s in enumerate(PROJECT_AT)]
        if pass1:
            events += [(s, "rows", (i, e)) for i, at in enumerate(ROWS_AT) for e, s in enumerate(at)]
        return [(s, kind, which, k) for k, (s, kind, which) in enumerate(sorted(events))]

    with ExitStack() as ctx:
        def sb(n, shape, dt=F32):
            return ctx.enter_context(nc.sbuf_tensor("att_" + n, shape, dt))

        def psum(n, shape):
            return ctx.enter_context(nc.psum_tensor("att_" + n, shape, F32))

        staged = sb("staged", [KROWS, HD, CH], BF16)
        qs = [sb(f"qs{s}", [P, HD * CH], BF16) for s in range(2)]
        ks = [sb(f"ks{s}", [P, HD * CH], BF16) for s in range(2)]
        vs = [sb(f"vs{s}", [P, CH * HD // P, 32]) for s in range(2)]
        probs = [[sb(f"probs{k}_{i}", [P, CH]) for i in range(4)] for k in range(2)]
        o_sb = [sb(f"o{k}", [P, 2, CH]) for k in range(2)]
        y_sb = sb("y", [P, L // P, D])
        yT = [sb(f"yT{k}", [P, KT, 2 * P]) for k in range(2)]
        x_res = [sb(f"x_res{k}", [P, 2, D]) for k in range(2)]
        x_bias = [sb(f"x_bias{k}", [P, 2, D]) for k in range(2)]
        out_sb = [sb(f"out{k}", [P, 2, D]) for k in range(2)]
        xt = [sb(f"x{s}", [P, TT, D]) for s in range(2)]
        xn = sb("xn", [P, TT, D])
        xnT = [sb(f"xnT{i}", [P, KT, CH], F32R) for i in range(2)]
        wq = [sb(f"wqkv{i}", [P, KT, 3 * D], F32R) for i in range(2)]
        whole = [sb(f"whole{k}", [P, CH]) for k in range(2)]
        rest = [sb(f"rest{k}", [P, CH]) for k in range(2)]
        parts = sb("parts", [P, 4, PARTS, CH], BF16)
        v_tok = sb("v_tok", [P, TT, D])
        wp = sb("wproj", [P, KT, D])
        b_raw, b_qk = sb("b_raw", [P, 4]), sb("b_qk", [P, 4])
        bv_row, bp_row = sb("bv_row", [P, D]), sb("bp_row", [P, D])
        mask_raw = [sb(f"mask_raw{k}", [P, P], BF16) for k in range(2)]
        mask = [sb(f"mask{k}", [P, P], BF16) for k in range(2)]
        stats, moments = sb("stats", [P, TT, 6]), sb("moments", [P, TT, 2])
        var_eps, rstd = sb("var_eps", [P, TT]), sb("rstd", [P, TT])
        eps, minus_half = sb("eps", [P, TT]), sb("minus_half", [P, TT])
        carrier = sb("carrier", [1, 1])
        row_max = [sb(f"row_max{k}", [P, NBLK]) for k in range(2)]
        max_lo = [sb(f"max_lo{k}", [P, NBLK // 2]) for k in range(2)]
        max_hi = [sb(f"max_hi{k}", [P, NBLK // 2]) for k in range(2)]
        neg_parts = [sb(f"neg_parts{k}", [P, NBLK, 32], BF16) for k in range(2)]
        recip = sb("recip", [P, 4, 4])

        s1_ps = [psum(f"s1_{k}", [P, 512]) for k in range(S1_BANKS)]
        s2_ps = [psum(f"s2_{k}", [P, 512]) for k in range(2)]
        a_banks = [psum(f"a_ps{k}", [P, 512]) for k in range(A_BANKS)]
        o_ps, b_ps = psum("o_ps", [P, 512]), psum("b_ps", [P, 512])

        x_loaded = [sem(f"att_x_loaded{s}") for s in range(2)]
        v_loaded = [sem(f"att_v_loaded{s}") for s in range(2)]
        rows_moved = [sem(f"att_rows_moved{k}") for k in range(2)]
        (loaded, xnT_lo_ready, const_ready, zeroed, weights_ready, stats_done, moments_done, eps_added, rstd_ready, xn_ready,
         a_full, a_free, rest_ready, middle_ready, parts_ready, v_ready, q_stored, k_stored, v_stored,
         stack_staged, q_laid_out, k_laid_out, mask_made, mask_ready, s1_full, s1_free,
         row_maxima, row_max_ready, neg_hi_ready, neg_ready, s2_full, exp_done, pv_done, o_free, b_full,
         b_free, recip_ready, bias_added) = [sem("att_" + n) for n in (
             "loaded xnT_lo_ready const_ready zeroed weights_ready stats_done moments_done eps_added rstd_ready xn_ready "
             "a_full a_free rest_ready middle_ready parts_ready v_ready q_stored k_stored v_stored stack_staged q_laid_out k_laid_out mask_made mask_ready s1_full s1_free "
             "row_maxima row_max_ready neg_hi_ready neg_ready s2_full exp_done pv_done o_free b_full "
             "b_free recip_ready bias_added").split()]

        wq_raw = y_sb[:, :, :].rearrange("p n d -> p (n d)")[:, 0:KT * 3 * D].rearrange("p (k n) -> p k n", k=KT)
        loads = [
            (wq_raw, wqkv.rearrange("(k p) n -> p k n", p=P)),
            (wp[:, :, :], wproj.rearrange("(k p) n -> p k n", p=P)),
            (b_raw[:, :], bqkv[0:2 * D].rearrange("(k p) -> p k", p=P)),
            (bv_row[:, :], bqkv[2 * D:3 * D].rearrange("(a n) -> a n", a=1).to_broadcast([P, D])),
            (bp_row[:, :], bproj.rearrange("(a n) -> a n", a=1).to_broadcast([P, D])),
        ]

        def stack_loads(s, side):
            for g, part in enumerate((PAIRS_Q, PAIRS_K)[side]):
                yield (staged[HD * g:HD * (g + 1), :, :],
                       qk_scratch[s, side, part].rearrange("(c d) t -> d c t", d=HD))

        def v_loads(s):
            src = v_scratch[s].rearrange("(n t c) d -> t c n d", t=BT, c=HD)
            for t in range(BT):
                yield vs[s][t:P:BT, :, 0:HD], src[t]

        N_STACK, N_V = len(PAIRS_Q), BT

        def slots(body):
            def sequence(b, first, last):
                for q in range(4):
                    body(b, q, first, not (last and q == 3), q % 2 == 0 and not (last and q == 2),
                         q % 2 == 1 and not last)
            return sequence

        def run(eng, sequence):
            sequence(0, True, False)
            with eng.Fori(1, NB - 1) as b:
                sequence(b, False, False)
            sequence(NB - 1, False, True)

        def coming(b, q):
            return ((2 * b + 1, 1, b), (2 * b + 2, 0, b + 1), (2 * b + 2, 0, b + 1), (2 * b + 3, 1, b + 1))[q]

        with nc.Block() as block:
            @block.sync
            def _(sp):
                with nc.allow_non_contiguous_dma(reason="a few short columns, once"):
                    sp.dma_start(xt[0][:, :, :], xs[0]).then_inc(x_loaded[0], 16)
                    for dst, src in loads:
                        sp.dma_start(dst, src).then_inc(loaded, 16)
                sp.dma_start(xt[1][:, :, :], xs[1]).then_inc(x_loaded[1], 16)

                def project(hb, s, turn, first, more):
                    for side, stored in enumerate((q_stored, k_stored)):
                        for o in range(2):
                            sp.wait_ge(parts_ready, 4 * hb + 2 * side + o + 1)
                            sp.dma_start(qk_scratch[s, side].rearrange("r (o p) t -> o p r t", p=P)[o],
                                         parts[:, 2 * side + o, :, :]).then_inc(stored, 16)
                        sp.wait_ge(stored, 32 * (hb + 1))
                        sp.wait_ge((k_laid_out, q_laid_out)[side], 32 * (hb + 1))
                        for dst, src in stack_loads(s, side):
                            sp.dma_start(dst, src).then_inc(stack_staged, 16)
                    sp.wait_ge(v_ready, 2 * hb + 2)
                    if more:
                        sp.dma_start(xt[s][:, :, :], xs[hb + 2]).then_inc(x_loaded[s], 16)
                    if not first:
                        sp.wait_ge(v_loaded[s], 16 * N_V * turn)
                    sp.dma_start(v_scratch[s].rearrange("(t p c) d -> p t (c d)", p=P, c=HD),
                                 v_tok[:, :, :]).then_inc(v_stored, 16)
                    sp.wait_ge(v_stored, 16 * (hb + 1))
                    if not first:
                        sp.wait_ge(pv_done, UNITS2 * (2 * hb - 2))
                    for dst, src in v_loads(s):
                        sp.dma_start(dst, src).then_inc(v_loaded[s], 16)

                def finish_loads(b):
                    for r in range(4):
                        if r >= 2:
                            sp.wait_ge(bias_added, 4 * b + r - 1)
                        for n in range(2):
                            sp.dma_start(x_res[r % 2][:, n, :], xr[8 * b + 2 * r + n]).then_inc(rows_moved[r % 2], 16)
                        if r >= 1:
                            finish_store(b, r - 1)
                    finish_store(b, 3)

                def finish_store(b, r):
                    sp.wait_ge(b_free, B_TOTAL * (b + 1) + 2 + 2 * r + 2)
                    for n in range(2):
                        sp.dma_start(ys[8 * b + 2 * r + n], out_sb[r % 2][:, n, :]).then_inc(rows_moved[r % 2], 16)

                def sequence(b, first, second_last, last):
                    project(*coming(b, 0), first, not last)
                    if not first:
                        finish_loads(b - 1)
                    if not last:
                        project(*coming(b, 2), False, not second_last)

                for k, m in enumerate(mask_raw):
                    sp.wait_ge(mask_made, k + 1)
                    for t in range(BT):
                        sp.dma_start(mask[k][t:P:BT, :], m[HD * t:HD * (t + 1), :]).then_inc(mask_ready, 16)
                project(0, 0, 0, True, True)
                sequence(0, True, False, False)
                with sp.Fori(1, NB - 2) as b:
                    sequence(b, False, False, False)
                sequence(NB - 2, False, True, False)
                sequence(NB - 1, False, False, True)
                finish_loads(NB - 1)
                for k in range(2):
                    sp.wait_ge(rows_moved[k], 128 * NB)

            @block.gpsimd
            def _(pool):
                g = nc.gpsimd
                g.memset(eps[:, :], EPS).then_inc(const_ready, 1)
                g.memset(minus_half[:, :], -0.5).then_inc(const_ready, 1)
                for s in range(2):
                    g.memset(vs[s][:, :, HD:32], 0.0).then_inc(zeroed, 1)
                    g.memset(neg_parts[s][:, :, :], 0.0).then_inc(zeroed, 1)
                for k in range(2):
                    g.memset(mask_raw[k][:, :], 0.0).then_inc(zeroed, 1)
                pool.wait_ge(zeroed, 6)
                for s in range(2):
                    g.memset(vs[s][:, :, HD:HD + 1], 1.0).then_inc(const_ready, 1)
                for k, sign in enumerate((1, -1)):
                    m = mask_raw[k][:, :].rearrange("p (c t) -> p c t", c=HD)
                    g.affine_select(out=m, in_=m, pattern=[[-sign, HD], [-sign * HD, BT]], compare_op=ALU.is_ge,
                                    fill=-1e30, base=0, channel_multiplier=sign).then_inc(mask_made, 1)
                pool.wait_ge(const_ready, 4)

                def rstds(hb):
                    pool.wait_ge(moments_done, hb + 1)
                    g.tensor_tensor(var_eps[:, :], moments[:, :, 1], eps[:, :], ALU.add).then_inc(eps_added, 1)
                    pool.wait_ge(eps_added, hb + 1)
                    g.tensor_tensor(rstd[:, :], var_eps[:, :], minus_half[:, :], ALU.pow).then_inc(rstd_ready, 1)

                def take_rest(hb, j, a_index):
                    pool.wait_ge(a_free, a_index + 1)
                    g.tensor_tensor(rest[j % 2][:, :], whole[j % 2][:, :], parts[:, j, 0, :],
                                    ALU.subtract).then_inc(rest_ready, 1)

                def last_part(hb, j):
                    pool.wait_ge(middle_ready, 4 * hb + j + 1)
                    g.tensor_tensor(parts[:, j, 2, :], rest[j % 2][:, :], parts[:, j, 1, :],
                                    ALU.subtract).then_inc(parts_ready, 1)

                def v_bias(hb, e, a_index):
                    pool.wait_ge(a_free, a_index + 1)
                    g.tensor_tensor(v_tok[:, 2 * e:2 * e + 2, :], v_tok[:, 2 * e:2 * e + 2, :],
                                    bv_row[:, :].unsqueeze(1).to_broadcast([P, 2, D]), ALU.add).then_inc(v_ready, 1)

                def a_index_of(b, q, project_j):
                    if b is None:
                        return project_j
                    k = {w: k for _, kind, w, k in a_events(True, True) if kind == "project"}[project_j]
                    return A_PROLOGUE + A_TOTAL * b + A_OFF[q] + k

                def project_tasks(hb, b, q):
                    for j in range(4):
                        at = PROJECT_AT[2 + j]
                        yield at + 2, lambda j=j: take_rest(hb, j, a_index_of(b, q, 2 + j))
                        yield at + 4, lambda j=j: last_part(hb, j)
                    for e in range(2):
                        yield PROJECT_AT[6 + e] + 2, lambda e=e: v_bias(hb, e, a_index_of(b, q, 6 + e))

                def bias(b, r):
                    pool.wait_ge(rows_moved[r % 2], 128 * b + 64 * (r // 2) + 32)
                    if not isinstance(b, int) or 4 * b + r >= 2:
                        pool.wait_ge(b_free, B_TOTAL * (b + 1 if r >= 2 else b) + 2 + 2 * ((r - 2) % 4) + 2)
                    g.tensor_tensor(x_bias[r % 2][:, :, :], x_res[r % 2][:, :, :],
                                    bp_row[:, :].unsqueeze(1).to_broadcast([P, 2, D]), ALU.add).then_inc(bias_added, 1)

                def slot(b, q, first, pass1, projects, normalises):
                    tasks = list(project_tasks(coming(b, q)[0], b, q)) if projects else []
                    if normalises:
                        tasks += [(PREPARE_AT, lambda: rstds(coming(b, q)[0]))]
                    if q == 1 and not first:
                        tasks += [(FINISH_AT[r][0], lambda r=r: bias(b - 1, r)) for r in range(4)]
                    for step in range(STEPS):
                        for at, task in tasks:
                            if at == step:
                                task()

                pool.wait_ge(loaded, 16 * len(loads))
                rstds(0)
                for _, task in sorted(project_tasks(0, None, 0), key=lambda x: x[0]):
                    task()
                rstds(1)
                run(pool, slots(slot))
                for r in range(4):
                    bias(NB - 1, r)

            @block.vector
            def _(dve):
                v = nc.vector

                def prepare(hb, s, turn):
                    dve.wait_ge(x_loaded[s], 16 * turn + 16)
                    for t in range(TT):
                        last = v.bn_stats(stats[:, t, :], xt[s][:, t, :])
                    last.then_inc(stats_done, 1)
                    dve.wait_ge(stats_done, hb + 1)
                    v.memset(carrier[:, :], 0.0)
                    for t in range(TT):
                        last = v.bn_aggr(moments[:, t, :], stats[:, t, :])
                    last.then_inc(moments_done, 1)

                def normalise(hb, s, turn):
                    dve.wait_ge(rstd_ready, hb + 1)
                    for t in range(TT):
                        last = v.tensor_scalar(xn[:, t, :], xt[s][:, t, :], moments[:, t, 0:1], rstd[:, t:t + 1],
                                               ALU.subtract, ALU.mult)
                    last.then_inc(xn_ready, 1)

                def lay_out(hb, s, side, e):
                    stack = (qs, ks)[side][s]
                    if e == 0:
                        dve.wait_ge(stack_staged, 16 * N_STACK * (2 * hb + side + 1))
                    n = CH // BT // PIECES
                    last = v.tensor_copy(
                        stack[0:KROWS, :].rearrange("p (n c t) -> p n c t", c=HD, t=BT)[:, e * n:(e + 1) * n],
                        staged[:, :, :].rearrange("p c (n t) -> p n c t", t=BT)[:, e * n:(e + 1) * n])
                    if e == PIECES - 1:
                        last.then_inc((q_laid_out, k_laid_out)[side], 32)

                def low(hb, j, a_index):
                    dve.wait_ge(a_free, a_index + 1)
                    v.tensor_tensor(xnT[1][:, j, :], a_banks[j % A_BANKS][:, :], xnT[0][:, j, :],
                                    ALU.subtract).then_inc(xnT_lo_ready, 1)

                def middle_part(hb, j):
                    dve.wait_ge(rest_ready, 4 * hb + j + 1)
                    v.tensor_copy(parts[:, j, 1, :], rest[j % 2][:, :]).then_inc(middle_ready, 1)

                def maxima(q_next, step):
                    i, unit, k = step // UNITS1, PASS1[step % UNITS1], (step // UNITS1) % 2
                    dve.wait_ge(s1_full, 4 * UNITS1 * q_next + step + 1)
                    col = 0
                    for blk, t0, t1 in unit:
                        n = HD * (t1 - t0)
                        dst = row_max[k][:, blk:blk + 1] if blk < 4 else \
                            (max_hi if t0 else max_lo)[k][:, blk - 4:blk - 3]
                        last = v.tensor_reduce(dst, s1_ps[step % S1_BANKS][:, col:col + n], AX.X, ALU.max)
                        col += n
                    last.then_inc(s1_free, 1)
                    if step % UNITS1 == UNITS1 - 1:
                        n = 4 * q_next + i
                        dve.wait_ge(s1_free, 4 * UNITS1 * q_next + step + 1)
                        v.tensor_tensor(row_max[k][:, 4:8], max_lo[k][:, :], max_hi[k][:, :],
                                        ALU.max).then_inc(row_max_ready, 1)
                        dve.wait_ge(row_max_ready, n + 1)
                        v.tensor_scalar(neg_parts[k][:, :, 0], row_max[k][:, :], -1.0, None,
                                        ALU.mult).then_inc(neg_hi_ready, 1)
                        dve.wait_ge(neg_hi_ready, n + 1)
                        v.scalar_tensor_tensor(out=neg_parts[k][:, :, 1], in0=row_max[k][:, :], scalar=-1.0,
                                               in1=neg_parts[k][:, :, 0], op0=ALU.mult,
                                               op1=ALU.subtract).then_inc(neg_ready, 1)

                def evacuate(quad, k, half):
                    dve.wait_ge(pv_done, UNITS2 * quad + LAST_U2[half] + 1)
                    v.tensor_copy(o_sb[k][:, half, :], o_ps[:, :]).then_inc(o_free, 1)

                def divide(b_index, quad, q, e):
                    dve.wait_ge(b_full, b_index + 1)
                    heads = b_ps[:, :].rearrange("p (n h w) -> p n h w", n=4, h=4)
                    v.reciprocal(recip[:, :, :], heads[:, :, :, HD]).then_inc(recip_ready, 1)
                    dve.wait_ge(recip_ready, 2 * quad + e + 1)
                    v.tensor_tensor(
                        y_sb[:, 4 * e:4 * e + 4, 64 * q:64 * q + 64].rearrange("p n (h w) -> p n h w", h=4),
                        heads[:, :, :, 0:HD], recip[:, :, :].unsqueeze(3).to_broadcast([P, 4, 4, HD]),
                        ALU.mult).then_inc(b_free, 1)

                def finish_turn(b_index, r):
                    dve.wait_ge(b_full, b_index + 1)
                    v.tensor_copy(yT[r % 2][:, :, :], b_ps[:, :].rearrange("p (k n) -> p k n", k=KT)).then_inc(b_free, 1)

                def finish_add(b_index, b, r):
                    dve.wait_ge(b_full, b_index + 1)
                    dve.wait_ge(bias_added, 4 * b + r + 1)
                    v.tensor_tensor(out_sb[r % 2][:, :, :], b_ps[:, :].rearrange("p (t d) -> p t d", t=2),
                                    x_bias[r % 2][:, :, :], ALU.add).then_inc(b_free, 1)

                def divide_tasks(b, q_done, base, at):
                    for e in range(2):
                        yield at[e] + 1, lambda e=e: divide(base + e, 4 * b + q_done, q_done, e)

                def finish_tasks(b, base):
                    for r, (turn_at, add_at) in enumerate(FINISH_AT):
                        yield turn_at + 1, lambda r=r: finish_turn(base + 2 * r, r)
                        yield add_at + 1, lambda r=r: finish_add(base + 2 * r + 1, b, r)

                def slot(b, q, first, pass1, projects, normalises):
                    tasks = []
                    base = B_TOTAL * b - B_SKIPPED
                    if projects:
                        hb, s, turn = coming(b, q)
                        a_base = A_PROLOGUE + A_TOTAL * b + A_OFF[q]
                        tasks += [(PROJECT_AT[j], lambda j=j: low(hb, j, a_base + j)) for j in range(KT)]
                        tasks += [(PROJECT_AT[2 + j] + 3, lambda j=j: middle_part(hb, j)) for j in range(4)]
                        tasks += [(LAY_OUT_AT[side] + e // LAY_OUT_RATE, lambda side=side, e=e: lay_out(hb, s, side, e))
                                  for side in range(2) for e in range(PIECES)]
                    if normalises:
                        comes = coming(b, q)
                        tasks += [(PREPARE_AT, lambda: prepare(*comes)), (PREPARE_AT + 2, lambda: normalise(*comes))]
                    if q == 0 and not first:
                        tasks += [(4, lambda: evacuate(4 * b - 1, 1, 1))]
                        tasks += divide_tasks(b - 1, 3, base, NORM_AT[0])
                    if q > 0:
                        tasks += [(4, lambda: evacuate(4 * b + q - 1, (q - 1) % 2, 1))]
                    if q == 1 and not first:
                        tasks += finish_tasks(b - 1, base + 2)
                    if q > 0:
                        tasks += divide_tasks(b, q - 1, base + B_OFF[q], NORM_AT[q])
                    tasks += [(16, lambda: evacuate(4 * b + q, q % 2, 0))]
                    for step in range(STEPS):
                        if pass1 and step < 4 * UNITS1:
                            maxima(4 * b + q + 1, step)
                        for at, task in tasks:
                            if at == step:
                                task()

                dve.wait_ge(loaded, 16 * len(loads))
                dve.wait_ge(const_ready, 4)
                v.memset(ks[0][KROWS:P, :], 1.0)
                v.memset(ks[1][KROWS:P, :], 1.0).then_inc(k_laid_out, 32)
                v.memset(carrier[:, :], 0.0).then_inc(b_free, B_SKIPPED)
                v.tensor_scalar(b_qk[:, 0:2], b_raw[:, 0:2], SCALE, None, ALU.mult)
                v.tensor_copy(b_qk[:, 2:4], b_raw[:, 2:4])
                v.tensor_copy(wq[0][:, :, :], wq_raw).then_inc(weights_ready, 1)
                dve.wait_ge(weights_ready, 1)
                v.tensor_tensor(wq[1][:, :, :], wq_raw, wq[0][:, :, :], ALU.subtract).then_inc(weights_ready, 1)
                prepare(0, 0, 0)
                normalise(0, 0, 0)
                for j in range(KT):
                    low(0, j, j)
                for j in range(4):
                    middle_part(0, j)
                for side in range(2):
                    for e in range(PIECES):
                        lay_out(0, 0, side, e)
                prepare(1, 1, 0)
                normalise(1, 1, 0)
                for step in range(4 * UNITS1):
                    maxima(0, step)
                run(dve, slots(slot))
                evacuate(4 * NB - 1, 1, 1)
                base = B_TOTAL * NB - B_SKIPPED
                for at, task in sorted(divide_tasks(NB - 1, 3, base, (0, 1)), key=lambda x: x[0]):
                    task()
                for at, task in sorted(finish_tasks(NB - 1, base + 2), key=lambda x: x[0]):
                    task()

            @block.scalar
            def _(act):
                a = nc.scalar.activation

                def exponentiate(b, q, step, old):
                    u, i = step // 4, step % 4
                    quad = 4 * b + q
                    act.wait_ge(s2_full, STEPS * quad + step + 1)
                    if old or u >= 2:
                        act.wait_ge(pv_done, UNITS2 * quad + u - 1)
                    n = sum(HD * (t1 - t0) for _, t0, t1 in PASS2[u])
                    a(probs[u % 2][i][:, 0:n], s2_ps[step % 2][:, 0:n], ACT.Exp).then_inc(exp_done, 1)

                def project(j, a_index, hb, old, k):
                    a_ps = a_banks[k % A_BANKS]
                    act.wait_ge(a_full, a_index + 1)
                    if j < 2:
                        a(xnT[0][:, j, :], a_ps[:, :], ACT.Copy).then_inc(a_free, 1)
                    elif j < 6:
                        j -= 2
                        if j >= 2:
                            act.wait_ge(rest_ready, 4 * hb + j - 1)
                        elif old:
                            act.wait_ge(rest_ready, 4 * hb + j - 1)
                        if old:
                            act.wait_ge((q_stored, k_stored)[j // 2], 32 * hb)
                        scale = SCALE if j < 2 else 1.0
                        a(whole[j % 2][:, :], a_ps[:, :], ACT.Identity, bias=b_qk[:, j:j + 1], scale=scale)
                        a(parts[:, j, 0, :], a_ps[:, :], ACT.Identity, bias=b_qk[:, j:j + 1],
                          scale=scale).then_inc(a_free, 1)
                    else:
                        e = j - 6
                        if old and e == 0:
                            act.wait_ge(v_stored, 16 * hb)
                        a(v_tok[:, 2 * e:2 * e + 2, :], a_ps[:, :].rearrange("p (t d) -> p t d", t=2),
                          ACT.Copy).then_inc(a_free, 1)

                def rows(s, head, e, a_index, k):
                    a_ps = a_banks[k % A_BANKS]
                    act.wait_ge(a_full, a_index + 1)
                    n0 = HD * (HT * head + HALF_T * e)
                    a(qs[s][KROWS:P, n0:n0 + CH], a_ps[KROWS:P, :], ACT.Copy).then_inc(a_free, 1)

                def a_tasks(b, q, projects, pass1, base, hb, old):
                    for step, kind, which, k in a_events(projects, pass1):
                        if kind == "project":
                            yield step, lambda which=which, k=k: project(which, base + k, hb, old, k)
                        else:
                            i, e = which
                            s1, head = ((q + 1) // 2) % 2, 4 * ((q + 1) % 2) + i
                            yield step, lambda s1=s1, head=head, e=e, k=k: rows(s1, head, e, base + k, k)

                def slot(b, q, first, pass1, projects, normalises):
                    base = A_PROLOGUE + A_TOTAL * b + A_OFF[q]
                    hb = coming(b, q)[0] if projects else None
                    tasks = list(a_tasks(b, q, projects, pass1, base, hb, True))
                    for step in range(STEPS):
                        exponentiate(b, q, step, not first or q > 0)
                        for at, task in tasks:
                            if at == step:
                                task()

                act.wait_ge(weights_ready, 1)
                for j in range(8):
                    project(j, j, 0, False, j)
                for _, task in a_tasks(None, -1, False, True, 8, None, True):
                    task()
                run(act, slots(slot))

            @block.tensor
            def _(pe):
                mm = pe.matmul

                def block_of(stack, rows, head, blk):
                    return span_of(stack, rows, head, BT * blk, BT * (blk + 1))

                def span_of(stack, rows, head, t0, t1):
                    return stack[0:rows, HD * (HT * head + t0):HD * (HT * head + t1)]

                def pass_one(q_next, quad_in_seq, step):
                    i, unit = step // UNITS1, PASS1[step % UNITS1]
                    s, head = quad_in_seq // 2, 4 * (quad_in_seq % 2) + i
                    if not isinstance(q_next, int) or q_next > 0 or step >= S1_BANKS:
                        pe.wait_ge(s1_free, 4 * UNITS1 * q_next + step - (S1_BANKS - 1))
                    col = 0
                    for blk, t0, t1 in unit:
                        n = t1 - t0
                        out = s1_ps[step % S1_BANKS][:, col:col + HD * n]
                        diagonal = t1 == BT * (blk + 1)
                        last = mm(out, block_of(qs[s], KROWS, head, blk), span_of(ks[s], KROWS, head, t0, t1),
                                  start=True, stop=not diagonal)
                        if diagonal:
                            last = mm(out[:, HD * n - P:HD * n], identb[:, :], mask[0][:, :], start=False, stop=True)
                        col += HD * n
                    last.then_inc(s1_full, 1)

                def rows(q_next, i, e, a_index, k):
                    a_ps = a_banks[k % A_BANKS]
                    pe.wait_ge(neg_ready, 4 * q_next + i + 1)
                    pe.wait_ge(a_free, a_index - (A_BANKS - 1))
                    for n in range(4):
                        last = mm(a_ps[KROWS:P, n * P:(n + 1) * P], neg_parts[i % 2][:, 4 * e + n, :], identb[:, :],
                                  start=True, stop=True)
                    last.then_inc(a_full, 1)

                def pass_two(b, q, step, row_index, old):
                    u, i = step // 4, step % 4
                    s, head = q // 2, 4 * (q % 2) + i
                    if old or step >= 2:
                        pe.wait_ge(exp_done, STEPS * (4 * b + q) + step - 1)
                    if u == 0:
                        pe.wait_ge(a_free, row_index + 1)
                    col = 0
                    for j, t0, t1 in PASS2[u]:
                        n = HD * (t1 - t0)
                        diagonal = t0 == BT * j
                        last = mm(s2_ps[step % 2][:, col:col + n], block_of(ks[s], P, head, j),
                                  span_of(qs[s], P, head, t0, t1), start=True, stop=not diagonal)
                        if diagonal:
                            last = mm(s2_ps[step % 2][:, col:col + P], identb[:, :], mask[1][:, :], start=False,
                                      stop=True)
                        col += n
                    last.then_inc(s2_full, 1)

                def times_v(b, q, u, old):
                    quad, s = 4 * b + q, q // 2
                    half = 0 if u <= LAST_U2[0] else 1
                    if u == FIRST_U2[0] and old:
                        pe.wait_ge(o_free, 2 * quad)
                    if u == FIRST_U2[1]:
                        pe.wait_ge(o_free, 2 * quad + 1)
                    pe.wait_ge(exp_done, STEPS * quad + 4 * u + 4)
                    if u == 0 and q % 2 == 0:
                        pe.wait_ge(v_loaded[s], 16 * N_V * (b + 1))
                    col = 0
                    for n_piece, (j, t0, t1) in enumerate(PASS2[u]):
                        n = t1 - t0
                        for i in range(4):
                            head = 4 * (q % 2) + i
                            first_t = HALF_T * half
                            last = mm(o_ps[32 * i:32 * i + 32, HD * (t0 - first_t):HD * (t1 - first_t)],
                                      vs[s][:, NBLK * head + j, :],
                                      probs[u % 2][i][:, col:col + HD * n],
                                      start=(u == FIRST_U2[half]), stop=(u == LAST_U2[half] and n_piece == len(PASS2[u]) - 1))
                        col += HD * n
                    last.then_inc(pv_done, 1)

                def project(j, s, a_index, k, first):
                    a_ps = a_banks[k % A_BANKS]
                    if j == 0:
                        pe.wait_ge(xn_ready, project.hb + 1)
                    if not first:
                        pe.wait_ge(a_free, a_index)
                    if j in (1, 2):
                        pe.wait_ge(xnT_lo_ready, KT * project.hb + j)
                    if j < 2:
                        for t in range(TT):
                            last = pe.transpose(a_ps[:, t * P:(t + 1) * P], xn[:, t, j * P:(j + 1) * P], identf[:, :])
                    elif j < 6:
                        cols = slice((j - 2) * P, (j - 1) * P)
                        for n, (f, (i, k)) in enumerate((f, part) for f in range(KT) for part in PARTS_R):
                            last = mm(a_ps[:, :], wq[i][:, f, cols], xnT[k][:, f, :], start=(n == 0),
                                      stop=(n == KT * len(PARTS_R) - 1))
                    else:
                        for t in range(2):
                            tok = slice((2 * (j - 6) + t) * P, (2 * (j - 6) + t + 1) * P)
                            for n, (f, (i, k)) in enumerate((f, part) for f in range(KT) for part in PARTS_R):
                                last = mm(a_ps[:, t * D:(t + 1) * D], xnT[k][:, f, tok], wq[i][:, f, 2 * D:3 * D],
                                          start=(n == 0), stop=(n == KT * len(PARTS_R) - 1))
                    last.then_inc(a_full, 1)

                def turn_heads(quad, k, b_index, e, first):
                    pe.wait_ge(o_free, 2 * quad + 2)
                    pe.wait_ge(b_free, b_index + B_SKIPPED)
                    for n in range(4):
                        last = pe.transpose(b_ps[:, n * P:(n + 1) * P], o_sb[k][:, e, n * P:(n + 1) * P], identf[:, :])
                    last.then_inc(b_full, 1)

                def finish_turn(b_index, r):
                    pe.wait_ge(b_free, b_index + B_SKIPPED)
                    for f in range(KT):
                        for t in range(2):
                            last = pe.transpose(b_ps[:, (2 * f + t) * P:(2 * f + t + 1) * P],
                                                y_sb[:, 2 * r + t, f * P:(f + 1) * P], identf[:, :])
                    last.then_inc(b_full, 1)

                def finish_project(b_index, r):
                    pe.wait_ge(b_free, b_index + B_SKIPPED)
                    for t in range(2):
                        for f in range(KT):
                            last = mm(b_ps[:, t * D:(t + 1) * D], yT[r % 2][:, f, t * P:(t + 1) * P], wp[:, f, :],
                                      start=(f == 0), stop=(f == KT - 1))
                    last.then_inc(b_full, 1)

                def heads_tasks(quad, k, base, at, first):
                    for e in range(2):
                        yield at[e], lambda e=e: turn_heads(quad, k, base + e, e, first and e == 0)

                def finish_tasks(base):
                    for r, (turn_at, project_at) in enumerate(FINISH_AT):
                        yield turn_at, lambda r=r: finish_turn(base + 2 * r, r)
                        yield project_at, lambda r=r: finish_project(base + 2 * r + 1, r)

                def row_use(projects, i):
                    return [k for _, kind, w, k in a_events(projects, True) if kind == "rows" and w == (i, 1)][0]

                def slot(b, q, first, pass1, projects, normalises):
                    a_base = A_PROLOGUE + A_TOTAL * b + A_OFF[q]
                    b_base = B_TOTAL * b - B_SKIPPED
                    tasks = []
                    s = coming(b, q)[1]
                    for step, kind, which, k in a_events(projects, pass1):
                        if kind == "project":
                            def task(which=which, k=k):
                                project.hb = coming(b, q)[0]
                                project(which, s, a_base + k, k, False)
                        else:
                            def task(which=which, k=k):
                                rows(4 * b + q + 1, which[0], which[1], a_base + k, k)
                        tasks.append((step, task))
                    if q == 0 and not first:
                        tasks += heads_tasks(4 * b - 1, 1, b_base, NORM_AT[0], False)
                    if q == 1 and not first:
                        tasks += finish_tasks(b_base + 2)
                    if q > 0:
                        tasks += heads_tasks(4 * b + q - 1, (q - 1) % 2, b_base + B_OFF[q], NORM_AT[q], first and q == 1)
                    for step in range(STEPS):
                        u, i = step // 4, step % 4
                        if pass1 and step < 4 * UNITS1:
                            if step == 0 and q in (1, 3):
                                pe.wait_ge(k_laid_out, 32 * (2 * b + 3 if q == 1 else 2 * b + 4))
                            pass_one(4 * b + q + 1, (q + 1) % 4, step)
                        before = (q - 1) % 4
                        row_base = A_PROLOGUE + A_TOTAL * (b if q else b - 1) + A_OFF[before]
                        k = row_use(before % 2 == 0 and pass1, i)
                        if first and q == 0:
                            row_base = 8
                        pass_two(b, q, step, row_base + k, not first or q > 0)
                        if i == 3:
                            if u > 0:
                                times_v(b, q, u - 1, not first or q > 0)
                            elif q > 0:
                                times_v(b, q - 1, UNITS2 - 1, True)
                            elif not first:
                                times_v(b - 1, 3, UNITS2 - 1, True)
                        for at, task in tasks:
                            if at == step:
                                task()

                pe.wait_ge(weights_ready, 2)
                project.hb = 0
                for j in range(8):
                    project(j, 0, j, j, j < A_BANKS)
                pe.wait_ge(k_laid_out, 64)
                pe.wait_ge(mask_ready, 32 * BT)
                rows_at = {at: w for at, kind, w, k in a_events(False, True)}
                for step in range(STEPS):
                    if step < 4 * UNITS1:
                        pass_one(0, 0, step)
                    if step in rows_at:
                        i, e = rows_at[step]
                        rows(0, i, e, 8 + 2 * i + e, e)
                run(pe, slots(slot))
                times_v(NB - 1, 3, UNITS2 - 1, True)
                b_base = B_TOTAL * NB - B_SKIPPED
                for _, task in sorted(heads_tasks(4 * NB - 1, 1, b_base, (0, 1), False), key=lambda x: x[0]):
                    task()
                for _, task in sorted(finish_tasks(b_base + 2), key=lambda x: x[0]):
                    task()


def mixed_layer(nc, ins, out):
    x, ssm, attention = ins[0], ins[1:11], ins[11:15]
    coupling, global_context, adaptive_range = ins[15:23], ins[23:29], ins[29]
    x1, x2, x3 = [nc.dram_tensor(n, x.shape, F32).ap() for n in ("x1", "x2", "x3")]
    qk_scratch = nc.dram_tensor("qk_scratch", (NCH, 2, 3, D, CH), BF16).ap()
    v_scratch = nc.dram_tensor("v_scratch", (NCH, CH * 16, 16), F32).ap()
    with ExitStack() as ctx:
        def sem(name):
            return ctx.enter_context(nc.semaphore(name))

        identf = ctx.enter_context(nc.sbuf_tensor("identf", [P, P], F32))
        identb = ctx.enter_context(nc.sbuf_tensor("identb", [P, P], BF16))
        make_identities(nc, sem, identf, identb)
        ssm_phase(nc, sem, identf, x, x1, *ssm)
        ffn_phase(nc, sem, "ffn1_", identf, x1, x2, coupling, global_context, adaptive_range)
        attention_phase(nc, sem, identf, identb, x2, x3, *attention, qk_scratch, v_scratch)
        ffn_phase(nc, sem, "ffn2_", identf, x3, out, coupling, global_context, adaptive_range)


_INS = ["L0_attn_a_x", "L0_attn_a_log_Lam_real", "L0_attn_a_Lam_imag", "L0_attn_a_B_real", "L0_attn_a_B_imag",
        "L0_attn_a_C_real", "L0_attn_a_C_imag", "L0_attn_a_D", "L0_attn_a_log_dt", "L0_attn_a_W_out",
        "L0_attn_a_b_out", "L0_attn_b_Wqkv", "L0_attn_b_bqkv", "L0_attn_b_Wproj", "L0_attn_b_bproj",
        "L0_ffn_cn_w1", "L0_ffn_cn_b1", "L0_ffn_cn_w2", "L0_ffn_cn_b2", "L0_ffn_cn_w3", "L0_ffn_cn_b3",
        "L0_ffn_cn_w4", "L0_ffn_cn_b4", "L0_ffn_gc_w1", "L0_ffn_gc_b1", "L0_ffn_gc_w2", "L0_ffn_gc_b2",
        "L0_ffn_gc_w3", "L0_ffn_gc_b3", "L0_ffn_adaptive_range"]


def kernel(**inputs):
    import numpy as _np
    import concourse.bacc as _bacc
    from concourse import mybir as _mybir
    from concourse.bass_utils import run_bass_kernel_spmd as _run

    nc = _bacc.Bacc("TRN2", target_bir_lowering=False, num_devices=1)
    arrays, args = {}, []
    for name in _INS:
        a = _np.ascontiguousarray(inputs[name])
        arrays[f"in_{name}_dram"] = a
        args.append(nc.dram_tensor(f"in_{name}_dram", a.shape, _mybir.dt.from_np(a.dtype), kind="ExternalInput").ap())
    shape = inputs["L0_attn_a_x"].shape
    out = nc.dram_tensor("out_0_dram", shape, _mybir.dt.float32, kind="ExternalOutput").ap()
    mixed_layer(nc, args, out)
    r = _run(nc, [arrays], core_ids=[0])
    return r.results[0]["out_0_dram"]
```
